# Optimizing a Trainium2 kernel written in Bass

```python
import numpy as np
import jax
import jax.numpy as jnp

def _softmax(x, axis=-1):
    return jax.nn.softmax(x, axis=axis)

def _gelu(x):
    return jax.nn.gelu(x, approximate=True)

def _silu(x):
    return jax.nn.silu(x)

def _sigmoid(x):
    return jax.nn.sigmoid(x)

def _layernorm(x, axis=-1, eps=1e-05):
    m = jnp.mean(x, axis=axis, keepdims=True)
    v = jnp.var(x, axis=axis, keepdims=True)
    return (x - m) / jnp.sqrt(v + eps)

def _scatter_add(tgt, idx, src, axis=0):
    return tgt.at[idx].add(src)

def _segment_sum(src, seg, n):
    return jax.ops.segment_sum(src, seg, n)
kernel_name = 'mk_adaln_d1_jaxref_r8_8ff9f5'

def setup_inputs(seed: int=0):
    np.random.seed(seed)
    _w = jnp.asarray

    def _L0_attn_setup():
        import jax, jax.numpy as jnp
        import numpy as np
        EPS_RMS = 1e-06
        EPS_GN = 1e-05

        def rms_norm(x, w, eps=EPS_RMS):
            var = jnp.mean(x * x, axis=-1, keepdims=True)
            return w * (x * jax.lax.rsqrt(var + eps))
        key = jax.random.key(seed)
        B, T, D, H, LORA, F = (4, 256, 128, 16, 64, 512)
        dk = D // H
        ks = jax.random.split(key, 20)
        s = 0.02

        def n(k, shape, scale=s):
            return jax.random.normal(k, shape, dtype=jnp.float32) * scale
        return {'x': n(ks[0], (B, T, D), 1.0), 'ln1_w': jnp.ones((D,), jnp.float32), 'mu_r': jax.random.uniform(ks[1], (D,), jnp.float32), 'mu_k': jax.random.uniform(ks[2], (D,), jnp.float32), 'mu_v': jax.random.uniform(ks[3], (D,), jnp.float32), 'mu_w': jax.random.uniform(ks[4], (D,), jnp.float32), 'mu_g': jax.random.uniform(ks[5], (D,), jnp.float32), 'Wr': n(ks[6], (D, D)), 'Wk': n(ks[7], (D, D)), 'Wv': n(ks[8], (D, D)), 'Wg': n(ks[9], (D, D)), 'Wo': n(ks[10], (D, D)), 'w0': n(ks[11], (D,), 0.5), 'wA': n(ks[12], (D, LORA)), 'wB': n(ks[13], (LORA, D)), 'u': n(ks[14], (H, dk), 0.5), 'gn_w': jnp.ones((H, dk), jnp.float32), 'gn_b': jnp.zeros((H, dk), jnp.float32), 'ln2_w': jnp.ones((D,), jnp.float32), 'ffn_w1': n(ks[15], (D, F)), 'ffn_w2': n(ks[16], (F, D))}
    _L0_attn_in = _L0_attn_setup()

    def _L0_ffn_setup():
        import jax, jax.numpy as jnp
        import numpy as np
        TOP_K = 2
        EPS = 1e-09
        key = jax.random.key(seed)
        ks = jax.random.split(key, 6)
        B, T, D, H, E = (4, 256, 128, 256, 8)
        x = jax.random.normal(ks[0], (B, T, D), dtype=jnp.float32)
        Wg = jax.random.normal(ks[1], (E, D), dtype=jnp.float32) * 0.02
        W1 = jax.random.normal(ks[2], (E, 2 * H, D), dtype=jnp.float32) * 0.02
        b1 = jax.random.normal(ks[3], (E, 2 * H), dtype=jnp.float32) * 0.02
        Wo = jax.random.normal(ks[4], (D, H), dtype=jnp.float32) * 0.02
        bo = jax.random.normal(ks[5], (D,), dtype=jnp.float32) * 0.02
        return {'x': x, 'Wg': Wg, 'W1': W1, 'b1': b1, 'Wo': Wo, 'bo': bo}
    _L0_ffn_in = _L0_ffn_setup()
    _L0_c = _w((lambda *s: np.random.randn(*s).astype(np.float32) * 0.05)(8, 128))
    _L0_wmod = _w((lambda *s: np.random.randn(*s).astype(np.float32) * 0.05)(128, 6 * 128) * 128 ** (-0.5))
    _d = {'L0_attn_x': _L0_attn_in['x'], 'L0_attn_ln1_w': _L0_attn_in['ln1_w'], 'L0_attn_mu_r': _L0_attn_in['mu_r'], 'L0_attn_mu_k': _L0_attn_in['mu_k'], 'L0_attn_mu_v': _L0_attn_in['mu_v'], 'L0_attn_mu_w': _L0_attn_in['mu_w'], 'L0_attn_mu_g': _L0_attn_in['mu_g'], 'L0_attn_Wr': _L0_attn_in['Wr'], 'L0_attn_Wk': _L0_attn_in['Wk'], 'L0_attn_Wv': _L0_attn_in['Wv'], 'L0_attn_Wg': _L0_attn_in['Wg'], 'L0_attn_Wo': _L0_attn_in['Wo'], 'L0_attn_w0': _L0_attn_in['w0'], 'L0_attn_wA': _L0_attn_in['wA'], 'L0_attn_wB': _L0_attn_in['wB'], 'L0_attn_u': _L0_attn_in['u'], 'L0_attn_gn_w': _L0_attn_in['gn_w'], 'L0_attn_gn_b': _L0_attn_in['gn_b'], 'L0_attn_ln2_w': _L0_attn_in['ln2_w'], 'L0_attn_ffn_w1': _L0_attn_in['ffn_w1'], 'L0_attn_ffn_w2': _L0_attn_in['ffn_w2'], 'L0_ffn_Wg': _L0_ffn_in['Wg'], 'L0_ffn_W1': _L0_ffn_in['W1'], 'L0_ffn_b1': _L0_ffn_in['b1'], 'L0_ffn_Wo': _L0_ffn_in['Wo'], 'L0_ffn_bo': _L0_ffn_in['bo'], 'L0_c': _L0_c, 'L0_wmod': _L0_wmod}
    _x0 = _d['L0_attn_x']
    _d['L0_attn_x'] = jax.random.normal(jax.random.fold_in(jax.random.key(seed), 1), (8, 1024, 128), dtype=_x0.dtype)
    del _x0
    return _d

def reference(L0_attn_x, L0_attn_ln1_w, L0_attn_mu_r, L0_attn_mu_k, L0_attn_mu_v, L0_attn_mu_w, L0_attn_mu_g, L0_attn_Wr, L0_attn_Wk, L0_attn_Wv, L0_attn_Wg, L0_attn_Wo, L0_attn_w0, L0_attn_wA, L0_attn_wB, L0_attn_u, L0_attn_gn_w, L0_attn_gn_b, L0_attn_ln2_w, L0_attn_ffn_w1, L0_attn_ffn_w2, L0_ffn_Wg, L0_ffn_W1, L0_ffn_b1, L0_ffn_Wo, L0_ffn_bo, L0_c, L0_wmod):

    def _L0_attn_ref(x, ln1_w, mu_r, mu_k, mu_v, mu_w, mu_g, Wr, Wk, Wv, Wg, Wo, w0, wA, wB, u, gn_w, gn_b, ln2_w, ffn_w1, ffn_w2):
        import jax, jax.numpy as jnp
        import numpy as np
        EPS_RMS = 1e-06
        EPS_GN = 1e-05

        def rms_norm(x, w, eps=EPS_RMS):
            var = jnp.mean(x * x, axis=-1, keepdims=True)
            return w * (x * jax.lax.rsqrt(var + eps))
        B, T, D = x.shape
        H, dk = u.shape
        h = rms_norm(x, ln1_w)
        xx = jnp.pad(h[:, :-1], ((0, 0), (1, 0), (0, 0))) - h
        xr = h + xx * mu_r
        xk = h + xx * mu_k
        xv = h + xx * mu_v
        xw = h + xx * mu_w
        xg = h + xx * mu_g
        r = (xr @ Wr).reshape(B, T, H, dk)
        k = (xk @ Wk).reshape(B, T, H, dk)
        v = (xv @ Wv).reshape(B, T, H, dk)
        g = jax.nn.silu(xg @ Wg)
        w = w0 + jnp.tanh(xw @ wA) @ wB
        decay = jnp.exp(-jnp.exp(w)).reshape(B, T, H, dk)
        rT = jnp.moveaxis(r, 1, 0)
        kT = jnp.moveaxis(k, 1, 0)
        vT = jnp.moveaxis(v, 1, 0)
        dT = jnp.moveaxis(decay, 1, 0)

        def step(S, inps):
            rt, kt, vt, dt = inps
            kv = kt[..., :, None] * vt[..., None, :]
            o = jnp.einsum('bhk,bhkv->bhv', rt, S + u[None, :, :, None] * kv)
            S = dt[..., None] * S + kv
            return (S, o)
        S0 = jnp.zeros((B, H, dk, dk), x.dtype)
        _, oT = jax.lax.scan(step, S0, (rT, kT, vT, dT))
        o = jnp.moveaxis(oT, 0, 1)
        mean = jnp.mean(o, axis=-1, keepdims=True)
        var = jnp.var(o, axis=-1, keepdims=True)
        o = (o - mean) * jax.lax.rsqrt(var + EPS_GN) * gn_w + gn_b
        o = (o * g.reshape(B, T, H, dk)).reshape(B, T, D)
        x = x + o @ Wo
        h2 = rms_norm(x, ln2_w)
        x = x + jax.nn.gelu(h2 @ ffn_w1, approximate=False) @ ffn_w2
        return x

    def _L0_ffn_ref(x, Wg, W1, b1, Wo, bo):
        import jax, jax.numpy as jnp
        import numpy as np
        TOP_K = 2
        EPS = 1e-09
        E = Wg.shape[0]
        gate_logits = jnp.einsum('btd,ed->bte', x, Wg)
        gate_scores = jax.nn.softmax(gate_logits, axis=-1)
        topk_val, topk_idx = jax.lax.top_k(gate_scores, TOP_K)
        topk_val = topk_val / (topk_val.sum(axis=-1, keepdims=True) + EPS)
        comb = (jax.nn.one_hot(topk_idx, E, dtype=x.dtype) * topk_val[..., None]).sum(axis=-2)
        out = jnp.zeros_like(x)
        for e in range(E):
            h = jnp.einsum('btd,hd->bth', x, W1[e]) + b1[e]
            a, b = jnp.split(h, 2, axis=-1)
            g = a * jax.nn.sigmoid(b)
            eo = jnp.einsum('bth,dh->btd', g, Wo) + bo
            out = out + eo * comb[..., e:e + 1]
        return out
    x = L0_attn_x
    mod = (_silu(L0_c) @ L0_wmod).reshape(L0_c.shape[0], 6, 1, -1)
    sa, ca, ga, sb, cb, gb = (mod[:, 0], mod[:, 1], mod[:, 2], mod[:, 3], mod[:, 4], mod[:, 5])
    ga = (2 * (ga >= 0) - 1) * jnp.maximum(jnp.abs(ga), 0.25)
    gb = (2 * (gb >= 0) - 1) * jnp.maximum(jnp.abs(gb), 0.25)
    h = _layernorm(x, axis=-1) * (1 + ca) + sa
    x = x + ga * _L0_attn_ref(h, L0_attn_ln1_w, L0_attn_mu_r, L0_attn_mu_k, L0_attn_mu_v, L0_attn_mu_w, L0_attn_mu_g, L0_attn_Wr, L0_attn_Wk, L0_attn_Wv, L0_attn_Wg, L0_attn_Wo, L0_attn_w0, L0_attn_wA, L0_attn_wB, L0_attn_u, L0_attn_gn_w, L0_attn_gn_b, L0_attn_ln2_w, L0_attn_ffn_w1, L0_attn_ffn_w2)
    h = _layernorm(x, axis=-1) * (1 + cb) + sb
    x = x + gb * _L0_ffn_ref(h, L0_ffn_Wg, L0_ffn_W1, L0_ffn_b1, L0_ffn_Wo, L0_ffn_bo)
    return x

_drawn_inputs = setup_inputs


def setup_inputs(seed=0):
    import zlib

    import numpy as np

    out = dict(_drawn_inputs(seed))
    spreads = {'L0_attn_ln1_w': (1.0, 0.6),
     'L0_attn_gn_w': (1.0, 0.6),
     'L0_attn_gn_b': (0.0, 0.8),
     'L0_attn_ln2_w': (1.0, 0.6)}
    factors = {'L0_attn_mu_r': 8.0,
     'L0_attn_mu_k': 8.0,
     'L0_attn_mu_v': 8.0,
     'L0_attn_mu_w': 8.0,
     'L0_attn_mu_g': 8.0,
     'L0_attn_Wr': 8.0,
     'L0_attn_Wk': 8.0,
     'L0_attn_Wv': 8.0,
     'L0_attn_Wg': 8.0,
     'L0_attn_Wo': 8.0,
     'L0_attn_w0': 8.0,
     'L0_attn_wA': 8.0,
     'L0_attn_wB': 8.0,
     'L0_attn_u': 8.0,
     'L0_attn_ffn_w1': 4.154,
     'L0_attn_ffn_w2': 4.09,
     'L0_ffn_Wg': 8.0,
     'L0_ffn_W1': 8.0,
     'L0_ffn_b1': 64.0,
     'L0_ffn_Wo': 8.0,
     'L0_ffn_bo': 64.0}
    for name, (base, spread) in spreads.items():
        noise = np.random.default_rng([zlib.crc32(name.encode()), seed]).standard_normal(out[name].shape)
        drawn = base * np.exp(spread * noise) if base else spread * noise
        out[name] = jnp.asarray(drawn.astype(out[name].dtype))
    for name, factor in factors.items():
        out[name] = (out[name] * factor).astype(out[name].dtype)
    return out
```

```python
from contextlib import ExitStack

import numpy as np

import concourse.bass as bass
from concourse import mybir

F32 = mybir.dt.float32
F32R = mybir.dt.float32r
ALU = mybir.AluOpType
ACT = mybir.ActivationFunctionType
AX_X = mybir.AxisListType.X

P = 128
EPS_LN = 1e-5
EPS_RMS = 1e-6
EPS_GN = 1e-5
EPS_TOPK = 1e-9
GATE_MIN = 0.25


class Signals:

    def __init__(self, nc, block, names, lists):
        self.by_name = {n: nc.alloc_semaphore(f"{block}_{n}") for n in names}
        for n, k in lists.items():
            self.by_name[n] = [nc.alloc_semaphore(f"{block}_{n}{i}") for i in range(k)]

    def __getitem__(self, name):
        return self.by_name[name]

    def reset(self, nc):
        handles = [h for v in self.by_name.values() for h in (v if isinstance(v, list) else [v])]
        nc.clear_and_free_semaphores(handles)
        nc.all_engine_barrier()


def after(eng, sem, tile, step=1, k=1):
    value = tile * step + k
    if isinstance(value, int) and value <= 0:
        return
    eng.wait_ge(sem, value)


def apart(eng, passed):
    eng.sem_inc(passed, 1)


def build(nc, ins, out):
    x_in = ins["L0_attn_x"]
    B, T, D = x_in.shape
    H, DK = ins["L0_attn_u"].shape
    LORA = ins["L0_attn_wA"].shape[1]
    FF = ins["L0_attn_ffn_w1"].shape[1]
    E, H2, _ = ins["L0_ffn_W1"].shape
    HE = H2 // 2
    NT = 512
    NQ = NT // P
    TPB = T // NT
    TILES = B * TPB
    NF = FF // P
    NH2 = HE // P
    assert D == P and H * DK == P and DK == 8 and TPB == 2 and TILES % 2 == 0 and HE % P == 0 and LORA <= P

    x_rows = x_in.rearrange("b (n q p) d -> (b n) p q d", n=TPB, q=NQ)
    out_rows = out.rearrange("b (n q p) d -> (b n) p q d", n=TPB, q=NQ)
    mods_dram = nc.dram_tensor("mods_scratch", (B, 6, D), F32, kind="Internal").ap()
    x2_dram = nc.dram_tensor("x2_scratch", (TILES, P, NQ, D), F32, kind="Internal").ap()
    h3_dram = nc.dram_tensor("h3_scratch", (TILES, P, NT), F32, kind="Internal").ap()
    comb_dram = nc.dram_tensor("comb_scratch", (TILES, NQ * E, P), F32, kind="Internal").ap()

    with ExitStack() as keep:
        csum_all = keep.enter_context(nc.sbuf_tensor("csum_all", [P, TILES * NQ], F32))
        ident = keep.enter_context(nc.sbuf_tensor("ident", [P, P], F32))
        signals = attention_block(nc, ins, x_rows, mods_dram, x2_dram, h3_dram, comb_dram, csum_all, ident,
                        B, D, H, DK, LORA, NF, E, NT, NQ, TPB, TILES)
        signals.reset(nc)
        expert_block(nc, ins, out_rows, mods_dram, x2_dram, h3_dram, comb_dram, csum_all, ident,
                     B, D, E, HE, NH2, NT, NQ, TPB, TILES)


def attention_block(nc, ins, x_rows, mods_dram, x2_dram, h3_dram, comb_dram, csum_all, ident,
                    B, D, H, DK, LORA, NF, E, NT, NQ, TPB, TILES):
    LAST = TILES - 1
    ORDER = [0, 2, 4, 6, 1, 3, 5, 7]
    STAGES = 6
    (ROW_LN1, ROW_MUR, ROW_MUK, ROW_MUV, ROW_MUW, ROW_MUG, ROW_W0, ROW_U, ROW_LN2, ROW_GNW, ROW_GNB) = range(11)
    NROWS = 11
    SA, A1, GA, SB, A2, GB = range(6)

    with ExitStack() as ctx:
        def sb(name, shape, dt=F32):
            return ctx.enter_context(nc.sbuf_tensor(name, shape, dt))

        def bank(name):
            return ctx.enter_context(nc.psum_tensor(name, [P, 512], F32))

        rows = sb("rows", [NROWS - 2, P])
        gn_rows, gn_turned = sb("gn_rows", [2, P]), sb("gn_turned", [2, P])
        cols = sb("cols", [P, NROWS])
        staged = sb("staged", [P, 6, P])
        wk, wv, wr, wg = (sb(n, [P, P]) for n in ("wk", "wv", "wr", "wg"))
        wa, wb = sb("wa", [P, P]), sb("wb", [P, P])
        wo = sb("wo", [P, P])
        w1 = sb("w1", [P, NF * P])
        w2 = sb("w2", [P, NF, P])
        gate_w = sb("gate_w", [P, P])
        gate_rows = sb("gate_rows", [E, P])
        spread = sb("spread", [P, DK, P], F32R)
        head_of_key = sb("head_of_key", [P, H])
        head_of_val = sb("head_of_val", [P, H])
        reduce_w = sb("reduce_w", [P, 2, 2 * H])
        bonus_w = sb("bonus_w", [P, P])
        center_w = sb("center_w", [P, P])
        minus_half = sb("minus_half", [P, NQ])
        eps_gn = sb("eps_gn", [P, 1])
        c_rows = sb("c_rows", [B, P])
        c_act = sb("c_act", [B, P])
        c_cols = sb("c_cols", [P, B])
        mod_rows = sb("mod_rows", [B, 6, P])
        mods = sb("mods", [P, B, 5, P])
        expert_rank = sb("expert_rank", [P, E])
        xin = [sb(f"xin{i}", [P, NQ, P]) for i in range(2)]
        st1, mv1 = sb("st1", [P, NQ, 6]), sb("mv1", [P, NQ, 2])
        ve1, rs1 = sb("ve1", [P, NQ]), sb("rs1", [P, NQ])
        xn1 = sb("xn1", [P, NQ, P])
        mod_sign, mod_abs = xn1[0:B, 0:2, :], xn1[0:B, 2:4, :]
        h_all = sb("h_all", [P, TILES, NQ, P])
        ssq1, ve2, rs2 = sb("ssq1", [P, NQ]), sb("ve2", [P, NQ]), sb("rs2", [P, NQ])
        hn = sb("hn", [P, NQ, P])
        hnT = [sb(f"hnT{i}", [P, 1 + NT]) for i in range(2)]
        xx = [sb(f"xx{i}", [P, NT]) for i in range(2)]
        mixA, mixB = sb("mixA", [P, NT]), sb("mixB", [P, NT])
        kT, rT, dT, vT = ([sb(f"{n}{i}", [P, NT]) for i in range(2)] for n in ("kT", "rT", "dT", "vT"))
        vhi, vlo = ([sb(f"{n}{i}", [P, NT], F32R) for i in range(2)] for n in ("vhi", "vlo"))
        lora = sb("lora", [P, NT])
        expw = sb("expw", [P, NT])
        mixG, ruk, tanh_g = sb("mixG", [P, NT]), sb("ruk", [P, NT]), sb("tanh_g", [P, NT])
        gate, bonus = ([sb(f"{n}{i}", [P, NT]) for i in range(2)] for n in ("gate", "bonus"))
        kv = [sb(f"kv{i}", [P, NT]) for i in range(2)]
        state = [sb(f"state{i}", [P, NT]) for i in range(3)]
        state_end = sb("state_end", [P, DK])
        rs_prod = [[sb(f"rs_prod{i}_{j}", [P, NT]) for j in range(4)] for i in range(2)]
        o_sum, o_sq = sb("o_sum", [P, NT]), sb("o_sq", [P, NT])
        var_g, sd_g, rs_g = (sb(n, [P, NQ, H]) for n in ("var_g", "sd_g", "rs_g"))
        o_norm, o_aff, o_gated = sb("o_norm", [P, NT]), sb("o_aff", [P, NT]), sb("o_gated", [P, NT])
        ssq3, ve3, rs3 = sb("ssq3", [P, NQ]), sb("ve3", [P, NQ]), sb("rs3", [P, NQ])
        h2, h2T = sb("h2", [P, NQ, P]), sb("h2T", [P, NT])
        gel = [sb(f"gel{c}", [P, NT]) for c in range(NF)]
        y = sb("y", [P, NQ, P])
        xre, x2 = ([sb(f"{n}{i}", [P, NQ, P]) for i in range(2)] for n in ("xre", "x2"))
        st4, mv4 = sb("st4", [P, NQ, 6]), sb("mv4", [P, NQ, 2])
        ve4, rs4 = sb("ve4", [P, NQ]), sb("rs4", [P, NQ])
        xn4, h3 = sb("xn4", [P, NQ, P]), sb("h3", [P, NQ, P])
        h3T = [sb(f"h3T{i}", [P, NT]) for i in range(2)]
        logits = sb("logits", [P, TILES, NQ, E])

        ps_f = [bank("ps_f0"), bank("ps_f1")]
        ps_v = [bank("ps_v0"), bank("ps_v1")]
        ps_o, ps_g, ps_k1, ps_k2 = bank("ps_o"), bank("ps_g"), bank("ps_k1"), bank("ps_k2")

        s = Signals(nc, "attention", (
            "act_passed dve_passed pool_passed vectors_in gn_turned weights_in more_in cond_in ident_zero ident_ready wpad_zero consts_ready "
            "cols_ps cols_ready weights_ready selectors_part selectors_ready gate_ps gate_ready silu_ready cT_ps cT_ready "
            "mod_ps mod_copied mod_step mod_ready mod_stored mods_in setup_step "
            "ln1_stats ln1_mv ln1_ve ln1_rstd xn1_ready h_scaled h_ready ssq1_ready rms1_ve rms1_rstd hn_ready "
            "hnT_ps hnT_ready xx_ready mixk_ready mixv_ready mixw_ready mixr_ready k_ps k_ready v_ps vhi_ready vT_ready "
            "vlo_ready lora_ps lora_ready w_ps expw_ready d_ready r_ps r_ready "
            "mixg_ready g_ps tanh_ready gate_set ruk_ready bonus_ps bonus_ready red_even red_odd "
            "o_ready cen_ps osq_ready var_ready sd_ready rsg_ready onorm_ready onT_ps oaff_ready ogated_ready wo_ps x1_ready "
            "ssq3_ready rms2_ve rms2_rstd h2_ready h2T_ps h2T_ready ffn2_ps y_ready y_gated x2_ready "
            "ln2_stats ln2_mv ln2_ve ln2_rstd xn4_ready h3_scaled h3_ready h3T_ps h3T_ready logits_ps logits_ready "
            "route_step exp_ready comb_ready combT_ps combT_ready comb_stored").split(),
            {"x_loaded": 2, "xre_loaded": 2, "x2_stored": 2, "h3_stored": 2, "spread_ps": 8, "kv_ready": 8,
             "scan_ready": 8, "rs_ready": 8, "ffn1_ps": NF, "gelu_ready": NF})

        def stage_tiles(it):
            return [it - lag for lag in range(STAGES)]

        def active(it):
            return [it is None or 0 <= it - lag <= LAST for lag in range(STAGES)]

        def run_pipeline(eng, step):
            for it in range(STAGES):
                step(it, it, it % 2, it // 2)
            with eng.Fori(STAGES // 2, TILES // 2) as g:
                for u in range(2):
                    step(None, g * 2 + u, u, g)
            for it in range(TILES, TILES + STAGES - 1):
                step(it, it, it % 2, it // 2)

        def upto(tile):
            return min(tile, LAST) if isinstance(tile, int) else tile

        def quarters(ap):
            return ap.rearrange("p (q d) -> p q d", q=NQ)

        def mod_row(which, batch):
            return mods[:, batch, which, :].unsqueeze(1).broadcast_to([P, NQ, P])

        def batch_of(pair, u, lag):
            return pair + (u - lag) // 2

        block = ctx.enter_context(nc.Block())

        @block.sync
        def _(sp):
            sp.dma_start(c_rows[:], ins["L0_c"]).then_inc(s["cond_in"], 16)
            sp.dma_start(staged[:, 0:6, :].rearrange("p a d -> p (a d)"), ins["L0_wmod"]).then_inc(s["cond_in"], 16)
            for row, name in ((ROW_LN1, "ln1_w"), (ROW_MUR, "mu_r"), (ROW_MUK, "mu_k"), (ROW_MUV, "mu_v"),
                              (ROW_MUW, "mu_w"), (ROW_MUG, "mu_g"), (ROW_W0, "w0"), (ROW_LN2, "ln2_w")):
                sp.dma_start(rows[row:row + 1, :], ins["L0_attn_" + name].rearrange("(a d) -> a d", a=1)) \
                    .then_inc(s["vectors_in"], 16)
            sp.dma_start(rows[ROW_U:ROW_U + 1, :].rearrange("a (h k) -> a h k", h=H),
                         ins["L0_attn_u"].rearrange("(a h) k -> a h k", a=1)).then_inc(s["vectors_in"], 16)
            for i, name in enumerate(("gn_w", "gn_b")):
                sp.dma_start(gn_rows[i:i + 1, :].rearrange("a (h j) -> a h j", h=H),
                             ins["L0_attn_" + name].rearrange("(a h) j -> a h j", a=1)).then_inc(s["vectors_in"], 16)
            for j in range(DK):
                sp.dma_start(wo[j * H:(j + 1) * H, :],
                             ins["L0_attn_Wo"].rearrange("(h j) d -> j h d", j=DK)[j]).then_inc(s["more_in"], 16)
            sp.dma_start(w2[:], ins["L0_attn_ffn_w2"].rearrange("(c p) d -> p c d", p=P)).then_inc(s["more_in"], 16)
            sp.dma_start(gate_rows[:], ins["L0_ffn_Wg"]).then_inc(s["more_in"], 16)
            sp.wait_ge(s["wpad_zero"], 3)
            sp.dma_start(wb[0:LORA, :], ins["L0_attn_wB"]).then_inc(s["more_in"], 16)
            sp.dma_start(wa[:, 0:LORA], ins["L0_attn_wA"]).then_inc(s["weights_in"], 16)
            sp.dma_start(w1[:], ins["L0_attn_ffn_w1"]).then_inc(s["weights_in"], 16)
            sp.wait_ge(s["mod_ps"], 2)
            for i, name in enumerate(("Wk", "Wv", "Wr", "Wg")):
                sp.dma_start(staged[:, i, :], ins["L0_attn_" + name]).then_inc(s["weights_in"], 16)
            sp.wait_ge(s["mod_ready"], 1)
            sp.dma_start(mods_dram, mod_rows[:]).then_inc(s["mod_stored"], 16)
            sp.wait_ge(s["mod_stored"], 16)
            sp.dma_start(mods[:], mods_dram[:, 0:5, :].unsqueeze(0).broadcast_to([P, B, 5, P])).then_inc(s["mods_in"], 16)

            def step(it, now, u, pair):
                f1, f2, m, k1, k2, k3 = stage_tiles(now)
                on = active(it)
                if on[0]:
                    p = u
                    after(sp, s["xn1_ready"], f1 - 2)
                    sp.dma_start(xin[p][:], x_rows[f1]).then_inc(s["x_loaded"][p], 16)
                if on[4]:
                    p = u
                    after(sp, s["x2_ready"], k2 - 2)
                    sp.dma_start(xre[p][:], x_rows[k2]).then_inc(s["xre_loaded"][p], 16)
                if on[5]:
                    p = 1 - u
                    after(sp, s["x2_ready"], k3)
                    sp.dma_start(x2_dram[k3], x2[p][:]).then_inc(s["x2_stored"][p], 16)
                    after(sp, s["h3T_ready"], k3)
                    sp.dma_start(h3_dram[k3], h3T[p][:]).then_inc(s["h3_stored"][p], 16)

            run_pipeline(sp, step)
            sp.wait_ge(s["combT_ready"], TILES // 4)
            combT = kv[0][:].rearrange("p (g t) -> p g t", g=TILES // 4)
            for g in range(TILES // 4):
                sp.dma_start(comb_dram[4 * g:4 * g + 4].rearrange("n r t -> (n r) t"), combT[:, g, :]) \
                    .then_inc(s["comb_stored"], 16)
            sp.wait_ge(s["comb_stored"], 16 * (TILES // 4))
            for p in range(2):
                sp.wait_ge(s["x2_stored"][p], 16 * (TILES // 2))
                sp.wait_ge(s["h3_stored"][p], 16 * (TILES // 2))

        @block.gpsimd
        def _(pool):
            pool.memset(wa[:], 0.0).then_inc(s["wpad_zero"], 1)
            pool.memset(wb[:], 0.0).then_inc(s["wpad_zero"], 1)
            pool.memset(gate_w[:], 0.0).then_inc(s["wpad_zero"], 1)
            pool.memset(ident[:], 0.0).then_inc(s["ident_zero"], 1)
            pool.wait_ge(s["ident_zero"], 1)
            pool.affine_select(out=ident[:], in_=ident[:], compare_op=ALU.not_equal, fill=1.0, base=0,
                               pattern=[[-1, P]], channel_multiplier=1).then_inc(s["ident_ready"], 1)
            pool.memset(minus_half[:], -0.5).then_inc(s["consts_ready"], 1)
            pool.memset(eps_gn[:], EPS_GN).then_inc(s["consts_ready"], 1)
            pool.memset(reduce_w[:], 0.0).then_inc(s["consts_ready"], 1)
            pool.memset(hnT[0][:, 0:1], 0.0).then_inc(s["consts_ready"], 1)
            for j in range(4):
                pool.memset(rs_prod[0][j][:, 0:1], 0.0).then_inc(s["consts_ready"], 1)
            for e in range(E):
                pool.memset(expert_rank[:, e:e + 1], float(E - e)).then_inc(s["consts_ready"], 1)
            pool.wait_ge(s["consts_ready"], 16)
            pool.wait_ge(s["mods_in"], 16)

            def rstd(src, tmp, dst, scale, eps, ready_in, tile, mid, done):
                after(pool, ready_in, tile)
                apart(pool, s["pool_passed"])
                pool.tensor_scalar(tmp[:], src, scale, eps, ALU.mult, ALU.add).then_inc(mid, 1)
                after(pool, mid, tile)
                pool.tensor_tensor(dst[:], tmp[:], minus_half[:], ALU.pow).then_inc(done, 1)

            def step(it, now, u, pair):
                f1, f2, m, k1, k2, k3 = stage_tiles(now)
                on = active(it)

                def products(idx):
                    p, j = u, ORDER[idx]
                    dst, st = rs_prod[p][idx % 4], state[idx % 3]
                    if idx == 0:
                        after(pool, s["r_ready"], m)
                    after(pool, s["scan_ready"][idx], m)
                    if idx < 4:
                        after(pool, s["red_odd"], m - 2)
                    else:
                        after(pool, s["red_even"], m)
                    pool.tensor_tensor(dst[:, 1:NT], rT[p][:, 1:NT], st[:, 0:NT - 1], ALU.mult)
                    if p == 0:
                        pool.tensor_copy(state_end[:, j:j + 1], st[:, NT - 1:NT]).then_inc(s["rs_ready"][idx], 1)
                    else:
                        after(pool, s["rs_ready"][idx], m - 1)
                        pool.tensor_tensor(dst[:, 0:1], rT[p][:, 0:1], state_end[:, j:j + 1], ALU.mult) \
                            .then_inc(s["rs_ready"][idx], 1)

                if on[4]:
                    after(pool, s["h2_ready"], k2 - 1)
                    rstd(ssq3[:], ve3, rs3, 1.0 / D, EPS_RMS, s["ssq3_ready"], k2, s["rms2_ve"], s["rms2_rstd"])
                if on[2]:
                    products(0)
                if on[0]:
                    after(pool, s["xn1_ready"], f1 - 1)
                    rstd(mv1[:, :, 1], ve1, rs1, 1.0, EPS_LN, s["ln1_mv"], f1, s["ln1_ve"], s["ln1_rstd"])
                if on[2]:
                    products(1)
                    products(2)
                if on[5]:
                    after(pool, s["xn4_ready"], k3 - 1)
                    rstd(mv4[:, :, 1], ve4, rs4, 1.0, EPS_LN, s["ln2_mv"], k3, s["ln2_ve"], s["ln2_rstd"])
                if on[2]:
                    products(3)
                if on[0]:
                    bt = batch_of(pair, u, 0)
                    after(pool, s["xn1_ready"], f1)
                    apart(pool, s["pool_passed"])
                    pool.tensor_tensor(h_all[:, f1], xn1[:], mod_row(A1, bt), ALU.mult).then_inc(s["h_scaled"], 1)
                    after(pool, s["h_scaled"], f1)
                    apart(pool, s["pool_passed"])
                    pool.tensor_tensor(h_all[:, f1], h_all[:, f1], mod_row(SA, bt), ALU.add).then_inc(s["h_ready"], 1)
                if on[2]:
                    products(4)
                if on[5]:
                    bt = batch_of(pair, u, 5)
                    after(pool, s["xn4_ready"], k3)
                    after(pool, s["h3T_ps"], k3 - 1)
                    apart(pool, s["pool_passed"])
                    pool.tensor_tensor(h3[:], xn4[:], mod_row(A2, bt), ALU.mult).then_inc(s["h3_scaled"], 1)
                    after(pool, s["h3_scaled"], k3)
                    apart(pool, s["pool_passed"])
                    pool.tensor_tensor(h3[:], h3[:], mod_row(SB, bt), ALU.add).then_inc(s["h3_ready"], 1)
                if on[2]:
                    products(5)
                if on[0]:
                    after(pool, s["hn_ready"], f1 - 1)
                    rstd(ssq1[:], ve2, rs2, 1.0 / D, EPS_RMS, s["ssq1_ready"], f1, s["rms1_ve"], s["rms1_rstd"])
                if on[2]:
                    products(6)
                    products(7)
                if on[4]:
                    p, bt = u, batch_of(pair, u, 4)
                    after(pool, s["y_ready"], k2)
                    after(pool, s["xn4_ready"], k2 - 2)
                    after(pool, s["x2_stored"][p], batch_of(pair, u, 4) - 1, 16, 16)
                    apart(pool, s["pool_passed"])
                    pool.tensor_tensor(x2[p][:], y[:], mod_row(GA, bt), ALU.mult).then_inc(s["y_gated"], 1)
                    after(pool, s["y_gated"], k2)
                    after(pool, s["xre_loaded"][p], batch_of(pair, u, 4), 16, 16)
                    pool.tensor_tensor(x2[p][:], x2[p][:], xre[p][:], ALU.add).then_inc(s["x2_ready"], 1)

            run_pipeline(pool, step)

        @block.scalar
        def _(act):
            act.wait_ge(s["cond_in"], 32)
            act.activation(c_act[:], c_rows[:], ACT.Silu).then_inc(s["silu_ready"], 1)
            act.wait_ge(s["cT_ps"], 1)
            act.activation(c_cols[:], ps_k1[:, 0:B], ACT.Copy).then_inc(s["cT_ready"], 1)
            for i in range(2):
                act.wait_ge(s["mod_ps"], i + 1)
                act.activation(mod_rows[:, 3 * i:3 * i + 3, :].rearrange("b a d -> b (a d)"), ps_f[i][0:B, 0:3 * P],
                               ACT.Copy).then_inc(s["mod_copied"], 1)
            act.wait_ge(s["cols_ps"], 1)
            act.activation(cols[:], ps_k2[:, 0:NROWS], ACT.Copy).then_inc(s["cols_ready"], 1)
            act.wait_ge(s["gate_ps"], 1)
            act.wait_ge(s["wpad_zero"], 3)
            act.activation(gate_w[:, 0:E], ps_o[:, 0:E], ACT.Copy).then_inc(s["gate_ready"], 1)
            act.wait_ge(s["consts_ready"], 16)
            act.wait_ge(s["setup_step"], 2)

            def sum_squares(src, room, dst, done):
                for q in range(NQ):
                    ins_ = act.activation(room[:, q, :], src[:, q, :], ACT.Square, accum_out=dst[:, q:q + 1])
                ins_.then_inc(done, 1)

            def scale_rows(dst, src, scale, done):
                for q in range(NQ):
                    ins_ = act.activation(dst[:, q, :], src[:, q, :], ACT.Copy, scale=scale[:, q:q + 1])
                ins_.then_inc(done, 1)

            def step(it, now, u, pair):
                f1, f2, m, k1, k2, k3 = stage_tiles(now)
                on = active(it)

                def gelu(c):
                    after(act, s["ffn1_ps"][c], k2)
                    after(act, s["ffn2_ps"], k2 - 1)
                    act.activation(gel[c][:], (ps_k2 if c % 2 == 0 else ps_g)[:], ACT.Gelu).then_inc(s["gelu_ready"][c], 1)

                if on[4]:
                    after(act, s["x1_ready"], k2)
                    after(act, s["rms2_ve"], k2 - 1)
                    after(act, s["h2T_ps"], k2 - 1)
                    apart(act, s["act_passed"])
                    sum_squares(h_all[:, k2], h2, ssq3, s["ssq3_ready"])
                if on[2]:
                    after(act, s["g_ps"], m)
                    after(act, s["gate_set"], m - 1)
                    act.activation(tanh_g[:], ps_g[:], ACT.Tanh, scale=0.5).then_inc(s["tanh_ready"], 1)
                if on[1]:
                    p = 1 - u
                    after(act, s["mixg_ready"], f2 - 2)
                    if p == 1:
                        after(act, s["hnT_ready"], f2 - 1)
                        act.activation(hnT[1][:, 0:1], hnT[0][:, NT:NT + 1], ACT.Copy)
                    after(act, s["hnT_ps"], f2)
                    act.activation(hnT[p][:, 1:NT + 1], ps_f[0][:], ACT.Copy).then_inc(s["hnT_ready"], 1)
                if on[3]:
                    after(act, s["cen_ps"], k1)
                    after(act, s["var_ready"], k1 - 1)
                    act.activation(o_sq[:], ps_k1[:], ACT.Square).then_inc(s["osq_ready"], 1)
                if on[4]:
                    after(act, s["rms2_rstd"], k2)
                    apart(act, s["act_passed"])
                    scale_rows(h2, h_all[:, k2], rs3, s["h2_ready"])
                if on[3]:
                    after(act, s["var_ready"], k1)
                    after(act, s["rsg_ready"], k1 - 1)
                    act.activation(sd_g[:], var_g[:], ACT.Sqrt, scale=1.0 / DK, bias=eps_gn[:]).then_inc(s["sd_ready"], 1)
                if on[4]:
                    after(act, s["h2T_ps"], k2)
                    after(act, s["ffn1_ps"][NF - 1], k2 - 1)
                    act.activation(h2T[:], ps_k2[:], ACT.Copy).then_inc(s["h2T_ready"], 1)
                if on[1]:
                    p = 1 - u
                    after(act, s["k_ps"], f2)
                    after(act, s["kv_ready"][DK - 1], f2 - 2)
                    after(act, s["ruk_ready"], f2 - 2)
                    act.activation(kT[p][:], ps_f[1][:], ACT.Copy).then_inc(s["k_ready"], 1)
                if on[4]:
                    gelu(0)
                if on[1]:
                    after(act, s["v_ps"], f2)
                    after(act, s["spread_ps"][DK - 1], f2 - 2)
                    act.activation(vhi[p][:], ps_f[0][:], ACT.Copy).then_inc(s["vhi_ready"], 1)
                    after(act, s["bonus_ready"], f2 - 2)
                    act.activation(vT[p][:], ps_f[0][:], ACT.Copy).then_inc(s["vT_ready"], 1)
                if on[4]:
                    gelu(1)
                if on[3]:
                    after(act, s["onT_ps"], k1)
                    after(act, s["ogated_ready"], k1 - 1)
                    act.activation(o_aff[:], ps_k1[:], ACT.Identity, scale=cols[:, ROW_GNW:ROW_GNW + 1],
                                   bias=cols[:, ROW_GNB:ROW_GNB + 1]).then_inc(s["oaff_ready"], 1)
                if on[4]:
                    gelu(2)
                if on[1]:
                    after(act, s["lora_ps"], f2)
                    after(act, s["w_ps"], f2 - 1)
                    act.activation(lora[:], ps_f[1][:], ACT.Tanh).then_inc(s["lora_ready"], 1)
                if on[4]:
                    gelu(3)
                if on[0]:
                    after(act, s["h_ready"], f1)
                    after(act, s["rms1_ve"], f1 - 1)
                    after(act, s["hnT_ps"], f1 - 1)
                    apart(act, s["act_passed"])
                    sum_squares(h_all[:, f1], hn, ssq1, s["ssq1_ready"])
                if on[1]:
                    p = 1 - u
                    after(act, s["w_ps"], f2)
                    act.activation(expw[:], ps_f[0][:], ACT.Exp, bias=cols[:, ROW_W0:ROW_W0 + 1]).then_inc(s["expw_ready"], 1)
                    after(act, s["expw_ready"], f2)
                    after(act, s["scan_ready"][DK - 1], f2 - 2)
                    act.activation(dT[p][:], expw[:], ACT.Exp, scale=-1.0).then_inc(s["d_ready"], 1)
                    after(act, s["r_ps"], f2)
                    after(act, s["rs_ready"][DK - 1], f2 - 2)
                    act.activation(rT[p][:], ps_f[1][:], ACT.Copy).then_inc(s["r_ready"], 1)
                if on[0]:
                    after(act, s["rms1_rstd"], f1)
                    apart(act, s["act_passed"])
                    scale_rows(hn, h_all[:, f1], rs2, s["hn_ready"])
                if on[5]:
                    p = 1 - u
                    after(act, s["h3T_ps"], k3)
                    after(act, s["h3_stored"][p], batch_of(pair, u, 5) - 1, 16, 16)
                    act.activation(h3T[p][:], ps_k2[:], ACT.Copy).then_inc(s["h3T_ready"], 1)
                    after(act, s["logits_ps"], k3)
                    apart(act, s["act_passed"])
                    act.activation(logits[:, k3], quarters(ps_k2[:])[:, :, 0:E], ACT.Copy).then_inc(s["logits_ready"], 1)

            run_pipeline(act, step)
            act.wait_ge(s["route_step"], 2)
            lg = logits[:].rearrange("p n q e -> p (n q e)")
            act.activation(lg, lg, ACT.Exp).then_inc(s["exp_ready"], 1)
            combT = kv[0][:].rearrange("p (g t) -> p g t", g=TILES // 4)
            for g in range(TILES // 4):
                act.wait_ge(s["combT_ps"], g + 1)
                act.activation(combT[:, g, :], (ps_k1, ps_k2)[g % 2][:, 0:P], ACT.Copy).then_inc(s["combT_ready"], 1)

        @block.tensor
        def _(pe):
            pe.wait_ge(s["ident_ready"], 1)
            pe.wait_ge(s["silu_ready"], 1)
            pe.transpose(ps_k1[:, 0:B], c_act[:], ident[0:B, 0:B]).then_inc(s["cT_ps"], 1)
            pe.wait_ge(s["cT_ready"], 1)
            for i in range(2):
                pe.matmul(ps_f[i][0:B, 0:3 * P], c_cols[:], staged[:, 3 * i:3 * i + 3, :].rearrange("p a d -> p (a d)"),
                          start=True, stop=True).then_inc(s["mod_ps"], 1)
            pe.wait_ge(s["vectors_in"], 16 * NROWS)
            pe.transpose(ps_k2[:, 0:ROW_GNW], rows[:], ident[0:ROW_GNW, 0:ROW_GNW])
            pe.wait_ge(s["gn_turned"], 1)
            pe.transpose(ps_k2[:, ROW_GNW:NROWS], gn_turned[:], ident[0:2, 0:2]).then_inc(s["cols_ps"], 1)
            pe.wait_ge(s["more_in"], 16 * (DK + 3))
            pe.transpose(ps_o[:, 0:E], gate_rows[:], ident[0:E, 0:E]).then_inc(s["gate_ps"], 1)
            pe.wait_ge(s["mod_copied"], 2)
            pe.wait_ge(s["cols_ready"], 1)
            pe.wait_ge(s["gate_ready"], 1)
            pe.wait_ge(s["setup_step"], 2)

            def step(it, now, u, pair):
                f1, f2, m, k1, k2, k3 = stage_tiles(now)
                on = active(it)

                def turn(dst, src, done):
                    for q in range(NQ):
                        mm = pe.transpose(dst[:, q * P:(q + 1) * P], src[:, q, :], ident[:])
                    mm.then_inc(done, 1)

                def spread_v(idx):
                    if not on[2]:
                        return
                    p, j = u, ORDER[idx]
                    if idx == 0:
                        after(pe, s["vhi_ready"], m)
                        after(pe, s["vlo_ready"], m)
                    after(pe, s["kv_ready"][(idx - 2) % DK], m if idx >= 2 else m - 1)
                    pe.matmul(ps_v[idx % 2][:], spread[:, j, :], vhi[p][:], start=True, stop=False)
                    pe.matmul(ps_v[idx % 2][:], spread[:, j, :], vlo[p][:], start=False, stop=True) \
                        .then_inc(s["spread_ps"][idx], 1)

                def reduce_heads(tile, p, half, done):
                    after(pe, s["rs_ready"][4 * half + 3], tile)
                    for quad in range(4):
                        mm = pe.matmul(ps_o[32 * quad:32 * quad + 32, :], reduce_w[:, half, :], rs_prod[p][quad][:],
                                       start=(half == 0), stop=(half == 1))
                    mm.then_inc(done, 1)

                def ffn1(c):
                    if not on[4]:
                        return
                    dst = ps_k2 if c % 2 == 0 else ps_g
                    if c == 0:
                        after(pe, s["h2T_ready"], k2)
                    elif c == 1:
                        after(pe, s["bonus_ready"], upto(k2 + 2))
                    else:
                        after(pe, s["gelu_ready"][c - 2], k2)
                    pe.matmul(dst[:], w1[:, c * P:(c + 1) * P], h2T[:], start=True, stop=True).then_inc(s["ffn1_ps"][c], 1)

                def project(dst, w, src, done):
                    pe.matmul(dst[:], w[:], src[:], start=True, stop=True).then_inc(done, 1)

                if on[3]:
                    reduce_heads(k1, 1 - u, 1, s["red_odd"])
                spread_v(0)
                spread_v(1)
                if on[2]:
                    after(pe, s["mixg_ready"], m)
                    after(pe, s["gelu_ready"][NF - 1], m - 3)
                    project(ps_g, wg, mixG, s["g_ps"])
                if on[3]:
                    after(pe, s["o_ready"], k1)
                    after(pe, s["x1_ready"], k1 - 1)
                    for q in range(NQ):
                        mm = pe.matmul(ps_k1[:, q * P:(q + 1) * P], o_sum[:, q * P:(q + 1) * P], center_w[:],
                                       start=True, stop=True)
                    mm.then_inc(s["cen_ps"], 1)
                if on[1]:
                    after(pe, s["hn_ready"], f2)
                    after(pe, s["expw_ready"], f2 - 1)
                    turn(ps_f[0], hn, s["hnT_ps"])
                spread_v(2)
                if on[4]:
                    after(pe, s["h2_ready"], k2)
                    after(pe, s["logits_ready"], k2 - 2)
                    if it is not None:
                        after(pe, s["y_ready"], k2 - 1)
                    turn(ps_k2, h2, s["h2T_ps"])
                spread_v(3)
                if on[2]:
                    after(pe, s["ruk_ready"], m)
                    after(pe, s["gate_set"], m)
                    project(ps_g, bonus_w, ruk, s["bonus_ps"])
                ffn1(0)
                spread_v(4)
                if on[1]:
                    after(pe, s["mixk_ready"], f2)
                    after(pe, s["r_ready"], f2 - 1)
                    project(ps_f[1], wk, mixA, s["k_ps"])
                if on[3]:
                    after(pe, s["onorm_ready"], k1)
                    turn(ps_k1, quarters(o_norm[:]), s["onT_ps"])
                if on[2]:
                    after(pe, s["o_ready"], m - 1)
                    reduce_heads(m, u, 0, s["red_even"])
                ffn1(1)
                spread_v(5)
                if on[1]:
                    after(pe, s["mixv_ready"], f2)
                    after(pe, s["hnT_ready"], f2)
                    project(ps_f[0], wv, mixB, s["v_ps"])
                ffn1(2)
                spread_v(6)
                if on[3]:
                    after(pe, s["ogated_ready"], k1)
                    after(pe, s["oaff_ready"], k1)
                    for q in range(NQ):
                        mm = pe.matmul(ps_k1[:, q * P:(q + 1) * P], o_gated[:, q * P:(q + 1) * P], wo[:],
                                       start=True, stop=True)
                    mm.then_inc(s["wo_ps"], 1)
                if on[1]:
                    after(pe, s["mixw_ready"], f2)
                    after(pe, s["k_ready"], f2)
                    project(ps_f[1], wa, mixA, s["lora_ps"])
                ffn1(3)
                spread_v(7)
                if on[1]:
                    after(pe, s["lora_ready"], f2)
                    after(pe, s["vT_ready"], f2)
                    after(pe, s["vlo_ready"], f2)
                    project(ps_f[0], wb, lora, s["w_ps"])
                    after(pe, s["mixr_ready"], f2)
                    project(ps_f[1], wr, mixB, s["r_ps"])
                if on[4]:
                    after(pe, s["gelu_ready"][2], k2)
                    after(pe, s["gelu_ready"][3], k2)
                    for q in range(NQ):
                        for c in range(NF):
                            mm = pe.matmul(ps_k2[:, q * P:(q + 1) * P], gel[c][:, q * P:(q + 1) * P], w2[:, c, :],
                                           start=(c == 0), stop=(c == NF - 1))
                    mm.then_inc(s["ffn2_ps"], 1)
                if on[5]:
                    p = 1 - u
                    after(pe, s["h3_ready"], k3)
                    after(pe, s["y_ready"], upto(k3 + 1))
                    if it is not None:
                        after(pe, s["logits_ready"], k3 - 1)
                    turn(ps_k2, h3, s["h3T_ps"])
                    after(pe, s["h3T_ready"], k3)
                    for q in range(NQ):
                        mm = pe.matmul(ps_k2[:, q * P:(q + 1) * P], h3T[p][:, q * P:(q + 1) * P], gate_w[:],
                                       start=True, stop=True)
                    mm.then_inc(s["logits_ps"], 1)

            run_pipeline(pe, step)
            pe.wait_ge(s["comb_ready"], 1)
            comb_cols = mixA[:]
            for g in range(TILES // 4):
                if g >= 2:
                    pe.wait_ge(s["combT_ready"], g - 1)
                pe.transpose((ps_k1, ps_k2)[g % 2][:, 0:P], comb_cols[:, g * P:(g + 1) * P], ident[:]).then_inc(s["combT_ps"], 1)

        @block.vector
        def _(dve):
            dve.wait_ge(s["ident_ready"], 1)
            dve.wait_ge(s["consts_ready"], 16)
            dve.tensor_reduce(head_of_key[:], ident[:].rearrange("p (h k) -> p h k", h=H), AX_X, ALU.add) \
                .then_inc(s["selectors_part"], 1)
            dve.tensor_reduce(head_of_val[:], ident[:].rearrange("p (j h) -> p h j", h=H), AX_X, ALU.add) \
                .then_inc(s["selectors_part"], 1)
            dve.wait_ge(s["selectors_part"], 2)
            for half in range(2):
                dve.tensor_copy(reduce_w[:, half, half * H:(half + 1) * H], head_of_key[:])
            dve.tensor_copy(bonus_w[:].rearrange("p (j h) -> p j h", h=H), head_of_key[:].unsqueeze(1).broadcast_to([P, DK, H]))
            dve.scalar_tensor_tensor(out=center_w[:].rearrange("p (j h) -> p j h", h=H),
                                     in0=head_of_val[:].unsqueeze(1).broadcast_to([P, DK, H]), scalar=-1.0 / DK,
                                     in1=ident[:].rearrange("p (j h) -> p j h", h=H), op0=ALU.mult, op1=ALU.add)
            for j in range(DK):
                last = dve.tensor_copy(spread[:, j, :].rearrange("p (h k) -> p h k", h=H),
                                       ident[:, j * H:(j + 1) * H].unsqueeze(2).broadcast_to([P, H, DK]))
            last.then_inc(s["setup_step"], 1)
            dve.wait_ge(s["vectors_in"], 16 * NROWS)
            dve.tensor_copy(gn_turned[:].rearrange("a (j h) -> a j h", h=H),
                            gn_rows[:].rearrange("a (h j) -> a j h", h=H)).then_inc(s["gn_turned"], 1)
            dve.wait_ge(s["mod_copied"], 2)
            pair_of = mod_rows[:].rearrange("b (g a) d -> b g a d", g=2)
            dve.tensor_scalar(mod_sign, pair_of[:, :, 2, :], 0.0, 2.0, ALU.is_ge, ALU.mult).then_inc(s["mod_step"], 1)
            dve.tensor_scalar(mod_abs, pair_of[:, :, 2, :], -1.0, None, ALU.mult).then_inc(s["mod_step"], 1)
            dve.wait_ge(s["mod_step"], 2)
            dve.tensor_tensor(mod_abs, mod_abs, pair_of[:, :, 2, :], ALU.max).then_inc(s["mod_step"], 1)
            dve.wait_ge(s["mod_step"], 3)
            dve.tensor_scalar(mod_abs, mod_abs, GATE_MIN, None, ALU.max).then_inc(s["mod_step"], 1)
            dve.wait_ge(s["mod_step"], 4)
            dve.scalar_tensor_tensor(out=pair_of[:, :, 2, :], in0=mod_sign, scalar=-1.0, in1=mod_abs,
                                     op0=ALU.add, op1=ALU.mult)
            dve.tensor_scalar(pair_of[:, :, 1, :], pair_of[:, :, 1, :], 1.0, None, ALU.add).then_inc(s["mod_ready"], 1)
            dve.wait_ge(s["cols_ready"], 1)
            dve.wait_ge(s["weights_in"], 16 * 6)
            ln1, ln2 = cols[:, ROW_LN1:ROW_LN1 + 1], cols[:, ROW_LN2:ROW_LN2 + 1]
            for i, w in ((0, wk), (2, wr)):
                dve.tensor_scalar(w[:], staged[:, i, :], ln1, None, ALU.mult)
            for i, w in ((1, wv), (3, wg)):
                dve.tensor_scalar(w[:].rearrange("p (j h) -> p j h", h=H),
                                  staged[:, i, :].rearrange("p (h j) -> p j h", h=H), ln1, None, ALU.mult)
            dve.tensor_scalar(wa[:], wa[:], ln1, None, ALU.mult)
            dve.tensor_scalar(cols[:, ROW_GNW:ROW_GNB + 1], cols[:, ROW_GNW:ROW_GNB + 1], 0.5, None, ALU.mult)
            dve.tensor_scalar(w1[:], w1[:], ln2, None, ALU.mult).then_inc(s["setup_step"], 1)

            def token_stats(src, st, mv, done_stats, done_mv, tile, read_by):
                for q in range(NQ):
                    ins_ = dve.bn_stats(st[:, q, :], src[:, q, :])
                ins_.then_inc(done_stats, 1)
                after(dve, done_stats, tile)
                after(dve, read_by, tile - 1)
                apart(dve, s["dve_passed"])
                for q in range(NQ):
                    ins_ = dve.bn_aggr(mv[:, q, :], st[:, q, :])
                ins_.then_inc(done_mv, 1)

            def normalize(dst, src, mv, rs, done):
                for q in range(NQ):
                    ins_ = dve.tensor_scalar(dst[:, q, :], src[:, q, :], mv[:, q, 0:1], rs[:, q:q + 1],
                                             ALU.subtract, ALU.mult)
                ins_.then_inc(done, 1)

            def step(it, now, u, pair):
                f1, f2, m, k1, k2, k3 = stage_tiles(now)
                on = active(it)

                def mix(dst, p, row, done):
                    dve.scalar_tensor_tensor(out=dst[:], in0=xx[p][:], scalar=cols[:, row:row + 1],
                                             in1=hnT[p][:, 1:NT + 1], op0=ALU.mult, op1=ALU.add).then_inc(done, 1)

                def scan(idx):
                    if not on[2]:
                        return
                    p, j = u, ORDER[idx]
                    if idx == 0:
                        after(dve, s["k_ready"], m)
                    after(dve, s["spread_ps"][idx], m)
                    dve.tensor_tensor(kv[idx % 2][:], ps_v[idx % 2][:], kT[p][:], ALU.mult).then_inc(s["kv_ready"][idx], 1)
                    after(dve, s["kv_ready"][idx], m)
                    if idx == 0:
                        after(dve, s["d_ready"], m)
                    after(dve, s["rs_ready"][(idx - 3) % DK], m if idx >= 3 else m - 1)
                    first = 0.0
                    if p == 1:
                        after(dve, s["rs_ready"][idx], m - 1)
                        first = state_end[:, j:j + 1]
                    dve.tensor_tensor_scan(state[idx % 3][:], dT[p][:], kv[idx % 2][:], first, ALU.mult, ALU.add) \
                        .then_inc(s["scan_ready"][idx], 1)

                scan(0)
                if on[3]:
                    p = 1 - u
                    after(dve, s["red_odd"], k1)
                    after(dve, s["bonus_ready"], k1)
                    after(dve, s["cen_ps"], k1 - 1)
                    dve.tensor_tensor(o_sum[:], ps_o[:], bonus[p][:], ALU.add).then_inc(s["o_ready"], 1)
                if on[2]:
                    after(dve, s["hnT_ready"], m)
                    after(dve, s["xx_ready"], m)
                    after(dve, s["g_ps"], m - 1)
                    mix(mixG, u, ROW_MUG, s["mixg_ready"])
                if on[0]:
                    after(dve, s["x_loaded"][u], pair, 16, 16)
                    token_stats(xin[u], st1, mv1, s["ln1_stats"], s["ln1_mv"], f1, s["ln1_ve"])
                scan(1)
                if on[2]:
                    after(dve, s["r_ready"], m)
                    after(dve, s["bonus_ps"], m - 1)
                    dve.scalar_tensor_tensor(out=ruk[:], in0=rT[u][:], scalar=cols[:, ROW_U:ROW_U + 1], in1=kT[u][:],
                                             op0=ALU.mult, op1=ALU.mult).then_inc(s["ruk_ready"], 1)
                if on[5]:
                    p = 1 - u
                    after(dve, s["x2_ready"], k3)
                    token_stats(x2[p], st4, mv4, s["ln2_stats"], s["ln2_mv"], k3, s["ln2_ve"])
                scan(2)
                if on[2]:
                    after(dve, s["tanh_ready"], m)
                    dve.scalar_tensor_tensor(out=gate[u][:], in0=tanh_g[:], scalar=1.0, in1=ps_g[:],
                                             op0=ALU.add, op1=ALU.mult).then_inc(s["gate_set"], 1)
                if on[3]:
                    after(dve, s["osq_ready"], k1)
                    after(dve, s["sd_ready"], k1 - 1)
                    dve.tensor_reduce(var_g[:], o_sq[:].rearrange("p (q j h) -> p q h j", q=NQ, h=H), AX_X, ALU.add) \
                        .then_inc(s["var_ready"], 1)
                if on[1]:
                    p = 1 - u
                    after(dve, s["hnT_ready"], f2)
                    dve.tensor_tensor(xx[p][:], hnT[p][:, 0:NT], hnT[p][:, 1:NT + 1], ALU.subtract).then_inc(s["xx_ready"], 1)
                    after(dve, s["xx_ready"], f2)
                    after(dve, s["lora_ps"], f2 - 1)
                    mix(mixA, p, ROW_MUK, s["mixk_ready"])
                scan(3)
                if on[2]:
                    after(dve, s["bonus_ps"], m)
                    after(dve, s["vT_ready"], m)
                    dve.tensor_tensor(bonus[u][:], ps_g[:], vT[u][:], ALU.mult).then_inc(s["bonus_ready"], 1)
                if on[1]:
                    after(dve, s["r_ps"], f2 - 1)
                    mix(mixB, 1 - u, ROW_MUV, s["mixv_ready"])
                if on[3]:
                    after(dve, s["sd_ready"], k1)
                    dve.reciprocal(rs_g[:], sd_g[:]).then_inc(s["rsg_ready"], 1)
                    after(dve, s["rsg_ready"], k1)
                    after(dve, s["onT_ps"], k1 - 1)
                    dve.tensor_tensor(o_norm[:].rearrange("p (q j h) -> p q j h", q=NQ, h=H),
                                      ps_k1[:].rearrange("p (q j h) -> p q j h", q=NQ, h=H),
                                      rs_g[:].unsqueeze(2).broadcast_to([P, NQ, DK, H]), ALU.mult) \
                        .then_inc(s["onorm_ready"], 1)
                scan(4)
                if on[0]:
                    after(dve, s["ln1_rstd"], f1)
                    after(dve, s["h_scaled"], f1 - 1)
                    normalize(xn1, xin[u], mv1, rs1, s["xn1_ready"])
                if on[5]:
                    after(dve, s["ln2_rstd"], k3)
                    after(dve, s["h3_scaled"], k3 - 1)
                    normalize(xn4, x2[1 - u], mv4, rs4, s["xn4_ready"])
                scan(5)
                if on[1]:
                    p = 1 - u
                    after(dve, s["vT_ready"], f2)
                    after(dve, s["spread_ps"][DK - 1], f2 - 2)
                    dve.tensor_tensor(vlo[p][:], ps_f[0][:], vhi[p][:].bitcast(F32), ALU.subtract).then_inc(s["vlo_ready"], 1)
                    after(dve, s["k_ps"], f2)
                    mix(mixA, p, ROW_MUW, s["mixw_ready"])
                    after(dve, s["v_ps"], f2)
                    mix(mixB, p, ROW_MUR, s["mixr_ready"])
                if on[3]:
                    p = 1 - u
                    after(dve, s["oaff_ready"], k1)
                    after(dve, s["wo_ps"], k1 - 1)
                    dve.tensor_tensor(o_gated[:], o_aff[:], gate[p][:], ALU.mult).then_inc(s["ogated_ready"], 1)
                scan(6)
                if on[3]:
                    after(dve, s["wo_ps"], k1)
                    dve.tensor_tensor(h_all[:, k1], quarters(ps_k1[:]), h_all[:, k1], ALU.add).then_inc(s["x1_ready"], 1)
                scan(7)
                if on[4]:
                    after(dve, s["ffn2_ps"], k2)
                    after(dve, s["y_gated"], k2 - 1)
                    dve.tensor_tensor(y[:], quarters(ps_k2[:]), h_all[:, k2], ALU.add).then_inc(s["y_ready"], 1)

            run_pipeline(dve, step)

            G = TILES * NQ
            lg = logits[:].rearrange("p n q e -> p (n q) e")
            hit = mixB[:].rearrange("p (g e) -> p g e", e=E)
            first = mixG[:].rearrange("p (g e) -> p g e", e=E)
            second = ruk[:].rearrange("p (g e) -> p g e", e=E)
            comb = mixA[:].rearrange("p (g e) -> p g e", e=E)
            top = kv[1][:].rearrange("p (a g) -> p a g", g=G)
            count = [0]

            def done(ins_):
                count[0] += 1
                ins_.then_inc(s["route_step"], 1)
                dve.wait_ge(s["route_step"], count[0])

            def wide(ap):
                return ap.unsqueeze(2).broadcast_to([P, G, E])

            rank = expert_rank[:].unsqueeze(1).broadcast_to([P, G, E])
            MAXL, Z, P1, R1, P2, R2, DEN = range(7)
            dve.wait_ge(s["logits_ready"], TILES)
            done(dve.tensor_reduce(top[:, MAXL, :], lg, AX_X, ALU.max))
            done(dve.tensor_tensor(lg, lg, wide(top[:, MAXL, :]), ALU.subtract))
            dve.wait_ge(s["exp_ready"], 1)
            done(dve.tensor_reduce(top[:, Z, :], lg, AX_X, ALU.add))
            done(dve.reciprocal(top[:, Z, :], top[:, Z, :]))
            done(dve.tensor_tensor(lg, lg, wide(top[:, Z, :]), ALU.mult))
            for value, place, mask in ((P1, R1, first), (P2, R2, second)):
                done(dve.tensor_reduce(top[:, value, :], lg, AX_X, ALU.max))
                done(dve.tensor_tensor(hit, lg, wide(top[:, value, :]), ALU.is_equal))
                done(dve.tensor_tensor(hit, hit, rank, ALU.mult))
                done(dve.tensor_reduce(top[:, place, :], hit, AX_X, ALU.max))
                done(dve.tensor_tensor(mask, rank, wide(top[:, place, :]), ALU.is_equal))
                if value == P1:
                    done(dve.scalar_tensor_tensor(out=lg, in0=mask, scalar=-2.0, in1=lg, op0=ALU.mult, op1=ALU.add))
            done(dve.scalar_tensor_tensor(out=top[:, DEN, :], in0=top[:, P1, :], scalar=EPS_TOPK, in1=top[:, P2, :],
                                          op0=ALU.add, op1=ALU.add))
            done(dve.reciprocal(top[:, DEN, :], top[:, DEN, :]))
            done(dve.tensor_tensor(top[:, P1, :], top[:, P1, :], top[:, DEN, :], ALU.mult))
            done(dve.tensor_tensor(top[:, P2, :], top[:, P2, :], top[:, DEN, :], ALU.mult))
            done(dve.tensor_tensor(csum_all[:], top[:, P1, :], top[:, P2, :], ALU.add))
            done(dve.tensor_tensor(first, first, wide(top[:, P1, :]), ALU.mult))
            done(dve.tensor_tensor(second, second, wide(top[:, P2, :]), ALU.mult))
            dve.tensor_tensor(comb, first, second, ALU.add).then_inc(s["comb_ready"], 1)

    return s


def expert_block(nc, ins, out_rows, mods_dram, x2_dram, h3_dram, comb_dram, csum_all, ident,
                 B, D, E, HE, NH2, NT, NQ, TPB, TILES):
    UNITS = E * NH2
    HALF = UNITS // 2
    DEPTH = 4
    TURN = UNITS // DEPTH
    CH = 2 * NH2
    GB = 5
    PEELED = 3
    with ExitStack() as ctx:
        def sb(name, shape, dt=F32):
            return ctx.enter_context(nc.sbuf_tensor(name, shape, dt))

        def bank(name):
            return ctx.enter_context(nc.psum_tensor(name, [P, 512], F32))

        w_rows = sb("w_rows", [P, E, CH, P])
        w_hi, w_lo = sb("w_hi", [P, E, CH * P], F32R), sb("w_lo", [P, E, CH * P], F32R)
        b1_rows, b1_cols = sb("b1_rows", [E * CH, P]), sb("b1_cols", [P, E * CH])
        out_w_rows, out_w = sb("out_w_rows", [P, HE]), sb("out_w", [P, NH2, P])
        out_b = sb("out_b", [P, P])
        gb_all = sb("gb_all", [P, B, P])
        h3 = [sb(f"h3_in{i}", [P, NT]) for i in range(2)]
        x_hi, x_lo = ([sb(f"{n}{i}", [P, NT], F32R) for i in range(2)] for n in ("x_hi", "x_lo"))
        comb = [sb(f"comb{i}", [P, NQ, E, P]) for i in range(2)]
        x2 = [sb(f"x2_in{i}", [P, NQ, P]) for i in range(2)]
        sig = [sb(f"sig{i}", [P, NT]) for i in range(DEPTH)]
        weighed = [sb(f"weighed{i}", [P, NT]) for i in range(DEPTH)]
        glu = [sb(f"glu{i}", [P, NT]) for i in range(DEPTH)]
        total = [[sb(f"total{i}_{h}", [P, NT]) for h in range(NH2)] for i in range(2)]
        moe = sb("moe", [P, NQ, P])
        res = [sb(f"res{i}", [P, NQ, P]) for i in range(2)]
        ps_a, ps_b = ([bank(f"{n}{i}") for i in range(k)] for n, k in (("ps_a", DEPTH), ("ps_b", 2)))
        ps_w = bank("ps_w")

        s = Signals(nc, "experts", (
            "pool_passed small_in w_ps w_hi_ready w_lo_ready small_ps small_ready "
            "x_hi_ready x_lo_ready out_ps moe_ready moe_gated res_ready total_ready").split(),
            {"w_in": E, "h3_loaded": 2, "comb_loaded": 2, "x2e_loaded": 2, "stored": 2,
             "b_ps": 2, "added": 2, "a_ps": DEPTH, "sig_ready": DEPTH, "weighed_ready": DEPTH, "glu_ready": DEPTH})

        def run_tiles(eng, tile, first=None, last=None):
            if first:
                first()
            for n in range(PEELED):
                tile(n, n % 2, n // 2)
            with eng.Fori(0, (TILES - 1 - PEELED) // 2) as g:
                for u in range(2):
                    tile(g * 2 + (PEELED + u), 1 - u, g + (PEELED // 2 + u))
            tile(TILES - 1, 1, TILES // 2 - 1)
            if last:
                last()

        def unit(i):
            return i // NH2, i % NH2

        block = ctx.enter_context(nc.Block())

        @block.sync
        def _(sp):
            w_dram = ins["L0_ffn_W1"].rearrange("e (c p) d -> e p c d", p=P)
            for e in range(E):
                sp.dma_start(w_rows[:, e], w_dram[e]).then_inc(s["w_in"][e], 16)
            sp.dma_start(b1_rows[:], ins["L0_ffn_b1"].rearrange("e (c p) -> (e c) p", p=P)).then_inc(s["small_in"], 16)
            sp.dma_start(out_w_rows[:], ins["L0_ffn_Wo"]).then_inc(s["small_in"], 16)
            sp.dma_start(out_b[:], ins["L0_ffn_bo"].unsqueeze(0).broadcast_to([P, P])).then_inc(s["small_in"], 16)
            sp.dma_start(gb_all[:], mods_dram[:, GB, :].unsqueeze(0).broadcast_to([P, B, P])).then_inc(s["small_in"], 16)

            def load(n, p, b):
                after(sp, s["x_lo_ready"], n - 2)
                sp.dma_start(h3[p][:], h3_dram[n]).then_inc(s["h3_loaded"][p], 16)
                after(sp, s["weighed_ready"][-1], n - 2, TURN, TURN)
                sp.dma_start(comb[p][:].rearrange("p q e t -> p (q e) t"),
                             comb_dram[n].unsqueeze(0).broadcast_to([P, NQ * E, P])).then_inc(s["comb_loaded"][p], 16)
                after(sp, s["res_ready"], n - 2)
                sp.dma_start(x2[p][:], x2_dram[n]).then_inc(s["x2e_loaded"][p], 16)

            def store(n, p):
                after(sp, s["res_ready"], n)
                sp.dma_start(out_rows[n], res[p][:]).then_inc(s["stored"][p], 16)

            def tile(n, p, b):
                if not isinstance(n, int) or n < TILES - 1:
                    load(n + 1, 1 - p, b)
                if not isinstance(n, int) or n > 0:
                    store(n - 1, 1 - p)

            run_tiles(sp, tile, first=lambda: load(0, 0, 0), last=lambda: store(TILES - 1, 1))
            for p in range(2):
                sp.wait_ge(s["stored"][p], 16 * (TILES // 2))

        @block.tensor
        def _(pe):
            for e in range(E):
                pe.wait_ge(s["w_in"][e], 16)
                if e >= 2:
                    pe.wait_ge(s["w_lo_ready"], e - 1)
                for c in range(CH):
                    mm = pe.transpose(ps_a[e % 2][:, c * P:(c + 1) * P], w_rows[:, e, c, :], ident[:])
                mm.then_inc(s["w_ps"], 1)
            pe.wait_ge(s["small_in"], 64)
            pe.transpose(ps_b[0][:, 0:E * CH], b1_rows[:], ident[0:E * CH, 0:E * CH])
            for h in range(NH2):
                mm = pe.transpose(ps_b[0][:, (h + 1) * P:(h + 2) * P], out_w_rows[:, h * P:(h + 1) * P], ident[:])
            mm.then_inc(s["small_ps"], 1)
            pe.wait_ge(s["w_lo_ready"], E)
            pe.wait_ge(s["small_ready"], 2)

            def project(n, p):
                after(pe, s["total_ready"], n)
                after(pe, s["moe_ready"], n - 1)
                for q in range(NQ):
                    for h in range(NH2):
                        mm = pe.matmul(ps_w[:, q * P:(q + 1) * P], total[p][h][:, q * P:(q + 1) * P], out_w[:, h, :],
                                       start=(h == 0), stop=(h == NH2 - 1))
                mm.then_inc(s["out_ps"], 1)

            def product(dst, e, c, p):
                cs = slice(c * P, (c + 1) * P)
                pe.matmul(dst[:], w_hi[:, e, cs], x_hi[p][:], start=True, stop=False)
                pe.matmul(dst[:], w_hi[:, e, cs], x_lo[p][:], start=False, stop=False)
                return pe.matmul(dst[:], w_lo[:, e, cs], x_hi[p][:], start=False, stop=True)

            def tile(n, p, b):
                after(pe, s["x_hi_ready"], n)
                after(pe, s["x_lo_ready"], n)
                for i in range(UNITS):
                    e, h = unit(i)
                    after(pe, s["sig_ready"][(i - 2) % DEPTH], n, TURN, (i - 2) // DEPTH + 1)
                    product(ps_b[i % 2], e, NH2 + h, p).then_inc(s["b_ps"][i % 2], 1)
                    after(pe, s["glu_ready"][i % DEPTH], n, TURN, i // DEPTH)
                    product(ps_a[i % DEPTH], e, h, p).then_inc(s["a_ps"][i % DEPTH], 1)
                    if i == 5 and (not isinstance(n, int) or n > 0):
                        project(n - 1, 1 - p)

            run_tiles(pe, tile, last=lambda: project(TILES - 1, 1))

        @block.scalar
        def _(act):
            for e in range(E):
                act.wait_ge(s["w_ps"], e + 1)
                act.activation(w_hi[:, e, :], ps_a[e % 2][:], ACT.Copy).then_inc(s["w_hi_ready"], 1)
            act.wait_ge(s["small_ps"], 1)
            act.activation(b1_cols[:], ps_b[0][:, 0:E * CH], ACT.Copy).then_inc(s["small_ready"], 1)
            act.activation(out_w[:].rearrange("p h d -> p (h d)"), ps_b[0][:, P:(NH2 + 1) * P], ACT.Copy) \
                .then_inc(s["small_ready"], 1)
            act.wait_ge(s["small_ready"], 2)

            def split(n, p, b):
                after(act, s["h3_loaded"][p], b, 16, 16)
                after(act, s["a_ps"][-1], n - 2, TURN, TURN)
                act.activation(x_hi[p][:], h3[p][:], ACT.Copy).then_inc(s["x_hi_ready"], 1)

            def tile(n, p, b):
                for i in range(UNITS):
                    e, h = unit(i)
                    bias = e * CH + NH2 + h
                    after(act, s["b_ps"][i % 2], n, HALF, i // 2 + 1)
                    after(act, s["weighed_ready"][i % DEPTH], n, TURN, i // DEPTH)
                    act.activation(sig[i % DEPTH][:], ps_b[i % 2][:], ACT.Sigmoid, bias=b1_cols[:, bias:bias + 1]) \
                        .then_inc(s["sig_ready"][i % DEPTH], 1)
                    if i == UNITS // 2 and (not isinstance(n, int) or n < TILES - 1):
                        split(n + 1, 1 - p, b + p)

            run_tiles(act, tile, first=lambda: split(0, 0, 0))

        @block.gpsimd
        def _(pool):
            def finish(n, p, b):
                after(pool, s["moe_ready"], n)
                after(pool, s["stored"][p], b - 1, 16, 16)
                apart(pool, s["pool_passed"])
                pool.tensor_tensor(res[p][:], moe[:], gb_all[:, b, :].unsqueeze(1).broadcast_to([P, NQ, P]), ALU.mult) \
                    .then_inc(s["moe_gated"], 1)
                after(pool, s["moe_gated"], n)
                after(pool, s["x2e_loaded"][p], b, 16, 16)
                pool.tensor_tensor(res[p][:], res[p][:], x2[p][:], ALU.add).then_inc(s["res_ready"], 1)

            def tile(n, p, b):
                after(pool, s["comb_loaded"][p], b, 16, 16)
                for i in range(UNITS):
                    e, h = unit(i)
                    after(pool, s["sig_ready"][i % DEPTH], n, TURN, i // DEPTH + 1)
                    after(pool, s["glu_ready"][i % DEPTH], n, TURN, i // DEPTH)
                    pool.tensor_tensor(weighed[i % DEPTH][:].rearrange("p (q t) -> p q t", q=NQ),
                                       sig[i % DEPTH][:].rearrange("p (q t) -> p q t", q=NQ),
                                       comb[p][:, :, e, :], ALU.mult).then_inc(s["weighed_ready"][i % DEPTH], 1)
                    if i == 11 and (not isinstance(n, int) or n > 0):
                        finish(n - 1, 1 - p, b - 1 + p)

            pool.wait_ge(s["small_in"], 64)
            run_tiles(pool, tile, last=lambda: finish(TILES - 1, 1, TILES // 2 - 1))

        @block.vector
        def _(dve):
            for e in range(E):
                dve.wait_ge(s["w_hi_ready"], e + 1)
                dve.tensor_tensor(w_lo[:, e, :], ps_a[e % 2][:], w_hi[:, e, :].bitcast(F32), ALU.subtract) \
                    .then_inc(s["w_lo_ready"], 1)
            dve.wait_ge(s["small_in"], 64)
            dve.wait_ge(s["small_ready"], 2)

            def split(n, p, b):
                after(dve, s["x_hi_ready"], n)
                after(dve, s["a_ps"][-1], n - 2, TURN, TURN)
                dve.tensor_tensor(x_lo[p][:], h3[p][:], x_hi[p][:].bitcast(F32), ALU.subtract).then_inc(s["x_lo_ready"], 1)

            def bias_out(n, p, b):
                after(dve, s["out_ps"], n)
                after(dve, s["moe_gated"], n - 1)
                for q in range(NQ):
                    at = n * NQ + q
                    ins_ = dve.scalar_tensor_tensor(out=moe[:, q, :], in0=out_b[:], scalar=csum_all[:, at:at + 1] if isinstance(at, int) else csum_all[:, bass.ds(at, 1)],
                                                    in1=ps_w[:, q * P:(q + 1) * P], op0=ALU.mult, op1=ALU.add)
                ins_.then_inc(s["moe_ready"], 1)

            def tile(n, p, b):
                def add(i):
                    e, h = unit(i)
                    after(dve, s["glu_ready"][i % DEPTH], n, TURN, i // DEPTH + 1)
                    if i - NH2 < NH2:
                        after(dve, s["glu_ready"][i - NH2], n, TURN, 1)
                    else:
                        after(dve, s["added"][i % 2], n, HALF - 1 - i % 2, i // 2 - 1)
                    ins_ = dve.tensor_tensor(total[p][h][:], total[p][h][:], glu[i % DEPTH][:], ALU.add)
                    ins_.then_inc(s["total_ready"] if i == UNITS - 1 else s["added"][i % 2], 1)

                for i in range(UNITS):
                    e, h = unit(i)
                    bias = e * CH + h
                    after(dve, s["a_ps"][i % DEPTH], n, TURN, i // DEPTH + 1)
                    after(dve, s["weighed_ready"][i % DEPTH], n, TURN, i // DEPTH + 1)
                    if e == 0:
                        after(dve, s["out_ps"], n - 2)
                    elif i == NH2:
                        after(dve, s["total_ready"], n - 1)
                    dve.scalar_tensor_tensor(out=(total[p][h] if e == 0 else glu[i % DEPTH])[:], in0=ps_a[i % DEPTH][:],
                                             scalar=b1_cols[:, bias:bias + 1], in1=weighed[i % DEPTH][:],
                                             op0=ALU.add, op1=ALU.mult).then_inc(s["glu_ready"][i % DEPTH], 1)
                    if i - 1 >= NH2:
                        add(i - 1)
                    if i == 8 and (not isinstance(n, int) or n > 0):
                        bias_out(n - 1, 1 - p, b)
                    if i == UNITS // 2 + 1 and (not isinstance(n, int) or n < TILES - 1):
                        split(n + 1, 1 - p, b + p)
                add(UNITS - 1)

            run_tiles(dve, tile, first=lambda: split(0, 0, 0), last=lambda: bias_out(TILES - 1, 1, 0))


_INS = ["L0_attn_x", "L0_attn_ln1_w", "L0_attn_mu_r", "L0_attn_mu_k", "L0_attn_mu_v", "L0_attn_mu_w", "L0_attn_mu_g",
        "L0_attn_Wr", "L0_attn_Wk", "L0_attn_Wv", "L0_attn_Wg", "L0_attn_Wo", "L0_attn_w0", "L0_attn_wA", "L0_attn_wB",
        "L0_attn_u", "L0_attn_gn_w", "L0_attn_gn_b", "L0_attn_ln2_w", "L0_attn_ffn_w1", "L0_attn_ffn_w2",
        "L0_ffn_Wg", "L0_ffn_W1", "L0_ffn_b1", "L0_ffn_Wo", "L0_ffn_bo", "L0_c", "L0_wmod"]


def kernel(**inputs):
    import concourse.bacc as bacc
    from concourse.bass_utils import run_bass_kernel_spmd

    nc = bacc.Bacc("TRN2", target_bir_lowering=False, num_devices=1)
    arrays, args = {}, {}
    for name in _INS:
        a = np.ascontiguousarray(inputs[name])
        arrays[f"in_{name}"] = a
        args[name] = nc.dram_tensor(f"in_{name}", a.shape, mybir.dt.from_np(a.dtype), kind="ExternalInput").ap()
    shape = inputs["L0_attn_x"].shape
    out = nc.dram_tensor("out_0", shape, F32, kind="ExternalOutput").ap()
    build(nc, args, out)
    r = run_bass_kernel_spmd(nc, [arrays], core_ids=[0])
    return r.results[0]["out_0"]
```

```python
from contextlib import ExitStack

import numpy as np

import concourse.bass as bass
from concourse import mybir

F32 = mybir.dt.float32
F32R = mybir.dt.float32r
ALU = mybir.AluOpType
ACT = mybir.ActivationFunctionType
AX_X = mybir.AxisListType.X

P = 128
EPS_LN = 1e-5
EPS_RMS = 1e-6
EPS_GN = 1e-5
EPS_TOPK = 1e-9
GATE_MIN = 0.25


class Signals:

    def __init__(self, nc, block, names, lists):
        self.by_name = {n: nc.alloc_semaphore(f"{block}_{n}") for n in names}
        for n, k in lists.items():
            self.by_name[n] = [nc.alloc_semaphore(f"{block}_{n}{i}") for i in range(k)]

    def __getitem__(self, name):
        return self.by_name[name]

    def reset(self, nc):
        handles = [h for v in self.by_name.values() for h in (v if isinstance(v, list) else [v])]
        nc.clear_and_free_semaphores(handles)
        nc.all_engine_barrier()


def after(eng, sem, tile, step=1, k=1):
    value = tile * step + k
    if isinstance(value, int) and value <= 0:
        return
    eng.wait_ge(sem, value)


def apart(eng, passed):
    eng.sem_inc(passed, 1)


def build(nc, ins, out):
    x_in = ins["L0_attn_x"]
    B, T, D = x_in.shape
    H, DK = ins["L0_attn_u"].shape
    LORA = ins["L0_attn_wA"].shape[1]
    FF = ins["L0_attn_ffn_w1"].shape[1]
    E, H2, _ = ins["L0_ffn_W1"].shape
    HE = H2 // 2
    NT = 512
    NQ = NT // P
    TPB = T // NT
    TILES = B * TPB
    NF = FF // P
    NH2 = HE // P
    assert D == P and H * DK == P and DK == 8 and TPB == 2 and TILES % 2 == 0 and HE % P == 0 and LORA <= P

    x_rows = x_in.rearrange("b (n q p) d -> (b n) p q d", n=TPB, q=NQ)
    out_rows = out.rearrange("b (n q p) d -> (b n) p q d", n=TPB, q=NQ)
    mods_dram = nc.dram_tensor("mods_scratch", (B, 6, D), F32, kind="Internal").ap()
    x2_dram = nc.dram_tensor("x2_scratch", (TILES, P, NQ, D), F32, kind="Internal").ap()
    h3_dram = nc.dram_tensor("h3_scratch", (TILES, P, NT), F32, kind="Internal").ap()
    comb_dram = nc.dram_tensor("comb_scratch", (TILES, NQ * E, P), F32, kind="Internal").ap()

    with ExitStack() as keep:
        csum_all = keep.enter_context(nc.sbuf_tensor("csum_all", [P, TILES * NQ], F32))
        ident = keep.enter_context(nc.sbuf_tensor("ident", [P, P], F32))
        signals = attention_block(nc, ins, x_rows, mods_dram, x2_dram, h3_dram, comb_dram, csum_all, ident,
                        B, D, H, DK, LORA, NF, E, NT, NQ, TPB, TILES)
        signals.reset(nc)
        expert_block(nc, ins, out_rows, mods_dram, x2_dram, h3_dram, comb_dram, csum_all, ident,
                     B, D, E, HE, NH2, NT, NQ, TPB, TILES)


def attention_block(nc, ins, x_rows, mods_dram, x2_dram, h3_dram, comb_dram, csum_all, ident,
                    B, D, H, DK, LORA, NF, E, NT, NQ, TPB, TILES):
    LAST = TILES - 1
    ORDER = [0, 2, 4, 6, 1, 3, 5, 7]
    (ROW_LN1, ROW_MUR, ROW_MUK, ROW_MUV, ROW_MUW, ROW_MUG, ROW_W0, ROW_U, ROW_LN2, ROW_GNW, ROW_GNB) = range(11)
    NROWS = 11
    SA, A1, GA, SB, A2, GB = range(6)

    with ExitStack() as ctx:
        def sb(name, shape, dt=F32):
            return ctx.enter_context(nc.sbuf_tensor(name, shape, dt))

        def bank(name):
            return ctx.enter_context(nc.psum_tensor(name, [P, 512], F32))

        rows = sb("rows", [NROWS - 2, P])
        gn_rows, gn_turned = sb("gn_rows", [2, P]), sb("gn_turned", [2, P])
        cols = sb("cols", [P, NROWS])
        wk, wv, wr, wg = (sb(n, [P, P]) for n in ("wk", "wv", "wr", "wg"))
        wa, wb = sb("wa", [P, P]), sb("wb", [P, P])
        wo = sb("wo", [P, P])
        w1 = sb("w1", [P, NF * P])
        w2 = sb("w2", [P, NF, P])
        gate_w = sb("gate_w", [P, P])
        gate_rows = sb("gate_rows", [E, P])
        spread = sb("spread", [P, DK, P], F32R)
        head_of_key = sb("head_of_key", [P, H])
        head_of_val = sb("head_of_val", [P, H])
        reduce_w = sb("reduce_w", [P, 2, 2 * H])
        bonus_w = sb("bonus_w", [P, P])
        center_w = sb("center_w", [P, P])
        minus_half = sb("minus_half", [P, NQ])
        eps_gn = sb("eps_gn", [P, 1])
        c_rows = sb("c_rows", [B, P])
        c_act = sb("c_act", [B, P])
        c_cols = sb("c_cols", [P, B])
        mod_rows = sb("mod_rows", [B, 6, P])
        mods = sb("mods", [P, B, 5, P])
        expert_rank = sb("expert_rank", [P, E])
        xin = [sb(f"xin{i}", [P, NQ, P]) for i in range(2)]
        st1, mv1 = sb("st1", [P, NQ, 6]), sb("mv1", [P, NQ, 2])
        ve1, rs1 = sb("ve1", [P, NQ]), sb("rs1", [P, NQ])
        xn1 = sb("xn1", [P, NQ, P])
        mod_sign, mod_abs = xn1[0:B, 0:2, :], xn1[0:B, 2:4, :]
        h_all = sb("h_all", [P, TILES, NQ, P])
        staged = h_all[:, TILES - 2:].rearrange("p n q d -> p (n q) d")[:, 0:6]
        ssq1, ve2, rs2 = sb("ssq1", [P, NQ]), sb("ve2", [P, NQ]), sb("rs2", [P, NQ])
        hn = sb("hn", [P, NQ, P])
        hnT = [sb(f"hnT{i}", [P, 1 + NT]) for i in range(2)]
        xx = [sb(f"xx{i}", [P, NT]) for i in range(2)]
        mixA, mixB = sb("mixA", [P, NT]), sb("mixB", [P, NT])
        kT, rT, dT, vT = ([sb(f"{n}{i}", [P, NT]) for i in range(2)] for n in ("kT", "rT", "dT", "vT"))
        vhi, vlo = ([sb(f"{n}{i}", [P, NT], F32R) for i in range(2)] for n in ("vhi", "vlo"))
        lora = sb("lora", [P, NT])
        expw = sb("expw", [P, NT])
        mixG, ruk, tanh_g = sb("mixG", [P, NT]), sb("ruk", [P, NT]), sb("tanh_g", [P, NT])
        gate, bonus = ([sb(f"{n}{i}", [P, NT]) for i in range(2)] for n in ("gate", "bonus"))
        kv = [sb(f"kv{i}", [P, NT]) for i in range(2)]
        state = [sb(f"state{i}", [P, NT]) for i in range(4)]
        state_end = sb("state_end", [P, DK])
        rs_prod = [[sb(f"rs_prod{i}_{j}", [P, NT]) for j in range(4)] for i in range(2)]
        o_sum, o_sq = sb("o_sum", [P, NT]), sb("o_sq", [P, NT])
        var_g, sd_g, rs_g = (sb(n, [P, NQ, H]) for n in ("var_g", "sd_g", "rs_g"))
        o_norm, o_aff, o_gated = sb("o_norm", [P, NT]), sb("o_aff", [P, NT]), sb("o_gated", [P, NT])
        ssq3, ve3, rs3 = sb("ssq3", [P, NQ]), sb("ve3", [P, NQ]), sb("rs3", [P, NQ])
        h2, h2T = sb("h2", [P, NQ, P]), sb("h2T", [P, NT])
        gel = [sb(f"gel{c}", [P, NT]) for c in range(NF)]
        y = sb("y", [P, NQ, P])
        xre, x2 = ([sb(f"{n}{i}", [P, NQ, P]) for i in range(2)] for n in ("xre", "x2"))
        st4, mv4 = sb("st4", [P, NQ, 6]), sb("mv4", [P, NQ, 2])
        ve4, rs4 = sb("ve4", [P, NQ]), sb("rs4", [P, NQ])
        xn4, h3 = sb("xn4", [P, NQ, P]), sb("h3", [P, NQ, P])
        h3T = [sb(f"h3T{i}", [P, NT]) for i in range(2)]
        logits = sb("logits", [P, TILES, NQ, E])

        ps_f = [bank("ps_f0"), bank("ps_f1")]
        ps_v = [bank("ps_v0"), bank("ps_v1")]
        ps_o, ps_g, ps_k1, ps_k2 = bank("ps_o"), bank("ps_g"), bank("ps_k1"), bank("ps_k2")

        s = Signals(nc, "attention", (
            "act_passed dve_passed pool_passed vectors_in gn_turned weights_in more_in cond_in ident_zero ident_ready wpad_zero consts_ready "
            "cols_ps cols_ready weights_ready selectors_part selectors_ready gate_ps gate_ready silu_ready cT_ps cT_ready "
            "mod_ps mod_copied mod_step mod_ready mod_stored mods_in setup_step "
            "ln1_stats ln1_mv ln1_ve ln1_rstd xn1_ready h_scaled h_ready ssq1_ready rms1_ve rms1_rstd hn_ready "
            "hnT_ps hnT_ready xx_ready mixk_ready mixv_ready mixw_ready mixr_ready k_ps k_ready v_ps vhi_ready vT_ready "
            "vlo_ready lora_ps lora_ready w_ps expw_ready d_ready r_ps r_ready "
            "mixg_ready g_ps tanh_ready gate_set ruk_ready bonus_ps bonus_ready red_even red_odd "
            "o_ready cen_ps osq_ready var_ready sd_ready rsg_ready onorm_ready onT_ps oaff_ready ogated_ready wo_ps x1_ready "
            "ssq3_ready rms2_ve rms2_rstd h2_ready h2T_ps h2T_ready ffn2_ps y_ready y_gated x2_ready "
            "ln2_stats ln2_mv ln2_ve ln2_rstd xn4_ready h3_scaled h3_ready h3T_ps h3T_ready logits_ps logits_ready "
            "route_step exp_ready comb_ready combT_ps combT_ready comb_stored").split(),
            {"x_loaded": 2, "xre_loaded": 2, "x2_stored": 2, "h3_stored": 2, "spread_ps": 8, "kv_ready": 8,
             "scan_ready": 8, "rs_ready": 8, "ffn1_ps": NF, "gelu_ready": NF})

        LOOP_FROM = 10
        MAX_LAG = 10

        def run_pipeline(eng, step):
            def peeled(it):
                step(lambda lag: [(it - lag, (it - lag) % 2, (it - lag) // TPB)] if 0 <= it - lag <= LAST else [])

            for it in range(LOOP_FROM):
                peeled(it)
            with eng.Fori(LOOP_FROM // 2, TILES // 2) as g:
                for u in range(2):
                    step(lambda lag: [(g * 2 + (u - lag), (u - lag) % 2, g + (u - lag) // 2)])
            for it in range(TILES, TILES + MAX_LAG):
                peeled(it)

        def upto(tile):
            return min(tile, LAST) if isinstance(tile, int) else tile

        def quarters(ap):
            return ap.rearrange("p (q d) -> p q d", q=NQ)

        def mod_row(which, batch):
            return mods[:, batch, which, :].unsqueeze(1).broadcast_to([P, NQ, P])

        block = ctx.enter_context(nc.Block())

        @block.sync
        def _(sp):
            sp.dma_start(c_rows[:], ins["L0_c"]).then_inc(s["cond_in"], 16)
            sp.dma_start(staged[:, 0:6, :].rearrange("p a d -> p (a d)"), ins["L0_wmod"]).then_inc(s["cond_in"], 16)
            for row, name in ((ROW_LN1, "ln1_w"), (ROW_MUR, "mu_r"), (ROW_MUK, "mu_k"), (ROW_MUV, "mu_v"),
                              (ROW_MUW, "mu_w"), (ROW_MUG, "mu_g"), (ROW_W0, "w0"), (ROW_LN2, "ln2_w")):
                sp.dma_start(rows[row:row + 1, :], ins["L0_attn_" + name].rearrange("(a d) -> a d", a=1)) \
                    .then_inc(s["vectors_in"], 16)
            sp.dma_start(rows[ROW_U:ROW_U + 1, :].rearrange("a (h k) -> a h k", h=H),
                         ins["L0_attn_u"].rearrange("(a h) k -> a h k", a=1)).then_inc(s["vectors_in"], 16)
            for i, name in enumerate(("gn_w", "gn_b")):
                sp.dma_start(gn_rows[i:i + 1, :].rearrange("a (h j) -> a h j", h=H),
                             ins["L0_attn_" + name].rearrange("(a h) j -> a h j", a=1)).then_inc(s["vectors_in"], 16)
            for j in range(DK):
                sp.dma_start(wo[j * H:(j + 1) * H, :],
                             ins["L0_attn_Wo"].rearrange("(h j) d -> j h d", j=DK)[j]).then_inc(s["more_in"], 16)
            sp.dma_start(w2[:], ins["L0_attn_ffn_w2"].rearrange("(c p) d -> p c d", p=P)).then_inc(s["more_in"], 16)
            sp.dma_start(gate_rows[:], ins["L0_ffn_Wg"]).then_inc(s["more_in"], 16)
            sp.wait_ge(s["wpad_zero"], 3)
            sp.dma_start(wb[0:LORA, :], ins["L0_attn_wB"]).then_inc(s["more_in"], 16)
            sp.dma_start(wa[:, 0:LORA], ins["L0_attn_wA"]).then_inc(s["weights_in"], 16)
            sp.dma_start(w1[:], ins["L0_attn_ffn_w1"]).then_inc(s["weights_in"], 16)
            sp.wait_ge(s["mod_ps"], 2)
            for i, name in enumerate(("Wk", "Wv", "Wr", "Wg")):
                sp.dma_start(staged[:, i, :], ins["L0_attn_" + name]).then_inc(s["weights_in"], 16)
            sp.wait_ge(s["mod_ready"], 1)
            sp.dma_start(mods_dram, mod_rows[:]).then_inc(s["mod_stored"], 16)
            sp.wait_ge(s["mod_stored"], 16)
            sp.dma_start(mods[:], mods_dram[:, 0:5, :].unsqueeze(0).broadcast_to([P, B, 5, P])).then_inc(s["mods_in"], 16)

            def step(tile):
                for t, p, b in tile(0):
                    after(sp, s["xn1_ready"], t - 2)
                    sp.dma_start(xin[p][:], x_rows[t]).then_inc(s["x_loaded"][p], 16)
                for t, p, b in tile(7):
                    after(sp, s["x2_ready"], t - 2)
                    sp.dma_start(xre[p][:], x_rows[t]).then_inc(s["xre_loaded"][p], 16)
                for t, p, b in tile(10):
                    after(sp, s["h3T_ready"], t)
                    sp.dma_start(h3_dram[t], h3T[p][:]).then_inc(s["h3_stored"][p], 16)
                for t, p, b in tile(9):
                    after(sp, s["x2_ready"], t)
                    sp.dma_start(x2_dram[t], x2[p][:]).then_inc(s["x2_stored"][p], 16)

            run_pipeline(sp, step)
            sp.wait_ge(s["combT_ready"], TILES // 4)
            combT = kv[0][:].rearrange("p (g t) -> p g t", g=TILES // 4)
            for g in range(TILES // 4):
                sp.dma_start(comb_dram[4 * g:4 * g + 4].rearrange("n r t -> (n r) t"), combT[:, g, :]) \
                    .then_inc(s["comb_stored"], 16)
            sp.wait_ge(s["comb_stored"], 16 * (TILES // 4))
            for p in range(2):
                sp.wait_ge(s["x2_stored"][p], 16 * (TILES // 2))
                sp.wait_ge(s["h3_stored"][p], 16 * (TILES // 2))

        @block.gpsimd
        def _(pool):
            pool.memset(wa[:], 0.0).then_inc(s["wpad_zero"], 1)
            pool.memset(wb[:], 0.0).then_inc(s["wpad_zero"], 1)
            pool.memset(gate_w[:], 0.0).then_inc(s["wpad_zero"], 1)
            pool.memset(ident[:], 0.0).then_inc(s["ident_zero"], 1)
            pool.wait_ge(s["ident_zero"], 1)
            pool.affine_select(out=ident[:], in_=ident[:], compare_op=ALU.not_equal, fill=1.0, base=0,
                               pattern=[[-1, P]], channel_multiplier=1).then_inc(s["ident_ready"], 1)
            pool.memset(minus_half[:], -0.5).then_inc(s["consts_ready"], 1)
            pool.memset(eps_gn[:], EPS_GN).then_inc(s["consts_ready"], 1)
            pool.memset(reduce_w[:], 0.0).then_inc(s["consts_ready"], 1)
            pool.memset(hnT[0][:, 0:1], 0.0).then_inc(s["consts_ready"], 1)
            for j in range(4):
                pool.memset(rs_prod[0][j][:, 0:1], 0.0).then_inc(s["consts_ready"], 1)
            for e in range(E):
                pool.memset(expert_rank[:, e:e + 1], float(E - e)).then_inc(s["consts_ready"], 1)
            pool.wait_ge(s["consts_ready"], 16)
            pool.wait_ge(s["mods_in"], 16)

            def products(idx, p):
                j = ORDER[idx]
                dst, st = rs_prod[p][idx % 4], state[idx % 4]
                pool.tensor_tensor(dst[:, 1:NT], rT[p][:, 1:NT], st[:, 0:NT - 1], ALU.mult)
                if p == 0:
                    pool.tensor_copy(state_end[:, j:j + 1], st[:, NT - 1:NT]).then_inc(s["rs_ready"][idx], 1)
                else:
                    pool.tensor_tensor(dst[:, 0:1], rT[p][:, 0:1], state_end[:, j:j + 1], ALU.mult) \
                        .then_inc(s["rs_ready"][idx], 1)

            def step(tile):
                for t, p, b in tile(1):
                    after(pool, s["ln1_ve"], t)
                    pool.tensor_tensor(rs1[:], ve1[:], minus_half[:], ALU.pow).then_inc(s["ln1_rstd"], 1)
                for t, p, b in tile(5):
                    after(pool, s["scan_ready"][4], t)
                    after(pool, s["red_even"], t)
                    products(4, p)
                for t, p, b in tile(8):
                    after(pool, s["y_gated"], t)
                    after(pool, s["xre_loaded"][p], b, 16, 16)
                    pool.tensor_tensor(x2[p][:], x2[p][:], xre[p][:], ALU.add).then_inc(s["x2_ready"], 1)
                for t, p, b in tile(2):
                    apart(pool, s["pool_passed"])
                    pool.tensor_tensor(h_all[:, t], h_all[:, t], mod_row(SA, b), ALU.add).then_inc(s["h_ready"], 1)
                for t, p, b in tile(5):
                    after(pool, s["scan_ready"][5], t)
                    after(pool, s["red_even"], t)
                    products(5, p)
                    after(pool, s["scan_ready"][6], t)
                    after(pool, s["red_even"], t)
                    products(6, p)
                for t, p, b in tile(1):
                    after(pool, s["xn1_ready"], t)
                    apart(pool, s["pool_passed"])
                    pool.tensor_tensor(h_all[:, t], xn1[:], mod_row(A1, b), ALU.mult).then_inc(s["h_scaled"], 1)
                for t, p, b in tile(5):
                    after(pool, s["scan_ready"][7], t)
                    after(pool, s["red_even"], t)
                    products(7, p)
                for t, p, b in tile(8):
                    after(pool, s["ln2_mv"], t)
                    apart(pool, s["pool_passed"])
                    pool.tensor_scalar(ve4[:], mv4[:, :, 1], 1.0, EPS_LN, ALU.mult, ALU.add).then_inc(s["ln2_ve"], 1)
                    after(pool, s["ln2_ve"], t)
                    pool.tensor_tensor(rs4[:], ve4[:], minus_half[:], ALU.pow).then_inc(s["ln2_rstd"], 1)
                for t, p, b in tile(4):
                    after(pool, s["scan_ready"][0], t)
                    after(pool, s["r_ready"], t)
                    products(0, p)
                    after(pool, s["scan_ready"][1], t)
                    products(1, p)
                for t, p, b in tile(8):
                    after(pool, s["xn4_ready"], t)
                    after(pool, s["h3T_ps"], t - 1)
                    apart(pool, s["pool_passed"])
                    pool.tensor_tensor(h3[:], xn4[:], mod_row(A2, b), ALU.mult).then_inc(s["h3_scaled"], 1)
                for t, p, b in tile(2):
                    after(pool, s["ssq1_ready"], t)
                    apart(pool, s["pool_passed"])
                    pool.tensor_scalar(ve2[:], ssq1[:], 1.0 / D, EPS_RMS, ALU.mult, ALU.add).then_inc(s["rms1_ve"], 1)
                for t, p, b in tile(0):
                    after(pool, s["ln1_mv"], t)
                    apart(pool, s["pool_passed"])
                    pool.tensor_scalar(ve1[:], mv1[:, :, 1], 1.0, EPS_LN, ALU.mult, ALU.add).then_inc(s["ln1_ve"], 1)
                for t, p, b in tile(6):
                    after(pool, s["ssq3_ready"], t)
                    apart(pool, s["pool_passed"])
                    pool.tensor_scalar(ve3[:], ssq3[:], 1.0 / D, EPS_RMS, ALU.mult, ALU.add).then_inc(s["rms2_ve"], 1)
                for t, p, b in tile(2):
                    after(pool, s["rms1_ve"], t)
                    pool.tensor_tensor(rs2[:], ve2[:], minus_half[:], ALU.pow).then_inc(s["rms1_rstd"], 1)
                for t, p, b in tile(4):
                    after(pool, s["scan_ready"][2], t)
                    products(2, p)
                for t, p, b in tile(8):
                    after(pool, s["h3_scaled"], t)
                    apart(pool, s["pool_passed"])
                    pool.tensor_tensor(h3[:], h3[:], mod_row(SB, b), ALU.add).then_inc(s["h3_ready"], 1)
                for t, p, b in tile(4):
                    after(pool, s["scan_ready"][3], t)
                    products(3, p)
                for t, p, b in tile(6):
                    after(pool, s["rms2_ve"], t)
                    pool.tensor_tensor(rs3[:], ve3[:], minus_half[:], ALU.pow).then_inc(s["rms2_rstd"], 1)
                for t, p, b in tile(7):
                    after(pool, s["y_ready"], t)
                    after(pool, s["x2_stored"][p], b - 1, 16, 16)
                    apart(pool, s["pool_passed"])
                    pool.tensor_tensor(x2[p][:], y[:], mod_row(GA, b), ALU.mult).then_inc(s["y_gated"], 1)

            run_pipeline(pool, step)

        @block.scalar
        def _(act):
            act.wait_ge(s["cond_in"], 32)
            act.activation(c_act[:], c_rows[:], ACT.Silu).then_inc(s["silu_ready"], 1)
            act.wait_ge(s["cT_ps"], 1)
            act.activation(c_cols[:], ps_k1[:, 0:B], ACT.Copy).then_inc(s["cT_ready"], 1)
            for i in range(2):
                act.wait_ge(s["mod_ps"], i + 1)
                act.activation(mod_rows[:, 3 * i:3 * i + 3, :].rearrange("b a d -> b (a d)"), ps_f[i][0:B, 0:3 * P],
                               ACT.Copy).then_inc(s["mod_copied"], 1)
            act.wait_ge(s["cols_ps"], 1)
            act.activation(cols[:], ps_k2[:, 0:NROWS], ACT.Copy).then_inc(s["cols_ready"], 1)
            act.wait_ge(s["gate_ps"], 1)
            act.wait_ge(s["wpad_zero"], 3)
            act.activation(gate_w[:, 0:E], ps_o[:, 0:E], ACT.Copy).then_inc(s["gate_ready"], 1)
            act.wait_ge(s["consts_ready"], 16)
            act.wait_ge(s["setup_step"], 2)

            def sum_squares(src, room, dst, done):
                for q in range(NQ):
                    ins_ = act.activation(room[:, q, :], src[:, q, :], ACT.Square, accum_out=dst[:, q:q + 1])
                ins_.then_inc(done, 1)

            def scale_rows(dst, src, scale, done):
                for q in range(NQ):
                    ins_ = act.activation(dst[:, q, :], src[:, q, :], ACT.Copy, scale=scale[:, q:q + 1])
                ins_.then_inc(done, 1)

            def step(tile):
                for t, p, b in tile(7):
                    after(act, s["h2T_ps"], t)
                    act.activation(h2T[:], ps_k2[:], ACT.Copy).then_inc(s["h2T_ready"], 1)
                for t, p, b in tile(6):
                    after(act, s["onT_ps"], t)
                    act.activation(o_aff[:], ps_k1[:], ACT.Identity, scale=cols[:, ROW_GNW:ROW_GNW + 1],
                                   bias=cols[:, ROW_GNB:ROW_GNB + 1]).then_inc(s["oaff_ready"], 1)
                for t, p, b in tile(3):
                    after(act, s["rms1_rstd"], t)
                    apart(act, s["act_passed"])
                    scale_rows(hn, h_all[:, t], rs2, s["hn_ready"])
                for t, p, b in tile(4):
                    after(act, s["w_ps"], t)
                    act.activation(expw[:], ps_f[0][:], ACT.Exp, bias=cols[:, ROW_W0:ROW_W0 + 1]).then_inc(s["expw_ready"], 1)
                    after(act, s["expw_ready"], t)
                    act.activation(dT[p][:], expw[:], ACT.Exp, scale=-1.0).then_inc(s["d_ready"], 1)
                for t, p, b in tile(7):
                    after(act, s["ffn1_ps"][1], t)
                    act.activation(gel[1][:], ps_g[:], ACT.Gelu).then_inc(s["gelu_ready"][1], 1)
                for t, p, b in tile(3):
                    after(act, s["hnT_ps"], t)
                    if p == 1:
                        act.activation(hnT[1][:, 0:1], hnT[0][:, NT:NT + 1], ACT.Copy)
                    act.activation(hnT[p][:, 1:NT + 1], ps_f[0][:], ACT.Copy).then_inc(s["hnT_ready"], 1)
                for t, p, b in tile(7):
                    after(act, s["ffn1_ps"][0], t)
                    act.activation(gel[0][:], ps_k2[:], ACT.Gelu).then_inc(s["gelu_ready"][0], 1)
                for t, p, b in tile(4):
                    after(act, s["r_ps"], t)
                    act.activation(rT[p][:], ps_f[1][:], ACT.Copy).then_inc(s["r_ready"], 1)
                for t, p, b in tile(7):
                    after(act, s["ffn1_ps"][3], t)
                    act.activation(gel[3][:], ps_g[:], ACT.Gelu).then_inc(s["gelu_ready"][3], 1)
                for t, p, b in tile(2):
                    after(act, s["h_ready"], t)
                    apart(act, s["act_passed"])
                    sum_squares(h_all[:, t], hn, ssq1, s["ssq1_ready"])
                for t, p, b in tile(7):
                    after(act, s["ffn1_ps"][2], t)
                    act.activation(gel[2][:], ps_k2[:], ACT.Gelu).then_inc(s["gelu_ready"][2], 1)
                for t, p, b in tile(6):
                    after(act, s["x1_ready"], t)
                    apart(act, s["act_passed"])
                    sum_squares(h_all[:, t], h2, ssq3, s["ssq3_ready"])
                for t, p, b in tile(3):
                    after(act, s["k_ps"], t)
                    act.activation(kT[p][:], ps_f[1][:], ACT.Copy).then_inc(s["k_ready"], 1)
                for t, p, b in tile(5):
                    after(act, s["cen_ps"], t)
                    act.activation(o_sq[:], ps_k1[:], ACT.Square).then_inc(s["osq_ready"], 1)
                for t, p, b in tile(3):
                    after(act, s["v_ps"], t)
                    act.activation(vhi[p][:], ps_f[0][:], ACT.Copy).then_inc(s["vhi_ready"], 1)
                    after(act, s["v_ps"], t)
                    after(act, s["vhi_ready"], t)
                    act.activation(vT[p][:], ps_f[0][:], ACT.Copy).then_inc(s["vT_ready"], 1)
                for t, p, b in tile(4):
                    after(act, s["g_ps"], t)
                    act.activation(tanh_g[:], ps_g[:], ACT.Tanh, scale=0.5).then_inc(s["tanh_ready"], 1)
                for t, p, b in tile(5):
                    after(act, s["var_ready"], t)
                    act.activation(sd_g[:], var_g[:], ACT.Sqrt, scale=1.0 / DK, bias=eps_gn[:]).then_inc(s["sd_ready"], 1)
                for t, p, b in tile(3):
                    after(act, s["lora_ps"], t)
                    act.activation(lora[:], ps_f[1][:], ACT.Tanh).then_inc(s["lora_ready"], 1)
                for t, p, b in tile(8):
                    after(act, s["h3T_ps"], t)
                    after(act, s["h3_stored"][p], b - 1, 16, 16)
                    act.activation(h3T[p][:], ps_k2[:], ACT.Copy).then_inc(s["h3T_ready"], 1)
                for t, p, b in tile(6):
                    after(act, s["rms2_rstd"], t)
                    apart(act, s["act_passed"])
                    scale_rows(h2, h_all[:, t], rs3, s["h2_ready"])
                for t, p, b in tile(8):
                    after(act, s["logits_ps"], t)
                    apart(act, s["act_passed"])
                    act.activation(logits[:, t], quarters(ps_k2[:])[:, :, 0:E], ACT.Copy).then_inc(s["logits_ready"], 1)

            run_pipeline(act, step)
            act.wait_ge(s["route_step"], 2)
            lg = logits[:].rearrange("p n q e -> p (n q e)")
            act.activation(lg, lg, ACT.Exp).then_inc(s["exp_ready"], 1)
            combT = kv[0][:].rearrange("p (g t) -> p g t", g=TILES // 4)
            for g in range(TILES // 4):
                act.wait_ge(s["combT_ps"], g + 1)
                act.activation(combT[:, g, :], (ps_k1, ps_k2)[g % 2][:, 0:P], ACT.Copy).then_inc(s["combT_ready"], 1)

        @block.tensor
        def _(pe):
            pe.wait_ge(s["ident_ready"], 1)
            pe.wait_ge(s["silu_ready"], 1)
            pe.transpose(ps_k1[:, 0:B], c_act[:], ident[0:B, 0:B]).then_inc(s["cT_ps"], 1)
            pe.wait_ge(s["cT_ready"], 1)
            for i in range(2):
                pe.matmul(ps_f[i][0:B, 0:3 * P], c_cols[:], staged[:, 3 * i:3 * i + 3, :].rearrange("p a d -> p (a d)"),
                          start=True, stop=True).then_inc(s["mod_ps"], 1)
            pe.wait_ge(s["vectors_in"], 16 * NROWS)
            pe.transpose(ps_k2[:, 0:ROW_GNW], rows[:], ident[0:ROW_GNW, 0:ROW_GNW])
            pe.wait_ge(s["gn_turned"], 1)
            pe.transpose(ps_k2[:, ROW_GNW:NROWS], gn_turned[:], ident[0:2, 0:2]).then_inc(s["cols_ps"], 1)
            pe.wait_ge(s["more_in"], 16 * (DK + 3))
            pe.transpose(ps_o[:, 0:E], gate_rows[:], ident[0:E, 0:E]).then_inc(s["gate_ps"], 1)
            pe.wait_ge(s["mod_copied"], 2)
            pe.wait_ge(s["cols_ready"], 1)
            pe.wait_ge(s["gate_ready"], 1)
            pe.wait_ge(s["setup_step"], 2)

            def turn(dst, src, done):
                for q in range(NQ):
                    mm = pe.transpose(dst[:, q * P:(q + 1) * P], src[:, q, :], ident[:])
                mm.then_inc(done, 1)

            def spread_v(idx, p):
                j = ORDER[idx]
                pe.matmul(ps_v[idx % 2][:], spread[:, j, :], vhi[p][:], start=True, stop=False)
                pe.matmul(ps_v[idx % 2][:], spread[:, j, :], vlo[p][:], start=False, stop=True) \
                    .then_inc(s["spread_ps"][idx], 1)

            def reduce_heads(p, half, done):
                for quad in range(4):
                    mm = pe.matmul(ps_o[32 * quad:32 * quad + 32, :], reduce_w[:, half, :], rs_prod[p][quad][:],
                                   start=(half == 0), stop=(half == 1))
                mm.then_inc(done, 1)

            def ffn1(c):
                dst = ps_k2 if c % 2 == 0 else ps_g
                pe.matmul(dst[:], w1[:, c * P:(c + 1) * P], h2T[:], start=True, stop=True).then_inc(s["ffn1_ps"][c], 1)

            def project(dst, w, src, done):
                pe.matmul(dst[:], w[:], src[:], start=True, stop=True).then_inc(done, 1)

            def step(tile):
                for t, p, b in tile(7):
                    after(pe, s["gelu_ready"][2], t)
                    after(pe, s["gelu_ready"][3], t)
                    for q in range(NQ):
                        for c in range(NF):
                            mm = pe.matmul(ps_k2[:, q * P:(q + 1) * P], gel[c][:, q * P:(q + 1) * P], w2[:, c, :],
                                           start=(c == 0), stop=(c == NF - 1))
                    mm.then_inc(s["ffn2_ps"], 1)
                for t, p, b in tile(4):
                    after(pe, s["kv_ready"][3], t)
                    spread_v(5, p)
                for t, p, b in tile(3):
                    after(pe, s["mixw_ready"], t)
                    after(pe, s["k_ready"], t)
                    project(ps_f[1], wa, mixA, s["lora_ps"])
                for t, p, b in tile(4):
                    after(pe, s["kv_ready"][4], t)
                    spread_v(6, p)
                    after(pe, s["rs_ready"][3], t)
                    reduce_heads(p, 0, s["red_even"])
                for t, p, b in tile(8):
                    after(pe, s["h3_ready"], t)
                    after(pe, s["y_ready"], upto(t + 1))
                    after(pe, s["logits_ready"], t - 1)
                    turn(ps_k2, h3, s["h3T_ps"])
                for t, p, b in tile(4):
                    after(pe, s["ruk_ready"], t)
                    after(pe, s["gate_set"], t)
                    project(ps_g, bonus_w, ruk, s["bonus_ps"])
                for t, p, b in tile(8):
                    after(pe, s["h3T_ready"], t)
                    for q in range(NQ):
                        mm = pe.matmul(ps_k2[:, q * P:(q + 1) * P], h3T[p][:, q * P:(q + 1) * P], gate_w[:], start=True, stop=True)
                    mm.then_inc(s["logits_ps"], 1)
                for t, p, b in tile(4):
                    after(pe, s["kv_ready"][5], t)
                    spread_v(7, p)
                for t, p, b in tile(6):
                    after(pe, s["h2_ready"], t)
                    after(pe, s["logits_ready"], t - 2)
                    turn(ps_k2, h2, s["h2T_ps"])
                for t, p, b in tile(3):
                    after(pe, s["vhi_ready"], t)
                    after(pe, s["vlo_ready"], t)
                    after(pe, s["kv_ready"][6], t - 1)
                    spread_v(0, p)
                for t, p, b in tile(5):
                    after(pe, s["onorm_ready"], t)
                    turn(ps_k1, quarters(o_norm[:]), s["onT_ps"])
                for t, p, b in tile(3):
                    after(pe, s["lora_ready"], t)
                    after(pe, s["vT_ready"], t)
                    after(pe, s["vlo_ready"], t)
                    project(ps_f[0], wb, lora, s["w_ps"])
                for t, p, b in tile(6):
                    after(pe, s["h2T_ready"], t)
                    after(pe, s["bonus_ready"], upto(t + 2))
                    ffn1(1)
                for t, p, b in tile(3):
                    after(pe, s["kv_ready"][7], t - 1)
                    spread_v(1, p)
                    after(pe, s["mixr_ready"], t)
                    after(pe, s["lora_ready"], t)
                    project(ps_f[1], wr, mixB, s["r_ps"])
                for t, p, b in tile(6):
                    after(pe, s["h2T_ready"], t)
                    ffn1(0)
                for t, p, b in tile(2):
                    after(pe, s["hn_ready"], t)
                    after(pe, s["expw_ready"], t - 1)
                    turn(ps_f[0], hn, s["hnT_ps"])
                for t, p, b in tile(5):
                    after(pe, s["ogated_ready"], t)
                    after(pe, s["oaff_ready"], t)
                    for q in range(NQ):
                        mm = pe.matmul(ps_k1[:, q * P:(q + 1) * P], o_gated[:, q * P:(q + 1) * P], wo[:], start=True, stop=True)
                    mm.then_inc(s["wo_ps"], 1)
                for t, p, b in tile(6):
                    after(pe, s["gelu_ready"][1], t)
                    ffn1(3)
                for t, p, b in tile(3):
                    after(pe, s["kv_ready"][0], t)
                    spread_v(2, p)
                for t, p, b in tile(4):
                    after(pe, s["rs_ready"][7], t)
                    reduce_heads(p, 1, s["red_odd"])
                for t, p, b in tile(6):
                    after(pe, s["gelu_ready"][0], t)
                    ffn1(2)
                for t, p, b in tile(3):
                    after(pe, s["mixg_ready"], t)
                    after(pe, s["gelu_ready"][3], t - 3)
                    project(ps_g, wg, mixG, s["g_ps"])
                for t, p, b in tile(4):
                    after(pe, s["o_ready"], t)
                    for q in range(NQ):
                        mm = pe.matmul(ps_k1[:, q * P:(q + 1) * P], o_sum[:, q * P:(q + 1) * P], center_w[:], start=True, stop=True)
                    mm.then_inc(s["cen_ps"], 1)
                for t, p, b in tile(3):
                    after(pe, s["kv_ready"][1], t)
                    spread_v(3, p)
                    after(pe, s["kv_ready"][2], t)
                    spread_v(4, p)
                for t, p, b in tile(2):
                    after(pe, s["mixk_ready"], t)
                    after(pe, s["r_ready"], t - 1)
                    project(ps_f[1], wk, mixA, s["k_ps"])
                    after(pe, s["mixv_ready"], t)
                    after(pe, s["hnT_ready"], t)
                    project(ps_f[0], wv, mixB, s["v_ps"])

            run_pipeline(pe, step)
            pe.wait_ge(s["comb_ready"], 1)
            comb_cols = mixA[:]
            for g in range(TILES // 4):
                if g >= 2:
                    pe.wait_ge(s["combT_ready"], g - 1)
                pe.transpose((ps_k1, ps_k2)[g % 2][:, 0:P], comb_cols[:, g * P:(g + 1) * P], ident[:]).then_inc(s["combT_ps"], 1)

        @block.vector
        def _(dve):
            dve.wait_ge(s["ident_ready"], 1)
            dve.wait_ge(s["consts_ready"], 16)
            dve.tensor_reduce(head_of_key[:], ident[:].rearrange("p (h k) -> p h k", h=H), AX_X, ALU.add) \
                .then_inc(s["selectors_part"], 1)
            dve.tensor_reduce(head_of_val[:], ident[:].rearrange("p (j h) -> p h j", h=H), AX_X, ALU.add) \
                .then_inc(s["selectors_part"], 1)
            dve.wait_ge(s["selectors_part"], 2)
            for half in range(2):
                dve.tensor_copy(reduce_w[:, half, half * H:(half + 1) * H], head_of_key[:])
            dve.tensor_copy(bonus_w[:].rearrange("p (j h) -> p j h", h=H), head_of_key[:].unsqueeze(1).broadcast_to([P, DK, H]))
            dve.scalar_tensor_tensor(out=center_w[:].rearrange("p (j h) -> p j h", h=H),
                                     in0=head_of_val[:].unsqueeze(1).broadcast_to([P, DK, H]), scalar=-1.0 / DK,
                                     in1=ident[:].rearrange("p (j h) -> p j h", h=H), op0=ALU.mult, op1=ALU.add)
            for j in range(DK):
                last = dve.tensor_copy(spread[:, j, :].rearrange("p (h k) -> p h k", h=H),
                                       ident[:, j * H:(j + 1) * H].unsqueeze(2).broadcast_to([P, H, DK]))
            last.then_inc(s["setup_step"], 1)
            dve.wait_ge(s["vectors_in"], 16 * NROWS)
            dve.tensor_copy(gn_turned[:].rearrange("a (j h) -> a j h", h=H),
                            gn_rows[:].rearrange("a (h j) -> a j h", h=H)).then_inc(s["gn_turned"], 1)
            dve.wait_ge(s["mod_copied"], 2)
            pair_of = mod_rows[:].rearrange("b (g a) d -> b g a d", g=2)
            dve.tensor_scalar(mod_sign, pair_of[:, :, 2, :], 0.0, 2.0, ALU.is_ge, ALU.mult).then_inc(s["mod_step"], 1)
            dve.tensor_scalar(mod_abs, pair_of[:, :, 2, :], -1.0, None, ALU.mult).then_inc(s["mod_step"], 1)
            dve.wait_ge(s["mod_step"], 2)
            dve.tensor_tensor(mod_abs, mod_abs, pair_of[:, :, 2, :], ALU.max).then_inc(s["mod_step"], 1)
            dve.wait_ge(s["mod_step"], 3)
            dve.tensor_scalar(mod_abs, mod_abs, GATE_MIN, None, ALU.max).then_inc(s["mod_step"], 1)
            dve.wait_ge(s["mod_step"], 4)
            dve.scalar_tensor_tensor(out=pair_of[:, :, 2, :], in0=mod_sign, scalar=-1.0, in1=mod_abs,
                                     op0=ALU.add, op1=ALU.mult)
            dve.tensor_scalar(pair_of[:, :, 1, :], pair_of[:, :, 1, :], 1.0, None, ALU.add).then_inc(s["mod_ready"], 1)
            dve.wait_ge(s["cols_ready"], 1)
            dve.wait_ge(s["weights_in"], 16 * 6)
            ln1, ln2 = cols[:, ROW_LN1:ROW_LN1 + 1], cols[:, ROW_LN2:ROW_LN2 + 1]
            for i, w in ((0, wk), (2, wr)):
                dve.tensor_scalar(w[:], staged[:, i, :], ln1, None, ALU.mult)
            for i, w in ((1, wv), (3, wg)):
                dve.tensor_scalar(w[:].rearrange("p (j h) -> p j h", h=H),
                                  staged[:, i, :].rearrange("p (h j) -> p j h", h=H), ln1, None, ALU.mult)
            dve.tensor_scalar(wa[:], wa[:], ln1, None, ALU.mult)
            dve.tensor_scalar(cols[:, ROW_GNW:ROW_GNB + 1], cols[:, ROW_GNW:ROW_GNB + 1], 0.5, None, ALU.mult)
            dve.tensor_scalar(w1[:], w1[:], ln2, None, ALU.mult).then_inc(s["setup_step"], 1)

            def token_stats(src, st, done):
                for q in range(NQ):
                    ins_ = dve.bn_stats(st[:, q, :], src[:, q, :])
                ins_.then_inc(done, 1)

            def token_moments(mv, st, done):
                for q in range(NQ):
                    ins_ = dve.bn_aggr(mv[:, q, :], st[:, q, :])
                ins_.then_inc(done, 1)

            def normalize(dst, src, mv, rs, done):
                for q in range(NQ):
                    ins_ = dve.tensor_scalar(dst[:, q, :], src[:, q, :], mv[:, q, 0:1], rs[:, q:q + 1],
                                             ALU.subtract, ALU.mult)
                ins_.then_inc(done, 1)

            def mix(dst, p, row, done):
                dve.scalar_tensor_tensor(out=dst[:], in0=xx[p][:], scalar=cols[:, row:row + 1],
                                         in1=hnT[p][:, 1:NT + 1], op0=ALU.mult, op1=ALU.add).then_inc(done, 1)

            def outer(idx, p):
                dve.tensor_tensor(kv[idx % 2][:], ps_v[idx % 2][:], kT[p][:], ALU.mult).then_inc(s["kv_ready"][idx], 1)

            def scan(idx, p):
                first = 0.0 if p == 0 else state_end[:, ORDER[idx]:ORDER[idx] + 1]
                dve.tensor_tensor_scan(state[idx % 4][:], dT[p][:], kv[idx % 2][:], first, ALU.mult, ALU.add) \
                    .then_inc(s["scan_ready"][idx], 1)

            def step(tile):
                for t, p, b in tile(4):
                    after(dve, s["hnT_ready"], t)
                    mix(mixG, p, ROW_MUG, s["mixg_ready"])
                for t, p, b in tile(5):
                    after(dve, s["tanh_ready"], t)
                    dve.scalar_tensor_tensor(out=gate[p][:], in0=tanh_g[:], scalar=1.0, in1=ps_g[:],
                                             op0=ALU.add, op1=ALU.mult).then_inc(s["gate_set"], 1)
                for t, p, b in tile(8):
                    after(dve, s["ffn2_ps"], t)
                    dve.tensor_tensor(y[:], quarters(ps_k2[:]), h_all[:, t], ALU.add).then_inc(s["y_ready"], 1)
                for t, p, b in tile(5):
                    after(dve, s["kv_ready"][4], t)
                    after(dve, s["rs_ready"][0], t)
                    scan(4, p)
                for t, p, b in tile(4):
                    after(dve, s["vhi_ready"], t)
                    after(dve, s["vT_ready"], t)
                    dve.tensor_tensor(vlo[p][:], ps_f[0][:], vhi[p][:].bitcast(F32), ALU.subtract).then_inc(s["vlo_ready"], 1)
                for t, p, b in tile(6):
                    after(dve, s["sd_ready"], t)
                    dve.reciprocal(rs_g[:], sd_g[:]).then_inc(s["rsg_ready"], 1)
                for t, p, b in tile(5):
                    after(dve, s["spread_ps"][5], t)
                    after(dve, s["scan_ready"][3], t)
                    outer(5, p)
                    after(dve, s["spread_ps"][6], t)
                    after(dve, s["scan_ready"][4], t)
                    outer(6, p)
                for t, p, b in tile(6):
                    after(dve, s["rsg_ready"], t)
                    dve.tensor_tensor(o_norm[:].rearrange("p (q j h) -> p q j h", q=NQ, h=H),
                                      ps_k1[:].rearrange("p (q j h) -> p q j h", q=NQ, h=H),
                                      rs_g[:].unsqueeze(2).broadcast_to([P, NQ, DK, H]), ALU.mult).then_inc(s["onorm_ready"], 1)
                for t, p, b in tile(5):
                    after(dve, s["kv_ready"][5], t)
                    after(dve, s["rs_ready"][1], t)
                    scan(5, p)
                    after(dve, s["bonus_ps"], t)
                    after(dve, s["vT_ready"], t)
                    dve.tensor_tensor(bonus[p][:], ps_g[:], vT[p][:], ALU.mult).then_inc(s["bonus_ready"], 1)
                    after(dve, s["kv_ready"][6], t)
                    after(dve, s["rs_ready"][2], t)
                    scan(6, p)
                    after(dve, s["spread_ps"][7], t)
                    after(dve, s["scan_ready"][5], t)
                    outer(7, p)
                for t, p, b in tile(1):
                    after(dve, s["ln1_rstd"], t)
                    normalize(xn1, xin[p], mv1, rs1, s["xn1_ready"])
                for t, p, b in tile(4):
                    after(dve, s["v_ps"], t)
                    mix(mixB, p, ROW_MUR, s["mixr_ready"])
                for t, p, b in tile(5):
                    after(dve, s["kv_ready"][7], t)
                    after(dve, s["rs_ready"][3], t)
                    scan(7, p)
                for t, p, b in tile(6):
                    after(dve, s["oaff_ready"], t)
                    dve.tensor_tensor(o_gated[:], o_aff[:], gate[p][:], ALU.mult).then_inc(s["ogated_ready"], 1)
                for t, p, b in tile(0):
                    after(dve, s["x_loaded"][p], b, 16, 16)
                    token_stats(xin[p], st1, s["ln1_stats"])
                for t, p, b in tile(8):
                    after(dve, s["x2_ready"], t)
                    token_stats(x2[p], st4, s["ln2_stats"])
                for t, p, b in tile(4):
                    after(dve, s["spread_ps"][0], t)
                    after(dve, s["k_ready"], t)
                    outer(0, p)
                for t, p, b in tile(8):
                    after(dve, s["ln2_stats"], t)
                    apart(dve, s["dve_passed"])
                    token_moments(mv4, st4, s["ln2_mv"])
                for t, p, b in tile(4):
                    after(dve, s["spread_ps"][1], t)
                    after(dve, s["scan_ready"][7], t - 1)
                    outer(1, p)
                    after(dve, s["kv_ready"][0], t)
                    after(dve, s["d_ready"], t)
                    after(dve, s["rs_ready"][4], t - 1)
                    scan(0, p)
                    after(dve, s["kv_ready"][1], t)
                    after(dve, s["rs_ready"][5], t - 1)
                    scan(1, p)
                for t, p, b in tile(3):
                    after(dve, s["hnT_ready"], t)
                    dve.tensor_tensor(xx[p][:], hnT[p][:, 0:NT], hnT[p][:, 1:NT + 1], ALU.subtract).then_inc(s["xx_ready"], 1)
                for t, p, b in tile(6):
                    after(dve, s["wo_ps"], t)
                    dve.tensor_tensor(h_all[:, t], quarters(ps_k1[:]), h_all[:, t], ALU.add).then_inc(s["x1_ready"], 1)
                for t, p, b in tile(5):
                    after(dve, s["red_odd"], t)
                    dve.tensor_tensor(o_sum[:], ps_o[:], bonus[p][:], ALU.add).then_inc(s["o_ready"], 1)
                for t, p, b in tile(8):
                    after(dve, s["ln2_rstd"], t)
                    normalize(xn4, x2[p], mv4, rs4, s["xn4_ready"])
                for t, p, b in tile(4):
                    after(dve, s["spread_ps"][2], t)
                    after(dve, s["scan_ready"][0], t)
                    outer(2, p)
                for t, p, b in tile(3):
                    after(dve, s["xx_ready"], t)
                    mix(mixA, p, ROW_MUK, s["mixk_ready"])
                for t, p, b in tile(0):
                    after(dve, s["ln1_stats"], t)
                    apart(dve, s["dve_passed"])
                    token_moments(mv1, st1, s["ln1_mv"])
                for t, p, b in tile(3):
                    mix(mixB, p, ROW_MUV, s["mixv_ready"])
                for t, p, b in tile(4):
                    after(dve, s["kv_ready"][2], t)
                    scan(2, p)
                    after(dve, s["spread_ps"][3], t)
                    outer(3, p)
                    after(dve, s["spread_ps"][4], t)
                    after(dve, s["scan_ready"][2], t)
                    outer(4, p)
                for t, p, b in tile(3):
                    after(dve, s["k_ps"], t)
                    mix(mixA, p, ROW_MUW, s["mixw_ready"])
                for t, p, b in tile(4):
                    after(dve, s["kv_ready"][3], t)
                    scan(3, p)
                for t, p, b in tile(5):
                    after(dve, s["osq_ready"], t)
                    dve.tensor_reduce(var_g[:], o_sq[:].rearrange("p (q j h) -> p q h j", q=NQ, h=H), AX_X, ALU.add) \
                        .then_inc(s["var_ready"], 1)
                for t, p, b in tile(4):
                    after(dve, s["r_ready"], t)
                    dve.scalar_tensor_tensor(out=ruk[:], in0=rT[p][:], scalar=cols[:, ROW_U:ROW_U + 1], in1=kT[p][:],
                                             op0=ALU.mult, op1=ALU.mult).then_inc(s["ruk_ready"], 1)

            run_pipeline(dve, step)

            G = TILES * NQ
            lg = logits[:].rearrange("p n q e -> p (n q) e")
            hit = mixB[:].rearrange("p (g e) -> p g e", e=E)
            first = mixG[:].rearrange("p (g e) -> p g e", e=E)
            second = ruk[:].rearrange("p (g e) -> p g e", e=E)
            comb = mixA[:].rearrange("p (g e) -> p g e", e=E)
            top = kv[1][:].rearrange("p (a g) -> p a g", g=G)
            count = [0]

            def done(ins_):
                count[0] += 1
                ins_.then_inc(s["route_step"], 1)
                dve.wait_ge(s["route_step"], count[0])

            def wide(ap):
                return ap.unsqueeze(2).broadcast_to([P, G, E])

            rank = expert_rank[:].unsqueeze(1).broadcast_to([P, G, E])
            MAXL, Z, P1, R1, P2, R2, DEN = range(7)
            dve.wait_ge(s["logits_ready"], TILES)
            done(dve.tensor_reduce(top[:, MAXL, :], lg, AX_X, ALU.max))
            done(dve.tensor_tensor(lg, lg, wide(top[:, MAXL, :]), ALU.subtract))
            dve.wait_ge(s["exp_ready"], 1)
            done(dve.tensor_reduce(top[:, Z, :], lg, AX_X, ALU.add))
            done(dve.reciprocal(top[:, Z, :], top[:, Z, :]))
            done(dve.tensor_tensor(lg, lg, wide(top[:, Z, :]), ALU.mult))
            for value, place, mask in ((P1, R1, first), (P2, R2, second)):
                done(dve.tensor_reduce(top[:, value, :], lg, AX_X, ALU.max))
                done(dve.tensor_tensor(hit, lg, wide(top[:, value, :]), ALU.is_equal))
                done(dve.tensor_tensor(hit, hit, rank, ALU.mult))
                done(dve.tensor_reduce(top[:, place, :], hit, AX_X, ALU.max))
                done(dve.tensor_tensor(mask, rank, wide(top[:, place, :]), ALU.is_equal))
                if value == P1:
                    done(dve.scalar_tensor_tensor(out=lg, in0=mask, scalar=-2.0, in1=lg, op0=ALU.mult, op1=ALU.add))
            done(dve.scalar_tensor_tensor(out=top[:, DEN, :], in0=top[:, P1, :], scalar=EPS_TOPK, in1=top[:, P2, :],
                                          op0=ALU.add, op1=ALU.add))
            done(dve.reciprocal(top[:, DEN, :], top[:, DEN, :]))
            done(dve.tensor_tensor(top[:, P1, :], top[:, P1, :], top[:, DEN, :], ALU.mult))
            done(dve.tensor_tensor(top[:, P2, :], top[:, P2, :], top[:, DEN, :], ALU.mult))
            done(dve.tensor_tensor(csum_all[:], top[:, P1, :], top[:, P2, :], ALU.add))
            done(dve.tensor_tensor(first, first, wide(top[:, P1, :]), ALU.mult))
            done(dve.tensor_tensor(second, second, wide(top[:, P2, :]), ALU.mult))
            dve.tensor_tensor(comb, first, second, ALU.add).then_inc(s["comb_ready"], 1)

    return s


def expert_block(nc, ins, out_rows, mods_dram, x2_dram, h3_dram, comb_dram, csum_all, ident,
                 B, D, E, HE, NH2, NT, NQ, TPB, TILES):
    UNITS = E * NH2
    HALF = UNITS // 2
    DEPTH = 4
    TURN = UNITS // DEPTH
    CH = 2 * NH2
    GB = 5
    PEELED = 3
    with ExitStack() as ctx:
        def sb(name, shape, dt=F32):
            return ctx.enter_context(nc.sbuf_tensor(name, shape, dt))

        def bank(name):
            return ctx.enter_context(nc.psum_tensor(name, [P, 512], F32))

        w_rows = sb("w_rows", [P, E, CH, P])
        w_hi, w_lo = sb("w_hi", [P, E, CH * P], F32R), sb("w_lo", [P, E, CH * P], F32R)
        b1_rows, b1_cols = sb("b1_rows", [E * CH, P]), sb("b1_cols", [P, E * CH])
        out_w_rows, out_w = sb("out_w_rows", [P, HE]), sb("out_w", [P, NH2, P])
        out_b = sb("out_b", [P, P])
        gb_all = sb("gb_all", [P, B, P])
        h3 = [sb(f"h3_in{i}", [P, NT]) for i in range(2)]
        x_hi, x_lo = ([sb(f"{n}{i}", [P, NT], F32R) for i in range(2)] for n in ("x_hi", "x_lo"))
        comb = [sb(f"comb{i}", [P, NQ, E, P]) for i in range(2)]
        x2 = [sb(f"x2_in{i}", [P, NQ, P]) for i in range(2)]
        sig = [sb(f"sig{i}", [P, NT]) for i in range(DEPTH)]
        weighed = [sb(f"weighed{i}", [P, NT]) for i in range(DEPTH)]
        glu = [sb(f"glu{i}", [P, NT]) for i in range(DEPTH)]
        total = [[sb(f"total{i}_{h}", [P, NT]) for h in range(NH2)] for i in range(2)]
        moe = sb("moe", [P, NQ, P])
        res = [sb(f"res{i}", [P, NQ, P]) for i in range(2)]
        ps_a, ps_b = ([bank(f"{n}{i}") for i in range(k)] for n, k in (("ps_a", DEPTH), ("ps_b", 2)))
        ps_w = bank("ps_w")

        s = Signals(nc, "experts", (
            "pool_passed small_in w_ps w_hi_ready w_lo_ready small_ps small_ready "
            "x_hi_ready x_lo_ready out_ps moe_ready moe_gated res_ready total_ready").split(),
            {"w_in": E, "h3_loaded": 2, "comb_loaded": 2, "x2e_loaded": 2, "stored": 2,
             "b_ps": 2, "added": 2, "a_ps": DEPTH, "sig_ready": DEPTH, "weighed_ready": DEPTH, "glu_ready": DEPTH})

        def run_tiles(eng, tile, first=None, last=None):
            if first:
                first()
            for n in range(PEELED):
                tile(n, n % 2, n // 2)
            with eng.Fori(0, (TILES - 1 - PEELED) // 2) as g:
                for u in range(2):
                    tile(g * 2 + (PEELED + u), 1 - u, g + (PEELED // 2 + u))
            tile(TILES - 1, 1, TILES // 2 - 1)
            if last:
                last()

        def unit(i):
            return i // NH2, i % NH2

        block = ctx.enter_context(nc.Block())

        @block.sync
        def _(sp):
            w_dram = ins["L0_ffn_W1"].rearrange("e (c p) d -> e p c d", p=P)
            for e in range(E):
                sp.dma_start(w_rows[:, e], w_dram[e]).then_inc(s["w_in"][e], 16)
            sp.dma_start(b1_rows[:], ins["L0_ffn_b1"].rearrange("e (c p) -> (e c) p", p=P)).then_inc(s["small_in"], 16)
            sp.dma_start(out_w_rows[:], ins["L0_ffn_Wo"]).then_inc(s["small_in"], 16)
            sp.dma_start(out_b[:], ins["L0_ffn_bo"].unsqueeze(0).broadcast_to([P, P])).then_inc(s["small_in"], 16)
            sp.dma_start(gb_all[:], mods_dram[:, GB, :].unsqueeze(0).broadcast_to([P, B, P])).then_inc(s["small_in"], 16)

            def load(n, p, b):
                after(sp, s["x_lo_ready"], n - 2)
                sp.dma_start(h3[p][:], h3_dram[n]).then_inc(s["h3_loaded"][p], 16)
                after(sp, s["weighed_ready"][-1], n - 2, TURN, TURN)
                sp.dma_start(comb[p][:].rearrange("p q e t -> p (q e) t"),
                             comb_dram[n].unsqueeze(0).broadcast_to([P, NQ * E, P])).then_inc(s["comb_loaded"][p], 16)
                after(sp, s["res_ready"], n - 2)
                sp.dma_start(x2[p][:], x2_dram[n]).then_inc(s["x2e_loaded"][p], 16)

            def store(n, p):
                after(sp, s["res_ready"], n)
                sp.dma_start(out_rows[n], res[p][:]).then_inc(s["stored"][p], 16)

            def tile(n, p, b):
                if not isinstance(n, int) or n < TILES - 1:
                    load(n + 1, 1 - p, b)
                if not isinstance(n, int) or n > 0:
                    store(n - 1, 1 - p)

            run_tiles(sp, tile, first=lambda: load(0, 0, 0), last=lambda: store(TILES - 1, 1))
            for p in range(2):
                sp.wait_ge(s["stored"][p], 16 * (TILES // 2))

        @block.tensor
        def _(pe):
            for e in range(E):
                pe.wait_ge(s["w_in"][e], 16)
                if e >= 2:
                    pe.wait_ge(s["w_lo_ready"], e - 1)
                for c in range(CH):
                    mm = pe.transpose(ps_a[e % 2][:, c * P:(c + 1) * P], w_rows[:, e, c, :], ident[:])
                mm.then_inc(s["w_ps"], 1)
            pe.wait_ge(s["small_in"], 64)
            pe.transpose(ps_b[0][:, 0:E * CH], b1_rows[:], ident[0:E * CH, 0:E * CH])
            for h in range(NH2):
                mm = pe.transpose(ps_b[0][:, (h + 1) * P:(h + 2) * P], out_w_rows[:, h * P:(h + 1) * P], ident[:])
            mm.then_inc(s["small_ps"], 1)
            pe.wait_ge(s["w_lo_ready"], E)
            pe.wait_ge(s["small_ready"], 2)

            def project(n, p):
                after(pe, s["total_ready"], n)
                after(pe, s["moe_ready"], n - 1)
                for q in range(NQ):
                    for h in range(NH2):
                        mm = pe.matmul(ps_w[:, q * P:(q + 1) * P], total[p][h][:, q * P:(q + 1) * P], out_w[:, h, :],
                                       start=(h == 0), stop=(h == NH2 - 1))
                mm.then_inc(s["out_ps"], 1)

            def product(dst, e, c, p):
                cs = slice(c * P, (c + 1) * P)
                pe.matmul(dst[:], w_hi[:, e, cs], x_hi[p][:], start=True, stop=False)
                pe.matmul(dst[:], w_hi[:, e, cs], x_lo[p][:], start=False, stop=False)
                return pe.matmul(dst[:], w_lo[:, e, cs], x_hi[p][:], start=False, stop=True)

            def tile(n, p, b):
                after(pe, s["x_hi_ready"], n)
                after(pe, s["x_lo_ready"], n)
                for i in range(UNITS):
                    e, h = unit(i)
                    after(pe, s["sig_ready"][(i - 2) % DEPTH], n, TURN, (i - 2) // DEPTH + 1)
                    product(ps_b[i % 2], e, NH2 + h, p).then_inc(s["b_ps"][i % 2], 1)
                    after(pe, s["glu_ready"][i % DEPTH], n, TURN, i // DEPTH)
                    product(ps_a[i % DEPTH], e, h, p).then_inc(s["a_ps"][i % DEPTH], 1)
                    if i == 5 and (not isinstance(n, int) or n > 0):
                        project(n - 1, 1 - p)

            run_tiles(pe, tile, last=lambda: project(TILES - 1, 1))

        @block.scalar
        def _(act):
            for e in range(E):
                act.wait_ge(s["w_ps"], e + 1)
                act.activation(w_hi[:, e, :], ps_a[e % 2][:], ACT.Copy).then_inc(s["w_hi_ready"], 1)
            act.wait_ge(s["small_ps"], 1)
            act.activation(b1_cols[:], ps_b[0][:, 0:E * CH], ACT.Copy).then_inc(s["small_ready"], 1)
            act.activation(out_w[:].rearrange("p h d -> p (h d)"), ps_b[0][:, P:(NH2 + 1) * P], ACT.Copy) \
                .then_inc(s["small_ready"], 1)
            act.wait_ge(s["small_ready"], 2)

            def split(n, p, b):
                after(act, s["h3_loaded"][p], b, 16, 16)
                after(act, s["a_ps"][-1], n - 2, TURN, TURN)
                act.activation(x_hi[p][:], h3[p][:], ACT.Copy).then_inc(s["x_hi_ready"], 1)

            def tile(n, p, b):
                for i in range(UNITS):
                    e, h = unit(i)
                    bias = e * CH + NH2 + h
                    after(act, s["b_ps"][i % 2], n, HALF, i // 2 + 1)
                    after(act, s["weighed_ready"][i % DEPTH], n, TURN, i // DEPTH)
                    act.activation(sig[i % DEPTH][:], ps_b[i % 2][:], ACT.Sigmoid, bias=b1_cols[:, bias:bias + 1]) \
                        .then_inc(s["sig_ready"][i % DEPTH], 1)
                    if i == UNITS // 2 and (not isinstance(n, int) or n < TILES - 1):
                        split(n + 1, 1 - p, b + p)

            run_tiles(act, tile, first=lambda: split(0, 0, 0))

        @block.gpsimd
        def _(pool):
            def finish(n, p, b):
                after(pool, s["moe_ready"], n)
                after(pool, s["stored"][p], b - 1, 16, 16)
                apart(pool, s["pool_passed"])
                pool.tensor_tensor(res[p][:], moe[:], gb_all[:, b, :].unsqueeze(1).broadcast_to([P, NQ, P]), ALU.mult) \
                    .then_inc(s["moe_gated"], 1)
                after(pool, s["moe_gated"], n)
                after(pool, s["x2e_loaded"][p], b, 16, 16)
                pool.tensor_tensor(res[p][:], res[p][:], x2[p][:], ALU.add).then_inc(s["res_ready"], 1)

            def tile(n, p, b):
                after(pool, s["comb_loaded"][p], b, 16, 16)
                for i in range(UNITS):
                    e, h = unit(i)
                    after(pool, s["sig_ready"][i % DEPTH], n, TURN, i // DEPTH + 1)
                    after(pool, s["glu_ready"][i % DEPTH], n, TURN, i // DEPTH)
                    pool.tensor_tensor(weighed[i % DEPTH][:].rearrange("p (q t) -> p q t", q=NQ),
                                       sig[i % DEPTH][:].rearrange("p (q t) -> p q t", q=NQ),
                                       comb[p][:, :, e, :], ALU.mult).then_inc(s["weighed_ready"][i % DEPTH], 1)
                    if i == 11 and (not isinstance(n, int) or n > 0):
                        finish(n - 1, 1 - p, b - 1 + p)

            pool.wait_ge(s["small_in"], 64)
            run_tiles(pool, tile, last=lambda: finish(TILES - 1, 1, TILES // 2 - 1))

        @block.vector
        def _(dve):
            for e in range(E):
                dve.wait_ge(s["w_hi_ready"], e + 1)
                dve.tensor_tensor(w_lo[:, e, :], ps_a[e % 2][:], w_hi[:, e, :].bitcast(F32), ALU.subtract) \
                    .then_inc(s["w_lo_ready"], 1)
            dve.wait_ge(s["small_in"], 64)
            dve.wait_ge(s["small_ready"], 2)

            def split(n, p, b):
                after(dve, s["x_hi_ready"], n)
                after(dve, s["a_ps"][-1], n - 2, TURN, TURN)
                dve.tensor_tensor(x_lo[p][:], h3[p][:], x_hi[p][:].bitcast(F32), ALU.subtract).then_inc(s["x_lo_ready"], 1)

            def bias_out(n, p, b):
                after(dve, s["out_ps"], n)
                after(dve, s["moe_gated"], n - 1)
                for q in range(NQ):
                    at = n * NQ + q
                    ins_ = dve.scalar_tensor_tensor(out=moe[:, q, :], in0=out_b[:], scalar=csum_all[:, at:at + 1] if isinstance(at, int) else csum_all[:, bass.ds(at, 1)],
                                                    in1=ps_w[:, q * P:(q + 1) * P], op0=ALU.mult, op1=ALU.add)
                ins_.then_inc(s["moe_ready"], 1)

            def tile(n, p, b):
                def add(i):
                    e, h = unit(i)
                    after(dve, s["glu_ready"][i % DEPTH], n, TURN, i // DEPTH + 1)
                    if i - NH2 < NH2:
                        after(dve, s["glu_ready"][i - NH2], n, TURN, 1)
                    else:
                        after(dve, s["added"][i % 2], n, HALF - 1 - i % 2, i // 2 - 1)
                    ins_ = dve.tensor_tensor(total[p][h][:], total[p][h][:], glu[i % DEPTH][:], ALU.add)
                    ins_.then_inc(s["total_ready"] if i == UNITS - 1 else s["added"][i % 2], 1)

                for i in range(UNITS):
                    e, h = unit(i)
                    bias = e * CH + h
                    after(dve, s["a_ps"][i % DEPTH], n, TURN, i // DEPTH + 1)
                    after(dve, s["weighed_ready"][i % DEPTH], n, TURN, i // DEPTH + 1)
                    if e == 0:
                        after(dve, s["out_ps"], n - 2)
                    elif i == NH2:
                        after(dve, s["total_ready"], n - 1)
                    dve.scalar_tensor_tensor(out=(total[p][h] if e == 0 else glu[i % DEPTH])[:], in0=ps_a[i % DEPTH][:],
                                             scalar=b1_cols[:, bias:bias + 1], in1=weighed[i % DEPTH][:],
                                             op0=ALU.add, op1=ALU.mult).then_inc(s["glu_ready"][i % DEPTH], 1)
                    if i - 1 >= NH2:
                        add(i - 1)
                    if i == 8 and (not isinstance(n, int) or n > 0):
                        bias_out(n - 1, 1 - p, b)
                    if i == UNITS // 2 + 1 and (not isinstance(n, int) or n < TILES - 1):
                        split(n + 1, 1 - p, b + p)
                add(UNITS - 1)

            run_tiles(dve, tile, first=lambda: split(0, 0, 0), last=lambda: bias_out(TILES - 1, 1, 0))


_INS = ["L0_attn_x", "L0_attn_ln1_w", "L0_attn_mu_r", "L0_attn_mu_k", "L0_attn_mu_v", "L0_attn_mu_w", "L0_attn_mu_g",
        "L0_attn_Wr", "L0_attn_Wk", "L0_attn_Wv", "L0_attn_Wg", "L0_attn_Wo", "L0_attn_w0", "L0_attn_wA", "L0_attn_wB",
        "L0_attn_u", "L0_attn_gn_w", "L0_attn_gn_b", "L0_attn_ln2_w", "L0_attn_ffn_w1", "L0_attn_ffn_w2",
        "L0_ffn_Wg", "L0_ffn_W1", "L0_ffn_b1", "L0_ffn_Wo", "L0_ffn_bo", "L0_c", "L0_wmod"]


def kernel(**inputs):
    import concourse.bacc as bacc
    from concourse.bass_utils import run_bass_kernel_spmd

    nc = bacc.Bacc("TRN2", target_bir_lowering=False, num_devices=1)
    arrays, args = {}, {}
    for name in _INS:
        a = np.ascontiguousarray(inputs[name])
        arrays[f"in_{name}"] = a
        args[name] = nc.dram_tensor(f"in_{name}", a.shape, mybir.dt.from_np(a.dtype), kind="ExternalInput").ap()
    shape = inputs["L0_attn_x"].shape
    out = nc.dram_tensor("out_0", shape, F32, kind="ExternalOutput").ap()
    build(nc, args, out)
    r = run_bass_kernel_spmd(nc, [arrays], core_ids=[0])
    return r.results[0]["out_0"]
```

```python
from contextlib import ExitStack

import numpy as np

import concourse.bass as bass
from concourse import mybir

F32 = mybir.dt.float32
F32R = mybir.dt.float32r
ALU = mybir.AluOpType
ACT = mybir.ActivationFunctionType
AX_X = mybir.AxisListType.X

P = 128
EPS_LN = 1e-5
EPS_RMS = 1e-6
EPS_GN = 1e-5
EPS_TOPK = 1e-9
GATE_MIN = 0.25


class Signals:

    def __init__(self, nc, block, names, lists):
        self.by_name = {n: nc.alloc_semaphore(f"{block}_{n}") for n in names}
        for n, k in lists.items():
            self.by_name[n] = [nc.alloc_semaphore(f"{block}_{n}{i}") for i in range(k)]

    def __getitem__(self, name):
        return self.by_name[name]

    def reset(self, nc):
        handles = [h for v in self.by_name.values() for h in (v if isinstance(v, list) else [v])]
        nc.clear_and_free_semaphores(handles)
        nc.all_engine_barrier()


class Router:
    MAXL, Z, P1, R1, P2, R2, DEN = range(7)

    def __init__(self, dve, stepped, logits, rank, csum, hit, first, second, comb, top):
        E = logits.shape[-1]
        self.dve, self.stepped, self.count = dve, stepped, 0
        self.lg = logits.rearrange("p n q e -> p (n q) e")
        self.groups = G = self.lg.shape[1]
        self.experts, self.csum = E, csum
        self.rank = rank[:].unsqueeze(1).broadcast_to([P, G, E])
        self.hit, self.first, self.second, self.comb = (a.rearrange("p (g e) -> p g e", e=E) for a in (hit, first, second, comb))
        self.top = top.rearrange("p (a g) -> p a g", g=G)

    def done(self, ins_):
        self.count += 1
        ins_.then_inc(self.stepped, 1)
        self.dve.wait_ge(self.stepped, self.count)

    def wide(self, row):
        return self.top[:, row, :].unsqueeze(2).broadcast_to([P, self.groups, self.experts])

    def shift(self):
        self.done(self.dve.tensor_reduce(self.top[:, self.MAXL, :], self.lg, AX_X, ALU.max))
        self.done(self.dve.tensor_tensor(self.lg, self.lg, self.wide(self.MAXL), ALU.subtract))

    def scores(self):
        self.done(self.dve.tensor_reduce(self.top[:, self.Z, :], self.lg, AX_X, ALU.add))
        self.done(self.dve.reciprocal(self.top[:, self.Z, :], self.top[:, self.Z, :]))
        self.done(self.dve.tensor_tensor(self.lg, self.lg, self.wide(self.Z), ALU.mult))

    def find(self, value):
        self.done(self.dve.tensor_reduce(self.top[:, value, :], self.lg, AX_X, ALU.max))
        self.done(self.dve.tensor_tensor(self.hit, self.lg, self.wide(value), ALU.is_equal))
        self.done(self.dve.tensor_tensor(self.hit, self.hit, self.rank, ALU.mult))

    def take(self, place, mask):
        self.done(self.dve.tensor_reduce(self.top[:, place, :], self.hit, AX_X, ALU.max))
        self.done(self.dve.tensor_tensor(mask, self.rank, self.wide(place), ALU.is_equal))

    def take_first(self):
        self.take(self.R1, self.first)
        self.done(self.dve.scalar_tensor_tensor(out=self.lg, in0=self.first, scalar=-2.0, in1=self.lg, op0=ALU.mult, op1=ALU.add))

    def take_second(self):
        self.take(self.R2, self.second)

    def shares(self, ready):
        dve, top, P1, P2, DEN = self.dve, self.top, self.P1, self.P2, self.DEN
        self.done(dve.scalar_tensor_tensor(out=top[:, DEN, :], in0=top[:, P1, :], scalar=EPS_TOPK, in1=top[:, P2, :],
                                           op0=ALU.add, op1=ALU.add))
        self.done(dve.reciprocal(top[:, DEN, :], top[:, DEN, :]))
        self.done(dve.tensor_tensor(top[:, P1, :], top[:, P1, :], top[:, DEN, :], ALU.mult))
        self.done(dve.tensor_tensor(top[:, P2, :], top[:, P2, :], top[:, DEN, :], ALU.mult))
        self.done(dve.tensor_tensor(self.csum, top[:, P1, :], top[:, P2, :], ALU.add))
        self.done(dve.tensor_tensor(self.first, self.first, self.wide(P1), ALU.mult))
        self.done(dve.tensor_tensor(self.second, self.second, self.wide(P2), ALU.mult))
        dve.tensor_tensor(self.comb, self.first, self.second, ALU.add).then_inc(ready, 1)


def after(eng, sem, tile, step=1, k=1):
    value = tile * step + k
    if isinstance(value, int) and value <= 0:
        return
    eng.wait_ge(sem, value)


def apart(eng, passed):
    eng.sem_inc(passed, 1)


def build(nc, ins, out):
    x_in = ins["L0_attn_x"]
    B, T, D = x_in.shape
    H, DK = ins["L0_attn_u"].shape
    LORA = ins["L0_attn_wA"].shape[1]
    FF = ins["L0_attn_ffn_w1"].shape[1]
    E, H2, _ = ins["L0_ffn_W1"].shape
    HE = H2 // 2
    NT = 512
    NQ = NT // P
    TPB = T // NT
    TILES = B * TPB
    NF = FF // P
    NH2 = HE // P
    assert D == P and H * DK == P and DK == 8 and TPB == 2 and TILES % 2 == 0 and HE % P == 0 and LORA <= P

    x_rows = x_in.rearrange("b (n q p) d -> (b n) p q d", n=TPB, q=NQ)
    out_rows = out.rearrange("b (n q p) d -> (b n) p q d", n=TPB, q=NQ)
    mods_dram = nc.dram_tensor("mods_scratch", (B, 6, D), F32, kind="Internal").ap()
    x2_dram = nc.dram_tensor("x2_scratch", (TILES, P, NQ, D), F32, kind="Internal").ap()
    h3_dram = nc.dram_tensor("h3_scratch", (TILES, P, NT), F32, kind="Internal").ap()
    comb_dram = nc.dram_tensor("comb_scratch", (TILES, NQ * E, P), F32, kind="Internal").ap()

    with ExitStack() as keep:
        csum_all = keep.enter_context(nc.sbuf_tensor("csum_all", [P, TILES * NQ], F32))
        ident = keep.enter_context(nc.sbuf_tensor("ident", [P, P], F32))
        with nc.sbuf_tensor("h_all", [P, TILES, NQ, P], F32) as h_all:
            pass
        w_hi, w_lo = (keep.enter_context(nc.sbuf_tensor(n, [P, E, H2], F32R)) for n in ("w_hi", "w_lo"))
        assert 2 * E * H2 <= TILES * NT and H2 == NT
        with nc.sbuf_tensor("rs_prod", [P, 2, 4, NT], F32) as rs_prod:
            pass
        comb0 = keep.enter_context(nc.sbuf_tensor("comb0", [P, NQ, E, P], F32))
        assert NQ * E * P == 2 * 4 * NT
        logits = keep.enter_context(nc.sbuf_tensor("logits", [P, TILES, NQ, E], F32))
        expert_rank = keep.enter_context(nc.sbuf_tensor("expert_rank", [P, E], F32))
        with nc.sbuf_tensor("state_pair", [P, 2, NT], F32) as state_pair:
            pass
        x_hi0, x_lo0 = (keep.enter_context(nc.sbuf_tensor(n, [P, NT], F32R)) for n in ("x_hi0", "x_lo0"))
        b1_cols = keep.enter_context(nc.sbuf_tensor("b1_cols", [P, E * H2 // P], F32))
        out_w = keep.enter_context(nc.sbuf_tensor("out_w", [P, NH2, P], F32))
        comb_stored, first_comb, rest_comb = (nc.alloc_semaphore(n) for n in ("comb_stored", "first_comb", "rest_comb"))
        kept = (w_hi, w_lo, b1_cols, out_w, x_hi0, x_lo0, logits, expert_rank, comb0, comb_stored, first_comb, rest_comb)
        EARLY = TILES - 4
        assert EARLY % 4 == 0 and 4 * NQ * E == P
        signals = attention_block(nc, ins, x_rows, mods_dram, x2_dram, h3_dram, comb_dram, csum_all, ident, h_all, rs_prod, state_pair, EARLY, kept,
                        B, D, H, DK, LORA, NF, E, NT, NQ, TPB, TILES)
        signals.reset(nc)
        expert_block(nc, ins, out_rows, mods_dram, x2_dram, h3_dram, comb_dram, csum_all, ident, EARLY, kept,
                     B, D, E, HE, NH2, NT, NQ, TPB, TILES)


def attention_block(nc, ins, x_rows, mods_dram, x2_dram, h3_dram, comb_dram, csum_all, ident, h_all, rs_prod, state_pair, EARLY, kept,
                    B, D, H, DK, LORA, NF, E, NT, NQ, TPB, TILES):
    LAST = TILES - 1
    ORDER = [0, 2, 4, 6, 1, 3, 5, 7]
    (ROW_LN1, ROW_MUR, ROW_MUK, ROW_MUV, ROW_MUW, ROW_MUG, ROW_W0, ROW_U, ROW_LN2, ROW_GNW, ROW_GNB) = range(11)
    NROWS = 11
    NMIX = ROW_MUG - ROW_MUR + 1
    w_hi, w_lo, b1_cols, out_w, x_hi0, x_lo0, logits, expert_rank, comb0, comb_stored, first_comb, rest_comb = kept
    NH2 = out_w.shape[1]
    MIX_R, MIX_K, MIX_V, MIX_W, MIX_G = (row - ROW_MUR for row in (ROW_MUR, ROW_MUK, ROW_MUV, ROW_MUW, ROW_MUG))
    NOW, BEFORE = range(2)
    SA, A1, GA, SB, A2, GB = range(6)

    with ExitStack() as ctx:
        def sb(name, shape, dt=F32):
            return ctx.enter_context(nc.sbuf_tensor(name, shape, dt))

        def bank(name):
            return ctx.enter_context(nc.psum_tensor(name, [P, 512], F32))

        rows = sb("rows", [NROWS - 2, P])
        gn_rows, gn_turned = sb("gn_rows", [2, P]), sb("gn_turned", [2, P])
        cols = sb("cols", [P, NROWS])
        shares = sb("shares", [P, 2, NMIX])
        mix_hi, mix_lo = sb("mix_hi", [P, 2, NMIX, P], F32R), sb("mix_lo", [P, 2, NMIX, P], F32R)
        wa, wb = sb("wa", [P, P]), sb("wb", [P, P])
        wo = sb("wo", [P, P])
        w1_hi, w1_lo = (sb(n, [P, NF * P], F32R) for n in ("w1_hi", "w1_lo"))
        w2 = sb("w2", [P, NF, P])
        gate_w = sb("gate_w", [P, P])
        gate_rows = sb("gate_rows", [E, P])
        head_of_key = sb("head_of_key", [P, H])
        head_of_val = sb("head_of_val", [P, H])
        reduce_w = sb("reduce_w", [P, 2, 2 * H])
        bonus_w = sb("bonus_w", [P, P])
        center_w = sb("center_w", [P, P])
        minus_half = sb("minus_half", [P, NQ])
        eps_gn = sb("eps_gn", [P, 1])
        c_rows = sb("c_rows", [B, P])
        c_act = sb("c_act", [B, P])
        c_cols = sb("c_cols", [P, B])
        mod_rows = sb("mod_rows", [B, 6, P])
        first_row = sb("first_row", [B, P])
        mods = sb("mods", [P, B, 5, P])
        b1_rows, out_w_rows = sb("b1_rows", [E * (NT // P), P]), sb("out_w_rows", [P, out_w.shape[1] * P])
        xin = [sb(f"xin{i}", [P, NQ, P]) for i in range(2)]
        st1, mv1, shift1 = sb("st1", [P, NQ, 6]), sb("mv1", [P, NQ, 2]), sb("shift1", [P, NQ])
        ve1, rs1 = sb("ve1", [P, NQ]), sb("rs1", [P, NQ])
        mod_sign, mod_abs = h_all[0:B, TILES - 3, 0:2], h_all[0:B, TILES - 3, 2:4]
        mix_full = h_all[:, TILES - 6:TILES - 3].rearrange("p n q d -> p (n q) d")[:, 0:2 * NMIX].rearrange("p (a m) d -> p a m d", a=2)
        w1_full = h_all[:, TILES - 7].rearrange("p q d -> p (q d)")
        staged = h_all[:, TILES - 2:].rearrange("p n q d -> p (n q) d")[:, 0:6]
        ssq1, ve2, rs2 = sb("ssq1", [P, NQ]), sb("ve2", [P, NQ]), sb("rs2", [P, NQ])
        hn = sb("hn", [P, NQ, P])
        hnT_hi, hnT_lo = ([sb(f"{n}{i}", [P, 1 + NT], F32R) for i in range(2)] for n in ("hnT_hi", "hnT_lo"))
        kT, rT, dT, vT = ([sb(f"{n}{i}", [P, NT]) for i in range(2)] for n in ("kT", "rT", "dT", "vT"))
        v_spread = [sb(f"v_spread{i}", [P, NT]) for i in range(DK)]
        lora = sb("lora", [P, NT])
        ruk = sb("ruk", [P, NT])
        gate, bonus = ([sb(f"{n}{i}", [P, NT]) for i in range(2)] for n in ("gate", "bonus"))
        kv = [sb(f"kv{i}", [P, NT]) for i in range(2)]
        state = [state_pair[:, 0], state_pair[:, 1]] + [sb(f"state{i}", [P, NT])[:] for i in range(2, 4)]
        state_end = sb("state_end", [P, DK])
        o_sum, o_sq = sb("o_sum", [P, NT]), sb("o_sq", [P, NT])
        var_g, sd_g, rs_g = (sb(n, [P, NQ, H]) for n in ("var_g", "sd_g", "rs_g"))
        o_norm, o_gated = sb("o_norm", [P, NT]), sb("o_gated", [P, NT])
        ssq3, ve3, rs3 = sb("ssq3", [P, NQ]), sb("ve3", [P, NQ]), sb("rs3", [P, NQ])
        h2 = sb("h2", [P, NQ, P])
        h2T_hi, h2T_lo = (sb(n, [P, NT], F32R) for n in ("h2T_hi", "h2T_lo"))
        gel = [sb(f"gel{c}", [P, NT]) for c in range(NF)]
        xre, x2 = ([sb(f"{n}{i}", [P, NQ, P]) for i in range(2)] for n in ("xre", "x2"))
        st4, mv4, shift4 = sb("st4", [P, NQ, 6]), sb("mv4", [P, NQ, 2]), sb("shift4", [P, NQ])
        ve4, rs4 = sb("ve4", [P, NQ]), sb("rs4", [P, NQ])
        h3 = sb("h3", [P, NQ, P])
        h3T = [sb(f"h3T{i}", [P, NT]) for i in range(2)]

        ps_f = [bank("ps_f0"), bank("ps_f1")]
        ps_o, ps_g, ps_m, ps_k1, ps_k2, ps_k3 = (bank(n) for n in ("ps_o", "ps_g", "ps_m", "ps_k1", "ps_k2", "ps_k3"))
        split_banks = ps_f + [ps_o, ps_g, ps_m, ps_k2]
        SPLIT_BANKS = len(split_banks)
        w_full = v_spread
        first_h3 = gel[0]
        assert E <= len(w_full)

        s = Signals(nc, "attention", (
            "sp_passed act_passed dve_passed pool_passed vectors_in weights_in more_in cond_in ident_zero ident_ready wpad_zero consts_ready "
            "cols_ps cols_ready selectors_part gate_ps gate_ready silu_ready cT_ps cT_ready "
            "mod_ps mod_copied mod_step mod_ready mod_stored first_mods_ps first_mods_ready mods_in setup_step weights_step mix_ready "
            "ln1_stats ln1_mv ln1_ve ln1_rstd xn1_ready h_scaled h_ready ssq1_ready rms1_ve rms1_rstd hn_ready "
            "hnT_ps hnT_ready hnlo_ready k_ps k_ready v_ps vT_ready "
            "lora_ps lora_ready w_ps expw_ready d_ready r_ps r_ready "
            "g_ps tanh_ready gate_set ruk_ready bonus_ps bonus_ready red_even red_odd "
            "o_ready cen_ps osq_ready var_ready sd_ready rsg_ready onorm_ready onT_ps oaff_ready ogated_ready wo_ps x1_ready "
            "ssq3_ready rms2_ve rms2_rstd h2_ready h2T_ps h2T_ready h2lo_ready ffn2_ps y_ready y_gated x2_ready "
            "shift1_ready shift2_ready kv_ready ln2_stats ln2_mv ln2_ve ln2_rstd xn4_ready h3_scaled h3_ready h3T_ps h3T_ready logits_ps logits_ready "
            "x_hi_ready x_lo_ready small_ps small_ready expert_in expert_ps expert_hi expert_lo route_step exp_ready comb_ready combT_ps combT_ready").split(),
            {"x_loaded": 2, "xre_loaded": 2, "x2_stored": 2, "h3_stored": 2, "v_spread": DK,
             "scan_ready": 8, "rs_ready": 8, "ffn1_ps": NF, "gelu_ready": NF})

        LOOP_FROM = 10
        MAX_LAG = 8

        WEIGHTS_AT, FIRST_PRODUCT_AT, GATE_AT, FIRST_KEY_AT = 2, 1, 5, 1
        EXPERTS_AT = TILES + 5
        CH = NT // P
        SOON = 2
        VECTOR_EXPERTS = E // 2

        def beside(t, tile, work, *args):
            if isinstance(t, int) and t == tile:
                work(*args)

        def run_pipeline(eng, step, before):
            def peeled(it):
                if it in before:
                    before[it]()
                step(lambda lag: [(it - lag, (it - lag) % 2, (it - lag) // TPB)] if 0 <= it - lag <= LAST else [])

            for it in range(LOOP_FROM):
                peeled(it)
            with eng.Fori(LOOP_FROM // 2, TILES // 2) as g:
                for u in range(2):
                    step(lambda lag: [(g * 2 + (u - lag), (u - lag) % 2, g + (u - lag) // 2)])
            for it in range(TILES, TILES + MAX_LAG):
                peeled(it)

        def upto(tile):
            return min(tile, LAST) if isinstance(tile, int) else tile

        def quarters(ap):
            return ap.rearrange("p (q d) -> p q d", q=NQ)

        def mod_row(which, batch):
            return mods[:, batch, which, :].unsqueeze(1).broadcast_to([P, NQ, P])

        block = ctx.enter_context(nc.Block())

        @block.sync
        def _(sp):
            def load_tokens(t, p):
                sp.dma_start(xin[p][:], x_rows[t]).then_inc(s["x_loaded"][p], 16)

            sp.dma_start(c_rows[:], ins["L0_c"]).then_inc(s["cond_in"], 16)
            sp.dma_start(staged[:, 0:6, :].rearrange("p a d -> p (a d)"), ins["L0_wmod"]).then_inc(s["cond_in"], 16)
            for row, name in ((ROW_LN1, "ln1_w"), (ROW_MUR, "mu_r"), (ROW_MUK, "mu_k"), (ROW_MUV, "mu_v"),
                              (ROW_MUW, "mu_w"), (ROW_MUG, "mu_g"), (ROW_W0, "w0"), (ROW_LN2, "ln2_w")):
                sp.dma_start(rows[row:row + 1, :], ins["L0_attn_" + name].rearrange("(a d) -> a d", a=1)) \
                    .then_inc(s["vectors_in"], 16)
            sp.dma_start(rows[ROW_U:ROW_U + 1, :].rearrange("a (h k) -> a h k", h=H),
                         ins["L0_attn_u"].rearrange("(a h) k -> a h k", a=1)).then_inc(s["vectors_in"], 16)
            for i, name in enumerate(("gn_w", "gn_b")):
                sp.dma_start(gn_rows[i:i + 1, :].rearrange("a (h j) -> a h j", h=H),
                             ins["L0_attn_" + name].rearrange("(a h) j -> a h j", a=1)).then_inc(s["vectors_in"], 16)
            for tile in range(2):
                load_tokens(tile, tile)
            sp.wait_ge(s["wpad_zero"], 3)
            sp.dma_start(wa[:, 0:LORA], ins["L0_attn_wA"]).then_inc(s["weights_in"], 16)
            sp.wait_ge(s["mod_ps"], 2)
            for i, name in enumerate(("Wk", "Wv", "Wr", "Wg")):
                sp.dma_start(staged[:, i, :], ins["L0_attn_" + name]).then_inc(s["weights_in"], 16)
            sp.wait_ge(s["mod_ready"], 1)
            sp.dma_start(mods_dram, mod_rows[:]).then_inc(s["mod_stored"], 16)
            sp.dma_start(w1_full, ins["L0_attn_ffn_w1"]).then_inc(s["weights_in"], 16)
            sp.dma_start(wb[0:LORA, :], ins["L0_attn_wB"]).then_inc(s["weights_in"], 16)
            sp.wait_ge(s["mod_stored"], 16)
            sp.dma_start(mods[:, 1:B], mods_dram[1:B, 0:5, :].unsqueeze(0).broadcast_to([P, B - 1, 5, P])).then_inc(s["mods_in"], 16)
            for j in range(DK):
                sp.dma_start(wo[j * H:(j + 1) * H, :],
                             ins["L0_attn_Wo"].rearrange("(h j) d -> j h d", j=DK)[j]).then_inc(s["more_in"], 16)
            sp.dma_start(w2[:], ins["L0_attn_ffn_w2"].rearrange("(c p) d -> p c d", p=P)).then_inc(s["more_in"], 16)
            sp.dma_start(gate_rows[:], ins["L0_ffn_Wg"]).then_inc(s["more_in"], 16)
            sp.dma_start(b1_rows[:], ins["L0_ffn_b1"].rearrange("e (c p) -> (e c) p", p=P)).then_inc(s["more_in"], 16)
            sp.dma_start(out_w_rows[:], ins["L0_ffn_Wo"]).then_inc(s["more_in"], 16)

            def spread_value(idx, p):
                j = ORDER[idx]
                sp.dma_start(v_spread[idx][:], vT[p][j * H:(j + 1) * H, :].unsqueeze(1).broadcast_to([H, DK, NT])) \
                    .then_inc(s["v_spread"][idx], 16)

            def step(tile):
                for t, p, b in tile(0):
                    if not isinstance(t, int) or t >= 2:
                        after(sp, s["xn1_ready"], t - 2)
                        apart(sp, s["sp_passed"])
                        load_tokens(t, p)
                for t, p, b in tile(3):
                    after(sp, s["vT_ready"], t)
                    apart(sp, s["sp_passed"])
                    after(sp, s["kv_ready"], t - 1, DK, 6)
                    apart(sp, s["sp_passed"])
                    spread_value(5, p)
                    after(sp, s["vT_ready"], t)
                    apart(sp, s["sp_passed"])
                    after(sp, s["kv_ready"], t - 1, DK, 7)
                    apart(sp, s["sp_passed"])
                    spread_value(6, p)
                    after(sp, s["vT_ready"], t)
                    apart(sp, s["sp_passed"])
                    after(sp, s["kv_ready"], t - 1, DK, 8)
                    apart(sp, s["sp_passed"])
                    spread_value(7, p)
                for t, p, b in tile(2):
                    after(sp, s["vT_ready"], t)
                    apart(sp, s["sp_passed"])
                    after(sp, s["kv_ready"], t - 1, DK, 1)
                    apart(sp, s["sp_passed"])
                    spread_value(0, p)
                    after(sp, s["vT_ready"], t)
                    apart(sp, s["sp_passed"])
                    after(sp, s["kv_ready"], t - 1, DK, 2)
                    apart(sp, s["sp_passed"])
                    spread_value(1, p)
                    after(sp, s["vT_ready"], t)
                    apart(sp, s["sp_passed"])
                    after(sp, s["kv_ready"], t - 1, DK, 3)
                    apart(sp, s["sp_passed"])
                    spread_value(2, p)
                for t, p, b in tile(5):
                    after(sp, s["x2_ready"], t - 2)
                    apart(sp, s["sp_passed"])
                    sp.dma_start(xre[p][:], x_rows[t]).then_inc(s["xre_loaded"][p], 16)
                for t, p, b in tile(2):
                    after(sp, s["vT_ready"], t)
                    apart(sp, s["sp_passed"])
                    after(sp, s["kv_ready"], t - 1, DK, 4)
                    apart(sp, s["sp_passed"])
                    spread_value(3, p)
                    after(sp, s["vT_ready"], t)
                    apart(sp, s["sp_passed"])
                    after(sp, s["kv_ready"], t - 1, DK, 5)
                    apart(sp, s["sp_passed"])
                    spread_value(4, p)
                for t, p, b in tile(7):
                    after(sp, s["x2_ready"], t)
                    apart(sp, s["sp_passed"])
                    sp.dma_start(x2_dram[t], x2[p][:]).then_inc(s["x2_stored"][p], 16)
                    beside(t, LAST, load_first_input)
                for t, p, b in tile(8):
                    after(sp, s["h3T_ready"], t)
                    apart(sp, s["sp_passed"])
                    sp.dma_start(h3_dram[t], h3T[p][:]).then_inc(s["h3_stored"][p], 16)

            def load_experts():
                w_dram = ins["L0_ffn_W1"].rearrange("e (c p) d -> e p c d", p=P)
                sp.wait_ge(s["red_odd"], TILES)
                for e in range(E):
                    sp.dma_start(rs_prod[:, e // 4, e % 4].rearrange("p (c d) -> p c d", d=P), w_dram[e]) \
                        .then_inc(s["expert_in"], 16)

            def load_first_input():
                sp.wait_ge(s["ffn2_ps"], TILES)
                sp.wait_ge(s["h3_stored"][0], 16)
                sp.dma_start(first_h3[:], h3_dram[0]).then_inc(s["more_in"], 16)

            run_pipeline(sp, step, {EXPERTS_AT: load_experts})
            sp.wait_ge(s["combT_ready"], 1)
            for g in range(EARLY // 4):
                sp.dma_start(comb_dram[4 * g:4 * g + 4].rearrange("n r t -> (n r) t"), kv[0][:, g * P:(g + 1) * P]) \
                    .then_inc(comb_stored, 16)
            sp.wait_ge(comb_stored, 16 * (EARLY // 4))
            rows_of = comb_dram[0].rearrange("(q e) t -> q (e t)", e=E)
            place = comb0[:].rearrange("p q e t -> p q (e t)")
            for cols_of, loaded in ((slice(0, SOON * P), first_comb), (slice(SOON * P, E * P), rest_comb)):
                sp.dma_start(place[:, :, cols_of], rows_of[:, cols_of].unsqueeze(0).broadcast_to(list(place[:, :, cols_of].shape))) \
                    .then_inc(loaded, 16)
            for p in range(2):
                sp.wait_ge(s["x2_stored"][p], 16 * (TILES // 2))
                sp.wait_ge(s["h3_stored"][p], 16 * (TILES // 2))

        @block.gpsimd
        def _(pool):
            pool.memset(wa[:], 0.0).then_inc(s["wpad_zero"], 1)
            pool.memset(wb[:], 0.0).then_inc(s["wpad_zero"], 1)
            pool.memset(gate_w[:], 0.0).then_inc(s["wpad_zero"], 1)
            pool.memset(ident[:], 0.0).then_inc(s["ident_zero"], 1)
            pool.memset(first_row[:], 0.0).then_inc(s["ident_zero"], 1)
            pool.wait_ge(s["ident_zero"], 2)
            pool.memset(first_row[0:1, :], 1.0).then_inc(s["consts_ready"], 1)
            pool.affine_select(out=ident[:], in_=ident[:], compare_op=ALU.not_equal, fill=1.0, base=0,
                               pattern=[[-1, P]], channel_multiplier=1).then_inc(s["ident_ready"], 1)
            pool.memset(minus_half[:], -0.5).then_inc(s["consts_ready"], 1)
            pool.memset(eps_gn[:], EPS_GN).then_inc(s["consts_ready"], 1)
            pool.memset(reduce_w[:], 0.0).then_inc(s["consts_ready"], 1)
            pool.memset(hnT_hi[0][:, 0:1].bitcast(F32), 0.0).then_inc(s["consts_ready"], 1)
            pool.memset(hnT_lo[0][:, 0:1].bitcast(F32), 0.0).then_inc(s["consts_ready"], 1)
            for j in range(4):
                pool.memset(rs_prod[:, 0, j, 0:1], 0.0).then_inc(s["consts_ready"], 1)
            for e in range(E):
                pool.memset(expert_rank[:, e:e + 1], float(E - e)).then_inc(s["consts_ready"], 1)
            pool.wait_ge(s["consts_ready"], 18)

            def products(idx, p):
                j = ORDER[idx]
                dst, st = rs_prod[:, p, idx % 4], state[idx % 4]
                pool.tensor_tensor(dst[:, 1:NT], rT[p][:, 1:NT], st[:, 0:NT - 1], ALU.mult)
                if p == 0:
                    pool.tensor_copy(state_end[:, j:j + 1], st[:, NT - 1:NT]).then_inc(s["rs_ready"][idx], 1)
                else:
                    pool.tensor_tensor(dst[:, 0:1], rT[p][:, 0:1], state_end[:, j:j + 1], ALU.mult) \
                        .then_inc(s["rs_ready"][idx], 1)

            def step(tile):
                for t, p, b in tile(8):
                    after(pool, s["xn4_ready"], t)
                    apart(pool, s["pool_passed"])
                    pool.tensor_tensor(h3[:], h3[:], mod_row(A2, b), ALU.mult).then_inc(s["h3_scaled"], 1)
                for t, p, b in tile(7):
                    if not isinstance(t, int) or t < LAST:
                        after(pool, s["y_ready"], t)
                        apart(pool, s["pool_passed"])
                        pool.tensor_tensor(x2[p][:], x2[p][:], mod_row(GA, b), ALU.mult).then_inc(s["y_gated"], 1)
                for t, p, b in tile(4):
                    after(pool, s["scan_ready"][6], t)
                    after(pool, s["red_even"], t)
                    products(6, p)
                    after(pool, s["scan_ready"][7], t)
                    after(pool, s["red_even"], t)
                    products(7, p)
                for t, p, b in tile(8):
                    after(pool, s["h3_scaled"], t)
                    apart(pool, s["pool_passed"])
                    pool.tensor_tensor(h3[:], h3[:], mod_row(SB, b), ALU.add).then_inc(s["h3_ready"], 1)
                for t, p, b in tile(3):
                    after(pool, s["scan_ready"][0], t)
                    after(pool, s["r_ready"], t)
                    products(0, p)
                for t, p, b in tile(1):
                    after(pool, s["xn1_ready"], t)
                    if isinstance(t, int):
                        pool.wait_ge(s["first_mods_ready"], 2)
                    apart(pool, s["pool_passed"])
                    pool.tensor_tensor(h_all[:, t], h_all[:, t], mod_row(A1, b), ALU.mult).then_inc(s["h_scaled"], 1)
                for t, p, b in tile(3):
                    after(pool, s["scan_ready"][1], t)
                    products(1, p)
                    after(pool, s["scan_ready"][2], t)
                    products(2, p)
                    after(pool, s["scan_ready"][3], t)
                    products(3, p)
                for t, p, b in tile(5):
                    after(pool, s["ssq3_ready"], t)
                    apart(pool, s["pool_passed"])
                    pool.tensor_scalar(ve3[:], ssq3[:], 1.0 / D, EPS_RMS, ALU.mult, ALU.add).then_inc(s["rms2_ve"], 1)
                    after(pool, s["rms2_ve"], t)
                    pool.tensor_tensor(rs3[:], ve3[:], minus_half[:], ALU.pow).then_inc(s["rms2_rstd"], 1)
                for t, p, b in tile(1):
                    after(pool, s["ssq1_ready"], t)
                    apart(pool, s["pool_passed"])
                    pool.tensor_scalar(ve2[:], ssq1[:], 1.0 / D, EPS_RMS, ALU.mult, ALU.add).then_inc(s["rms1_ve"], 1)
                    after(pool, s["rms1_ve"], t)
                    pool.tensor_tensor(rs2[:], ve2[:], minus_half[:], ALU.pow).then_inc(s["rms1_rstd"], 1)
                for t, p, b in tile(7):
                    after(pool, s["ln2_mv"], t)
                    apart(pool, s["pool_passed"])
                    pool.tensor_scalar(ve4[:], mv4[:, :, 1], 1.0, EPS_LN, ALU.mult, ALU.add).then_inc(s["ln2_ve"], 1)
                    after(pool, s["ln2_ve"], t)
                    pool.tensor_tensor(rs4[:], ve4[:], minus_half[:], ALU.pow).then_inc(s["ln2_rstd"], 1)
                for t, p, b in tile(3):
                    after(pool, s["scan_ready"][4], t)
                    after(pool, s["red_even"], t)
                    products(4, p)
                for t, p, b in tile(0):
                    after(pool, s["ln1_mv"], t)
                    apart(pool, s["pool_passed"])
                    pool.tensor_scalar(ve1[:], mv1[:, :, 1], 1.0, EPS_LN, ALU.mult, ALU.add).then_inc(s["ln1_ve"], 1)
                for t, p, b in tile(3):
                    after(pool, s["scan_ready"][5], t)
                    after(pool, s["red_even"], t)
                    products(5, p)
                for t, p, b in tile(0):
                    after(pool, s["ln1_ve"], t)
                    pool.tensor_tensor(rs1[:], ve1[:], minus_half[:], ALU.pow).then_inc(s["ln1_rstd"], 1)

            run_pipeline(pool, step, {TPB: lambda: pool.wait_ge(s["mods_in"], 16)})
            for e in range(VECTOR_EXPERTS, E):
                pool.wait_ge(s["expert_hi"], e + 1)
                pool.tensor_tensor(w_lo[:, e], w_full[e][:], w_hi[:, e].bitcast(F32), ALU.subtract).then_inc(s["expert_lo"], 1)
            pool.wait_ge(s["x_hi_ready"], 1)
            pool.tensor_tensor(x_lo0[:], first_h3[:], x_hi0[:].bitcast(F32), ALU.subtract).then_inc(s["x_lo_ready"], 1)
            pool.wait_ge(s["x_lo_ready"], 1)
            pool.wait_ge(s["expert_lo"], E)

        @block.scalar
        def _(act):
            act.wait_ge(s["cond_in"], 32)
            act.activation(c_act[:], c_rows[:], ACT.Silu).then_inc(s["silu_ready"], 1)
            act.wait_ge(s["cT_ps"], 1)
            act.activation(c_cols[:], ps_k1[:, 0:B], ACT.Copy).then_inc(s["cT_ready"], 1)
            for i in range(2):
                act.wait_ge(s["mod_ps"], i + 1)
                act.activation(mod_rows[:, 3 * i:3 * i + 3, :].rearrange("b a d -> b (a d)"), ps_f[i][0:B, 0:3 * P],
                               ACT.Copy).then_inc(s["mod_copied"], 1)
            act.wait_ge(s["cols_ps"], 1)
            act.activation(cols[:], ps_k2[:, 0:NROWS], ACT.Copy).then_inc(s["cols_ready"], 1)
            act.wait_ge(s["consts_ready"], 18)
            act.wait_ge(s["first_mods_ps"], 1)
            act.activation(mods[:, 0, 0:4, :], quarters(ps_g[:]), ACT.Copy).then_inc(s["first_mods_ready"], 1)
            act.activation(mods[:, 0, 4, :], ps_m[:, 0:P], ACT.Copy).then_inc(s["first_mods_ready"], 1)

            def keep_gate():
                act.wait_ge(s["gate_ps"], 1)
                act.wait_ge(s["wpad_zero"], 3)
                act.activation(gate_w[:, 0:E], ps_k3[:, 0:E], ACT.Copy).then_inc(s["gate_ready"], 1)

            def sum_squares(src, room, dst, done):
                for q in range(NQ):
                    ins_ = act.activation(room[:, q, :], src[:, q, :], ACT.Square, accum_out=dst[:, q:q + 1])
                ins_.then_inc(done, 1)

            def normalize(dst, src, scale, shift, done):
                for q in range(NQ):
                    ins_ = act.activation(dst[:, q, :], src[:, q, :], ACT.Identity, scale=scale[:, q:q + 1], bias=shift[:, q:q + 1])
                ins_.then_inc(done, 1)

            def scale_rows(dst, src, scale, done):
                for q in range(NQ):
                    ins_ = act.activation(dst[:, q, :], src[:, q, :], ACT.Copy, scale=scale[:, q:q + 1])
                ins_.then_inc(done, 1)

            def step(tile):
                for t, p, b in tile(2):
                    after(act, s["expw_ready"], t)
                    act.activation(dT[p][:], dT[p][:], ACT.Exp, scale=-1.0).then_inc(s["d_ready"], 1)
                for t, p, b in tile(8):
                    after(act, s["logits_ps"], t)
                    apart(act, s["act_passed"])
                    act.activation(logits[:, t], quarters(ps_k3[:])[:, :, 0:E], ACT.Copy).then_inc(s["logits_ready"], 1)
                    beside(t, LAST - 2, keep_small)
                    beside(t, LAST - 2, round_experts, 0, 2)
                    beside(t, LAST - 1, round_experts, 6, 7)
                    beside(t, LAST - 1, round_first_input)
                for t, p, b in tile(2):
                    after(act, s["r_ps"], t)
                    act.activation(rT[p][:], ps_f[1][:], ACT.Copy).then_inc(s["r_ready"], 1)
                for t, p, b in tile(1):
                    after(act, s["hnT_ps"], t)
                    if p == 1:
                        act.activation(hnT_hi[1][:, 0:1], hnT_hi[0][:, NT:NT + 1], ACT.Copy)
                    act.activation(hnT_hi[p][:, 1:NT + 1], ps_f[0][:], ACT.Copy).then_inc(s["hnT_ready"], 1)
                for t, p, b in tile(0):
                    after(act, s["shift1_ready"], t)
                    after(act, s["ln1_rstd"], t)
                    apart(act, s["act_passed"])
                    normalize(h_all[:, t], xin[p], rs1, shift1, s["xn1_ready"])
                for t, p, b in tile(5):
                    after(act, s["ffn1_ps"][1], t)
                    act.activation(gel[1][:], ps_m[:], ACT.Gelu).then_inc(s["gelu_ready"][1], 1)
                    after(act, s["ffn1_ps"][0], t)
                    act.activation(gel[0][:], ps_k2[:], ACT.Gelu).then_inc(s["gelu_ready"][0], 1)
                for t, p, b in tile(1):
                    after(act, s["k_ps"], t)
                    act.activation(kT[p][:], ps_f[1][:], ACT.Copy).then_inc(s["k_ready"], 1)
                for t, p, b in tile(2):
                    after(act, s["g_ps"], t)
                    act.activation(gate[p][:], ps_g[:], ACT.Tanh, scale=0.5).then_inc(s["tanh_ready"], 1)
                for t, p, b in tile(4):
                    after(act, s["x1_ready"], t)
                    apart(act, s["act_passed"])
                    sum_squares(h_all[:, t], h2, ssq3, s["ssq3_ready"])
                for t, p, b in tile(1):
                    after(act, s["v_ps"], t)
                    after(act, s["v_spread"][7], t - 2, 16, 16)
                    act.activation(vT[p][:], ps_f[0][:], ACT.Copy).then_inc(s["vT_ready"], 1)
                for t, p, b in tile(5):
                    after(act, s["ffn1_ps"][3], t)
                    act.activation(gel[3][:], ps_m[:], ACT.Gelu).then_inc(s["gelu_ready"][3], 1)
                    after(act, s["ffn1_ps"][2], t)
                    act.activation(gel[2][:], ps_k2[:], ACT.Gelu).then_inc(s["gelu_ready"][2], 1)
                    beside(t, LAST, exponentials)
                for t, p, b in tile(3):
                    after(act, s["cen_ps"], t)
                    act.activation(o_sq[:], ps_k1[:], ACT.Square).then_inc(s["osq_ready"], 1)
                for t, p, b in tile(0):
                    after(act, s["h_ready"], t)
                    apart(act, s["act_passed"])
                    sum_squares(h_all[:, t], hn, ssq1, s["ssq1_ready"])
                for t, p, b in tile(1):
                    after(act, s["lora_ps"], t)
                    act.activation(lora[:], ps_f[1][:], ACT.Tanh).then_inc(s["lora_ready"], 1)
                for t, p, b in tile(4):
                    after(act, s["rms2_rstd"], t)
                    apart(act, s["act_passed"])
                    scale_rows(h2, h_all[:, t], rs3, s["h2_ready"])
                for t, p, b in tile(3):
                    after(act, s["var_ready"], t)
                    act.activation(sd_g[:], var_g[:], ACT.Sqrt, scale=1.0 / DK, bias=eps_gn[:]).then_inc(s["sd_ready"], 1)
                for t, p, b in tile(0):
                    after(act, s["rms1_rstd"], t)
                    apart(act, s["act_passed"])
                    scale_rows(hn, h_all[:, t], rs2, s["hn_ready"])
                for t, p, b in tile(6):
                    after(act, s["shift2_ready"], t)
                    after(act, s["ln2_rstd"], t)
                    after(act, s["h3T_ps"], t - 1)
                    apart(act, s["act_passed"])
                    normalize(h3, x2[p], rs4, shift4, s["xn4_ready"])
                for t, p, b in tile(1):
                    after(act, s["w_ps"], t)
                    act.activation(dT[p][:], ps_f[0][:], ACT.Exp, bias=cols[:, ROW_W0:ROW_W0 + 1]).then_inc(s["expw_ready"], 1)
                for t, p, b in tile(7):
                    after(act, s["h3T_ps"], t)
                    after(act, s["h3_stored"][p], b - 1, 16, 16)
                    act.activation(h3T[p][:], ps_k3[:], ACT.Copy).then_inc(s["h3T_ready"], 1)
                    beside(t, LAST - 1, round_experts, 2, 6)
                    beside(t, LAST, keep_comb)
                    beside(t, LAST, round_experts, 7, E)
                for t, p, b in tile(4):
                    after(act, s["h2T_ps"], t)
                    act.activation(h2T_hi[:], ps_k2[:], ACT.Copy).then_inc(s["h2T_ready"], 1)
                for t, p, b in tile(3):
                    after(act, s["onT_ps"], t)
                    act.activation(o_gated[:], ps_k1[:], ACT.Identity, scale=cols[:, ROW_GNW:ROW_GNW + 1],
                                   bias=cols[:, ROW_GNB:ROW_GNB + 1]).then_inc(s["oaff_ready"], 1)

            def exponentials():
                act.wait_ge(s["route_step"], 2)
                lg = logits[:, 0:EARLY].rearrange("p n q e -> p (n q e)")
                act.activation(lg, lg, ACT.Exp).then_inc(s["exp_ready"], 1)

            def keep_small():
                act.wait_ge(s["small_ps"], 1)
                act.activation(b1_cols[:], ps_k1[:, 0:E * CH], ACT.Copy).then_inc(s["small_ready"], 1)
                act.activation(out_w[:], ps_k1[:, P:P + NH2 * P].rearrange("p (h d) -> p h d", h=NH2), ACT.Copy).then_inc(s["small_ready"], 1)

            def round_experts(first, end):
                act.wait_ge(s["y_ready"], TILES)
                for e in range(first, end):
                    act.wait_ge(s["expert_ps"], e + 1)
                    act.activation(w_full[e][:], split_banks[e % SPLIT_BANKS][:], ACT.Copy)
                    act.activation(w_hi[:, e], split_banks[e % SPLIT_BANKS][:], ACT.Copy).then_inc(s["expert_hi"], 1)

            def round_first_input():
                act.wait_ge(s["more_in"], 16 * (DK + 5))
                act.activation(x_hi0[:], first_h3[:], ACT.Copy).then_inc(s["x_hi_ready"], 1)

            def keep_comb():
                act.wait_ge(s["combT_ps"], 1)
                act.activation(kv[0][:, 0:EARLY * NQ * E], ps_k1[:, 0:EARLY * NQ * E], ACT.Copy).then_inc(s["combT_ready"], 1)

            run_pipeline(act, step, {FIRST_KEY_AT + 1: keep_gate})
            act.wait_ge(s["x_hi_ready"], 1)
            act.wait_ge(s["small_ready"], 2)

        @block.tensor
        def _(pe):
            pe.wait_ge(s["ident_ready"], 1)
            pe.wait_ge(s["silu_ready"], 1)
            pe.transpose(ps_k1[:, 0:B], c_act[:], ident[0:B, 0:B]).then_inc(s["cT_ps"], 1)
            pe.wait_ge(s["cT_ready"], 1)
            for i in range(2):
                pe.matmul(ps_f[i][0:B, 0:3 * P], c_cols[:], staged[:, 3 * i:3 * i + 3, :].rearrange("p a d -> p (a d)"),
                          start=True, stop=True).then_inc(s["mod_ps"], 1)
            pe.wait_ge(s["vectors_in"], 16 * NROWS)
            pe.transpose(ps_k2[:, 0:ROW_GNW], rows[:], ident[0:ROW_GNW, 0:ROW_GNW])
            pe.wait_ge(s["setup_step"], 2)
            pe.transpose(ps_k2[:, ROW_GNW:NROWS], gn_turned[:], ident[0:2, 0:2]).then_inc(s["cols_ps"], 1)
            pe.wait_ge(s["mod_ready"], 1)
            pe.wait_ge(s["consts_ready"], 18)
            pe.matmul(ps_g[:], first_row[:], mod_rows[:, 0:4, :].rearrange("b a d -> b (a d)"), start=True, stop=True)
            pe.matmul(ps_m[:, 0:P], first_row[:], mod_rows[:, 4, :], start=True, stop=True).then_inc(s["first_mods_ps"], 1)
            pe.wait_ge(s["first_mods_ready"], 2)
            pe.wait_ge(s["mod_copied"], 2)
            pe.wait_ge(s["cols_ready"], 1)

            def await_weights():
                pe.wait_ge(s["weights_in"], 16 * 7)
                pe.wait_ge(s["setup_step"], 2)
                pe.wait_ge(s["mix_ready"], 1)
                pe.wait_ge(s["more_in"], 16 * (DK + 4))
                pe.transpose(ps_k3[:, 0:E], gate_rows[:], ident[0:E, 0:E]).then_inc(s["gate_ps"], 1)

            def await_gate():
                pe.wait_ge(s["gate_ready"], 1)
                pe.wait_ge(s["setup_step"], 3)

            def turn(dst, src, done):
                for q in range(NQ):
                    mm = pe.transpose(dst[:, q * P:(q + 1) * P], src[:, q, :], ident[:])
                mm.then_inc(done, 1)

            def reduce_heads(p, half, done):
                for quad in range(4):
                    mm = pe.matmul(ps_o[32 * quad:32 * quad + 32, :], reduce_w[:, half, :], rs_prod[:, p, quad],
                                   start=(half == 0), stop=(half == 1))
                mm.then_inc(done, 1)

            def ffn1(c):
                dst = ps_k2 if c % 2 == 0 else ps_m
                cs = slice(c * P, (c + 1) * P)
                pe.matmul(dst[:], w1_hi[:, cs], h2T_hi[:], start=True, stop=False)
                pe.matmul(dst[:], w1_hi[:, cs], h2T_lo[:], start=False, stop=False)
                pe.matmul(dst[:], w1_lo[:, cs], h2T_hi[:], start=False, stop=True).then_inc(s["ffn1_ps"][c], 1)

            def mixed(dst, m, p, done):
                for a, cols_of in ((NOW, slice(1, NT + 1)), (BEFORE, slice(0, NT))):
                    pe.matmul(dst[:], mix_hi[:, a, m, :], hnT_hi[p][:, cols_of], start=(a == NOW), stop=False)
                    pe.matmul(dst[:], mix_hi[:, a, m, :], hnT_lo[p][:, cols_of], start=False, stop=False)
                    mm = pe.matmul(dst[:], mix_lo[:, a, m, :], hnT_hi[p][:, cols_of], start=False, stop=(a == BEFORE))
                mm.then_inc(done, 1)

            def project(dst, w, src, done):
                pe.matmul(dst[:], w[:], src[:], start=True, stop=True).then_inc(done, 1)

            def step(tile):
                for t, p, b in tile(3):
                    after(pe, s["rs_ready"][3], t)
                    reduce_heads(p, 0, s["red_even"])
                for t, p, b in tile(6):
                    after(pe, s["gelu_ready"][2], t)
                    after(pe, s["gelu_ready"][3], t)
                    for q in range(NQ):
                        for c in range(NF):
                            mm = pe.matmul(ps_k2[:, q * P:(q + 1) * P], gel[c][:, q * P:(q + 1) * P], w2[:, c, :],
                                           start=(c == 0), stop=(c == NF - 1))
                    mm.then_inc(s["ffn2_ps"], 1)
                    beside(t, LAST, turn_small)
                    beside(t, LAST, turn_experts, 0, SPLIT_BANKS)
                for t, p, b in tile(2):
                    after(pe, s["lora_ready"], t)
                    after(pe, s["vT_ready"], t)
                    project(ps_f[0], wb, lora, s["w_ps"])
                for t, p, b in tile(3):
                    after(pe, s["ruk_ready"], t)
                    after(pe, s["gate_set"], t)
                    project(ps_g, bonus_w, ruk, s["bonus_ps"])
                for t, p, b in tile(2):
                    after(pe, s["hnT_ready"], t)
                    after(pe, s["hnlo_ready"], t)
                    after(pe, s["lora_ready"], t)
                    mixed(ps_f[1], MIX_R, p, s["r_ps"])
                for t, p, b in tile(5):
                    after(pe, s["h2_ready"], t)
                    after(pe, s["y_ready"], t - 1)
                    turn(ps_k2, h2, s["h2T_ps"])
                for t, p, b in tile(4):
                    after(pe, s["onorm_ready"], t)
                    turn(ps_k1, quarters(o_norm[:]), s["onT_ps"])
                for t, p, b in tile(1):
                    after(pe, s["hn_ready"], t)
                    after(pe, s["expw_ready"], t - 1)
                    turn(ps_f[0], hn, s["hnT_ps"])
                for t, p, b in tile(8):
                    after(pe, s["h3T_ready"], t)
                    for q in range(NQ):
                        mm = pe.matmul(ps_k3[:, q * P:(q + 1) * P], h3T[p][:, q * P:(q + 1) * P], gate_w[:], start=True, stop=True)
                    mm.then_inc(s["logits_ps"], 1)
                for t, p, b in tile(2):
                    after(pe, s["hnT_ready"], t)
                    after(pe, s["hnlo_ready"], t)
                    after(pe, s["bonus_ready"], t - 1)
                    mixed(ps_g, MIX_G, p, s["g_ps"])
                for t, p, b in tile(5):
                    after(pe, s["h2T_ready"], t)
                    after(pe, s["h2lo_ready"], t)
                    ffn1(1)
                for t, p, b in tile(4):
                    after(pe, s["ogated_ready"], t)
                    after(pe, s["oaff_ready"], t)
                    for q in range(NQ):
                        mm = pe.matmul(ps_k1[:, q * P:(q + 1) * P], o_gated[:, q * P:(q + 1) * P], wo[:], start=True, stop=True)
                    mm.then_inc(s["wo_ps"], 1)
                for t, p, b in tile(5):
                    after(pe, s["h2T_ready"], t)
                    after(pe, s["h2lo_ready"], t)
                    ffn1(0)
                for t, p, b in tile(3):
                    after(pe, s["rs_ready"][7], t)
                    reduce_heads(p, 1, s["red_odd"])
                for t, p, b in tile(1):
                    after(pe, s["hnT_ready"], t)
                    after(pe, s["hnlo_ready"], t)
                    mixed(ps_f[1], MIX_K, p, s["k_ps"])
                    after(pe, s["hnT_ready"], t)
                    after(pe, s["hnlo_ready"], t)
                    mixed(ps_f[0], MIX_V, p, s["v_ps"])
                for t, p, b in tile(5):
                    after(pe, s["gelu_ready"][1], t)
                    ffn1(3)
                    after(pe, s["gelu_ready"][0], t)
                    ffn1(2)
                for t, p, b in tile(3):
                    after(pe, s["o_ready"], t)
                    for q in range(NQ):
                        mm = pe.matmul(ps_k1[:, q * P:(q + 1) * P], o_sum[:, q * P:(q + 1) * P], center_w[:], start=True, stop=True)
                    mm.then_inc(s["cen_ps"], 1)
                for t, p, b in tile(7):
                    after(pe, s["h3_ready"], t)
                    after(pe, s["logits_ready"], t - 1)
                    turn(ps_k3, h3, s["h3T_ps"])
                    beside(t, LAST - 1, turn_experts, SPLIT_BANKS, E)
                    beside(t, LAST, turn_comb)
                for t, p, b in tile(1):
                    after(pe, s["hnT_ready"], t)
                    after(pe, s["hnlo_ready"], t)
                    after(pe, s["k_ready"], t)
                    mixed(ps_f[1], MIX_W, p, s["lora_ps"])

            def turn_small():
                pe.wait_ge(s["x1_ready"], TILES)
                pe.transpose(ps_k1[:, 0:E * CH], b1_rows[:], ident[0:E * CH, 0:E * CH])
                for h in range(NH2):
                    mm = pe.transpose(ps_k1[:, (1 + h) * P:(2 + h) * P], out_w_rows[:, h * P:(h + 1) * P], ident[:])
                mm.then_inc(s["small_ps"], 1)

            def turn_experts(first, end):
                pe.wait_ge(s["expert_in"], 16 * E)
                for e in range(first, end):
                    if split_banks[e % SPLIT_BANKS] is ps_k2:
                        pe.wait_ge(s["y_ready"], TILES)
                    if e >= SPLIT_BANKS:
                        pe.wait_ge(s["expert_hi"], e - SPLIT_BANKS + 1)
                    for c in range(CH):
                        mm = pe.transpose(split_banks[e % SPLIT_BANKS][:, c * P:(c + 1) * P], rs_prod[:, e // 4, e % 4, c * P:(c + 1) * P], ident[:])
                    mm.then_inc(s["expert_ps"], 1)

            def turn_comb():
                pe.wait_ge(s["comb_ready"], 1)
                pe.wait_ge(s["small_ready"], 2)
                for g in range(EARLY // 4):
                    mm = pe.transpose(ps_k1[:, g * P:(g + 1) * P], kT[1][:, g * P:(g + 1) * P], ident[:])
                mm.then_inc(s["combT_ps"], 1)

            run_pipeline(pe, step, {FIRST_PRODUCT_AT: await_weights, GATE_AT: await_gate})

        @block.vector
        def _(dve):
            dve.wait_ge(s["ident_ready"], 1)
            dve.wait_ge(s["consts_ready"], 18)
            dve.tensor_reduce(head_of_key[:], ident[:].rearrange("p (h k) -> p h k", h=H), AX_X, ALU.add) \
                .then_inc(s["selectors_part"], 1)
            dve.tensor_reduce(head_of_val[:], ident[:].rearrange("p (j h) -> p h j", h=H), AX_X, ALU.add) \
                .then_inc(s["selectors_part"], 1)
            dve.wait_ge(s["selectors_part"], 2)
            for half in range(2):
                dve.tensor_copy(reduce_w[:, half, half * H:(half + 1) * H], head_of_key[:])
            dve.tensor_copy(bonus_w[:].rearrange("p (j h) -> p j h", h=H), head_of_key[:].unsqueeze(1).broadcast_to([P, DK, H]))
            dve.scalar_tensor_tensor(out=center_w[:].rearrange("p (j h) -> p j h", h=H),
                                     in0=head_of_val[:].unsqueeze(1).broadcast_to([P, DK, H]), scalar=-1.0 / DK,
                                     in1=ident[:].rearrange("p (j h) -> p j h", h=H), op0=ALU.mult, op1=ALU.add) \
                .then_inc(s["setup_step"], 1)
            dve.wait_ge(s["vectors_in"], 16 * NROWS)
            dve.tensor_copy(gn_turned[:].rearrange("a (j h) -> a j h", h=H),
                            gn_rows[:].rearrange("a (h j) -> a j h", h=H)).then_inc(s["setup_step"], 1)
            dve.wait_ge(s["mod_copied"], 2)
            pair_of = mod_rows[:].rearrange("b (g a) d -> b g a d", g=2)
            dve.tensor_scalar(mod_sign, pair_of[:, :, 2, :], 0.0, 2.0, ALU.is_ge, ALU.mult).then_inc(s["mod_step"], 1)
            dve.tensor_scalar(mod_abs, pair_of[:, :, 2, :], -1.0, None, ALU.mult).then_inc(s["mod_step"], 1)
            dve.wait_ge(s["mod_step"], 2)
            dve.tensor_tensor(mod_abs, mod_abs, pair_of[:, :, 2, :], ALU.max).then_inc(s["mod_step"], 1)
            dve.wait_ge(s["mod_step"], 3)
            dve.tensor_scalar(mod_abs, mod_abs, GATE_MIN, None, ALU.max).then_inc(s["mod_step"], 1)
            dve.wait_ge(s["mod_step"], 4)
            dve.scalar_tensor_tensor(out=pair_of[:, :, 2, :], in0=mod_sign, scalar=-1.0, in1=mod_abs,
                                     op0=ALU.add, op1=ALU.mult)
            dve.tensor_scalar(pair_of[:, :, 1, :], pair_of[:, :, 1, :], 1.0, None, ALU.add).then_inc(s["mod_ready"], 1)
            def prepare_weights():
                dve.wait_ge(s["cols_ready"], 1)
                dve.wait_ge(s["weights_in"], 16 * 7)
                ln1, ln2 = cols[:, ROW_LN1:ROW_LN1 + 1], cols[:, ROW_LN2:ROW_LN2 + 1]
                mu = cols[:, ROW_MUR:ROW_MUG + 1]
                dve.tensor_scalar(shares[:, BEFORE, :], mu, ln1, None, ALU.mult).then_inc(s["weights_step"], 1)
                dve.wait_ge(s["weights_step"], 1)
                dve.tensor_scalar(shares[:, NOW, :], shares[:, BEFORE, :], -1.0, ln1, ALU.mult, ALU.add).then_inc(s["weights_step"], 1)
                dve.wait_ge(s["weights_step"], 2)
                for a in (NOW, BEFORE):
                    for m, raw, by_head in ((MIX_K, staged[:, 0], False), (MIX_V, staged[:, 1], True), (MIX_R, staged[:, 2], False),
                                            (MIX_G, staged[:, 3], True), (MIX_W, wa[:], False)):
                        dst = mix_full[:, a, m]
                        if by_head:
                            dst, raw = dst.rearrange("p (j h) -> p j h", h=H), raw.rearrange("p (h j) -> p j h", h=H)
                        scaled = dve.tensor_scalar(dst, raw, shares[:, a, m:m + 1], None, ALU.mult)
                dve.tensor_scalar(cols[:, ROW_GNW:ROW_GNB + 1], cols[:, ROW_GNW:ROW_GNB + 1], 0.5, None, ALU.mult)
                dve.tensor_scalar(w1_full, w1_full, ln2, None, ALU.mult).then_inc(s["weights_step"], 1)
                dve.wait_ge(s["weights_step"], 3)
                dve.tensor_copy(mix_hi[:], mix_full)
                dve.tensor_copy(w1_hi[:], w1_full).then_inc(s["weights_step"], 1)
                dve.wait_ge(s["weights_step"], 4)
                dve.tensor_tensor(mix_lo[:], mix_full, mix_hi[:].bitcast(F32), ALU.subtract).then_inc(s["mix_ready"], 1)
                dve.tensor_tensor(w1_lo[:], w1_full, w1_hi[:].bitcast(F32), ALU.subtract).then_inc(s["setup_step"], 1)

            def token_stats(src, st, done):
                for q in range(NQ):
                    ins_ = dve.bn_stats(st[:, q, :], src[:, q, :])
                ins_.then_inc(done, 1)

            def token_moments(mv, st, done):
                for q in range(NQ):
                    ins_ = dve.bn_aggr(mv[:, q, :], st[:, q, :])
                ins_.then_inc(done, 1)

            def mean_shift(dst, mv, rs, done):
                dve.scalar_tensor_tensor(out=dst[:], in0=mv[:, :, 0], scalar=-1.0, in1=rs[:], op0=ALU.mult, op1=ALU.mult).then_inc(done, 1)

            def outer(idx, p):
                dve.tensor_tensor(kv[idx % 2][:], v_spread[idx][:], kT[p][:], ALU.mult).then_inc(s["kv_ready"], 1)

            def scan(idx, p):
                first = 0.0 if p == 0 else state_end[:, ORDER[idx]:ORDER[idx] + 1]
                dve.tensor_tensor_scan(state[idx % 4], dT[p][:], kv[idx % 2][:], first, ALU.mult, ALU.add) \
                    .then_inc(s["scan_ready"][idx], 1)

            def step(tile):
                for t, p, b in tile(1):
                    after(dve, s["ln1_stats"], t)
                    apart(dve, s["dve_passed"])
                    token_moments(mv1, st1, s["ln1_mv"])
                for t, p, b in tile(5):
                    after(dve, s["osq_ready"], t)
                    dve.tensor_reduce(var_g[:], o_sq[:].rearrange("p (q j h) -> p q h j", q=NQ, h=H), AX_X, ALU.add) \
                        .then_inc(s["var_ready"], 1)
                for t, p, b in tile(4):
                    after(dve, s["kv_ready"], t, DK, 5)
                    after(dve, s["rs_ready"][0], t)
                    scan(4, p)
                    after(dve, s["kv_ready"], t, DK, 6)
                    after(dve, s["rs_ready"][1], t)
                    scan(5, p)
                    after(dve, s["v_spread"][6], t, 16, 16)
                    after(dve, s["scan_ready"][4], t)
                    outer(6, p)
                    after(dve, s["tanh_ready"], t)
                    dve.scalar_tensor_tensor(out=gate[p][:], in0=gate[p][:], scalar=1.0, in1=ps_g[:],
                                             op0=ALU.add, op1=ALU.mult).then_inc(s["gate_set"], 1)
                for t, p, b in tile(8):
                    after(dve, s["ln2_rstd"], t)
                    apart(dve, s["dve_passed"])
                    mean_shift(shift4, mv4, rs4, s["shift2_ready"])
                    beside(t, LAST, router.take_first)
                    beside(t, LAST, router.find, router.P2)
                    beside(t, LAST, router.take_second)
                    beside(t, LAST, router.shares, s["comb_ready"])
                    beside(t, LAST, experts_rest)
                for t, p, b in tile(4):
                    after(dve, s["kv_ready"], t, DK, 7)
                    after(dve, s["rs_ready"][2], t)
                    scan(6, p)
                for t, p, b in tile(5):
                    after(dve, s["sd_ready"], t)
                    dve.reciprocal(rs_g[:], sd_g[:]).then_inc(s["rsg_ready"], 1)
                for t, p, b in tile(4):
                    after(dve, s["v_spread"][7], t, 16, 16)
                    outer(7, p)
                for t, p, b in tile(7):
                    after(dve, s["ffn2_ps"], t)
                    after(dve, s["x2_stored"][p], b - 1, 16, 16)
                    dve.tensor_tensor(x2[p][:], quarters(ps_k2[:]), h_all[:, t], ALU.add).then_inc(s["y_ready"], 1)
                    beside(t, LAST, gate_last)
                for t, p, b in tile(5):
                    after(dve, s["rsg_ready"], t)
                    dve.tensor_tensor(o_norm[:].rearrange("p (q j h) -> p q j h", q=NQ, h=H),
                                      ps_k1[:].rearrange("p (q j h) -> p q j h", q=NQ, h=H),
                                      rs_g[:].unsqueeze(2).broadcast_to([P, NQ, DK, H]), ALU.mult).then_inc(s["onorm_ready"], 1)
                for t, p, b in tile(4):
                    after(dve, s["bonus_ps"], t)
                    after(dve, s["vT_ready"], t)
                    dve.tensor_tensor(bonus[p][:], ps_g[:], vT[p][:], ALU.mult).then_inc(s["bonus_ready"], 1)
                    after(dve, s["kv_ready"], t, DK, 8)
                    after(dve, s["rs_ready"][3], t)
                    scan(7, p)
                for t, p, b in tile(3):
                    after(dve, s["v_spread"][0], t, 16, 16)
                    after(dve, s["k_ready"], t)
                    outer(0, p)
                    after(dve, s["v_spread"][1], t, 16, 16)
                    after(dve, s["scan_ready"][7], t - 1)
                    outer(1, p)
                for t, p, b in tile(6):
                    after(dve, s["h2T_ready"], t)
                    dve.tensor_tensor(h2T_lo[:], ps_k2[:], h2T_hi[:].bitcast(F32), ALU.subtract).then_inc(s["h2lo_ready"], 1)
                    beside(t, LAST, route_shift)
                for t, p, b in tile(5):
                    after(dve, s["oaff_ready"], t)
                    dve.tensor_tensor(o_gated[:], o_gated[:], gate[p][:], ALU.mult).then_inc(s["ogated_ready"], 1)
                for t, p, b in tile(1):
                    after(dve, s["ln1_rstd"], t)
                    apart(dve, s["dve_passed"])
                    mean_shift(shift1, mv1, rs1, s["shift1_ready"])
                for t, p, b in tile(3):
                    after(dve, s["kv_ready"], t, DK, 1)
                    after(dve, s["d_ready"], t)
                    after(dve, s["rs_ready"][4], t - 1)
                    scan(0, p)
                    after(dve, s["kv_ready"], t, DK, 2)
                    after(dve, s["rs_ready"][5], t - 1)
                    scan(1, p)
                for t, p, b in tile(2):
                    after(dve, s["hnT_ready"], t)
                    if p == 1:
                        dve.tensor_copy(hnT_lo[1][:, 0:1], hnT_lo[0][:, NT:NT + 1])
                    dve.tensor_tensor(hnT_lo[p][:, 1:NT + 1], ps_f[0][:], hnT_hi[p][:, 1:NT + 1].bitcast(F32), ALU.subtract) \
                        .then_inc(s["hnlo_ready"], 1)
                for t, p, b in tile(3):
                    after(dve, s["v_spread"][2], t, 16, 16)
                    after(dve, s["scan_ready"][0], t)
                    outer(2, p)
                for t, p, b in tile(7):
                    after(dve, s["y_gated"], t)
                    after(dve, s["xre_loaded"][p], b, 16, 16)
                    apart(dve, s["dve_passed"])
                    dve.tensor_tensor(x2[p][:], x2[p][:], xre[p][:], ALU.add).then_inc(s["x2_ready"], 1)
                for t, p, b in tile(3):
                    after(dve, s["r_ready"], t)
                    dve.scalar_tensor_tensor(out=ruk[:], in0=rT[p][:], scalar=cols[:, ROW_U:ROW_U + 1], in1=kT[p][:],
                                             op0=ALU.mult, op1=ALU.mult).then_inc(s["ruk_ready"], 1)
                    after(dve, s["v_spread"][3], t, 16, 16)
                    after(dve, s["scan_ready"][1], t)
                    outer(3, p)
                for t, p, b in tile(5):
                    after(dve, s["wo_ps"], t)
                    dve.tensor_tensor(h_all[:, t], quarters(ps_k1[:]), h_all[:, t], ALU.add).then_inc(s["x1_ready"], 1)
                for t, p, b in tile(3):
                    after(dve, s["kv_ready"], t, DK, 3)
                    after(dve, s["rs_ready"][6], t - 1)
                    scan(2, p)
                for t, p, b in tile(4):
                    after(dve, s["red_odd"], t)
                    dve.tensor_tensor(o_sum[:], ps_o[:], bonus[p][:], ALU.add).then_inc(s["o_ready"], 1)
                for t, p, b in tile(3):
                    after(dve, s["kv_ready"], t, DK, 4)
                    scan(3, p)
                for t, p, b in tile(7):
                    after(dve, s["x2_ready"], t)
                    token_stats(x2[p], st4, s["ln2_stats"])
                for t, p, b in tile(1):
                    after(dve, s["h_scaled"], t)
                    dve.tensor_tensor(h_all[:, t], h_all[:, t], mod_row(SA, b), ALU.add).then_inc(s["h_ready"], 1)
                for t, p, b in tile(0):
                    after(dve, s["x_loaded"][p], b, 16, 16)
                    token_stats(xin[p], st1, s["ln1_stats"])
                for t, p, b in tile(3):
                    after(dve, s["v_spread"][4], t, 16, 16)
                    after(dve, s["scan_ready"][2], t)
                    outer(4, p)
                for t, p, b in tile(7):
                    after(dve, s["ln2_stats"], t)
                    apart(dve, s["dve_passed"])
                    token_moments(mv4, st4, s["ln2_mv"])
                    beside(t, LAST - 1, route_scores)
                    beside(t, LAST, router.find, router.P1)
                for t, p, b in tile(3):
                    after(dve, s["v_spread"][5], t, 16, 16)
                    after(dve, s["scan_ready"][3], t)
                    outer(5, p)

            early = EARLY * NQ * E
            router = Router(dve, s["route_step"], logits[:, 0:EARLY], expert_rank, csum_all[:, 0:EARLY * NQ], hit=dT[0][:, 0:early],
                            first=kT[0][:, 0:early], second=ruk[:, 0:early], comb=kT[1][:, 0:early], top=kv[1][:, 0:7 * EARLY * NQ])

            def route_shift():
                dve.wait_ge(s["logits_ready"], EARLY)
                router.shift()

            def route_scores():
                dve.wait_ge(s["exp_ready"], 1)
                router.scores()

            def gate_last():
                dve.wait_ge(s["y_ready"], TILES)
                dve.tensor_tensor(x2[LAST % 2][:], x2[LAST % 2][:], mod_row(GA, LAST // TPB), ALU.mult).then_inc(s["y_gated"], 1)

            def experts_rest():
                for e in range(VECTOR_EXPERTS):
                    dve.wait_ge(s["expert_hi"], e + 1)
                    dve.tensor_tensor(w_lo[:, e], w_full[e][:], w_hi[:, e].bitcast(F32), ALU.subtract).then_inc(s["expert_lo"], 1)

            run_pipeline(dve, step, {WEIGHTS_AT: prepare_weights})
            dve.wait_ge(s["expert_lo"], E)

    return s


def expert_block(nc, ins, out_rows, mods_dram, x2_dram, h3_dram, comb_dram, csum_all, ident, EARLY, kept,
                 B, D, E, HE, NH2, NT, NQ, TPB, TILES):
    UNITS = E * NH2
    HALF = UNITS // 2
    DEPTH = 4
    TURN = UNITS // DEPTH
    CH = 2 * NH2
    GB = 5
    PEELED = 5
    SOON = 2
    LATE = TILES - EARLY
    ROUTED_IN, ROUTED_AT = 4, 13
    PROJECT_AT, BIAS_AT, GATED_BIAS_AT, FINISH_AT, SPLIT_AT, GATE_AT = (5, 7), (7, 9), 3, 12, 11, 6
    w_hi, w_lo, b1_cols, out_w, x_hi0, x_lo0, logits, expert_rank, comb0, comb_stored, first_comb, rest_comb = kept
    with ExitStack() as ctx:
        def sb(name, shape, dt=F32):
            return ctx.enter_context(nc.sbuf_tensor(name, shape, dt))

        def bank(name):
            return ctx.enter_context(nc.psum_tensor(name, [P, 512], F32))

        out_b = sb("out_b", [P, P])
        gb_all = sb("gb_all", [P, B, P])
        gated_w, gated_b = sb("gated_w", [P, B, NH2, P]), sb("gated_b", [P, B, P])
        h3 = [sb(f"h3_in{i}", [P, NT]) for i in range(2)]
        x_hi, x_lo = [x_hi0, sb("x_hi1", [P, NT], F32R)], [x_lo0, sb("x_lo1", [P, NT], F32R)]
        comb = [comb0, sb("comb1", [P, NQ, E, P])]
        x2 = [sb(f"x2_in{i}", [P, NQ, P]) for i in range(2)]
        sig = [sb(f"sig{i}", [P, NT]) for i in range(DEPTH)]
        weighed = [sb(f"weighed{i}", [P, NT]) for i in range(DEPTH)]
        glu = [sb(f"glu{i}", [P, NT]) for i in range(DEPTH)]
        total = [[sb(f"total{i}_{h}", [P, NT]) for h in range(NH2)] for i in range(2)]
        moe, token_bias = sb("moe", [P, NQ, P]), sb("token_bias", [P, NQ, P])
        res = [sb(f"res{i}", [P, NQ, P]) for i in range(2)]
        ps_a, ps_b = ([bank(f"{n}{i}") for i in range(k)] for n, k in (("ps_a", DEPTH), ("ps_b", 2)))
        ps_w = [bank("ps_w0"), bank("ps_w1")]
        ps_t = ps_w[1]
        late = LATE * NQ * E
        hit, first, second, late_comb, late_combT = (sb(n, [P, late]) for n in ("hit", "first", "second", "late_comb", "late_combT"))
        top = sb("top", [P, 7 * LATE * NQ])

        s = Signals(nc, "experts", (
            "small_in route_step exp_ready comb_ready combT_ps combT_ready "
            "x_hi_ready x_lo_ready out_ps moe_ready bias_ready gated_ready res_ready total_ready").split(),
            {"h3_loaded": 2, "comb_loaded": 2, "x2e_loaded": 2, "stored": 2,
             "b_ps": 2, "added": 2, "a_ps": DEPTH, "sig_ready": DEPTH, "weighed_ready": DEPTH, "glu_ready": DEPTH})

        def run_tiles(eng, tile, last=None):
            for n in range(PEELED):
                tile(n, n % 2, n // 2)
            with eng.Fori(0, (TILES - 1 - PEELED) // 2) as g:
                for u in range(2):
                    tile(g * 2 + (PEELED + u), 1 - u, g + (PEELED // 2 + u))
            tile(TILES - 1, 1, TILES // 2 - 1)
            if last:
                last()

        def unit(i):
            return i // NH2, i % NH2

        block = ctx.enter_context(nc.Block())

        @block.sync
        def _(sp):
            def load_gates():
                sp.dma_start(out_b[:], ins["L0_ffn_bo"].unsqueeze(0).broadcast_to([P, P])).then_inc(s["small_in"], 16)
                sp.dma_start(gb_all[:], mods_dram[:, GB, :].unsqueeze(0).broadcast_to([P, B, P])).then_inc(s["small_in"], 16)

            def load(n, p, b):
                if not isinstance(n, int) or n > 0:
                    after(sp, s["x_lo_ready"], n - 3)
                    sp.dma_start(h3[p][:], h3_dram[n]).then_inc(s["h3_loaded"][p], 16)
                if not isinstance(n, int) or n > 0:
                    after(sp, s["weighed_ready"][-1], n - 2, TURN, TURN)
                    sp.dma_start(comb[p][:].rearrange("p q e t -> p (q e) t"),
                                 comb_dram[n].unsqueeze(0).broadcast_to([P, NQ * E, P])).then_inc(s["comb_loaded"][p], 16)
                after(sp, s["res_ready"], n - 2)
                sp.dma_start(x2[p][:], x2_dram[n]).then_inc(s["x2e_loaded"][p], 16)

            def store(n, p):
                after(sp, s["res_ready"], n)
                sp.dma_start(out_rows[n], res[p][:]).then_inc(s["stored"][p], 16)

            def tile(n, p, b):
                if not isinstance(n, int) or n < TILES - 1:
                    load(n + 1, 1 - p, b)
                if not isinstance(n, int) or n > 0:
                    store(n - 1, 1 - p)
                if isinstance(n, int) and n == ROUTED_IN:
                    sp.wait_ge(s["combT_ready"], 1)
                    sp.dma_start(comb_dram[EARLY:].rearrange("n r t -> (n r) t"), late_combT[:]).then_inc(comb_stored, 16)
                    sp.wait_ge(comb_stored, 16 * (TILES // 4))

            load(0, 0, 0)
            load_gates()
            run_tiles(sp, tile, last=lambda: store(TILES - 1, 1))
            for p in range(2):
                sp.wait_ge(s["stored"][p], 16 * (TILES // 2))

        @block.tensor
        def _(pe):
            def project(n, p, b, half):
                if half == 0:
                    after(pe, s["gated_ready"], b)
                    after(pe, s["total_ready"], n)
                    after(pe, s["moe_ready"], n - 1)
                for q in range(half * NQ // 2, (half + 1) * NQ // 2):
                    for h in range(NH2):
                        mm = pe.matmul(ps_w[half][:, q * P:(q + 1) * P], total[p][h][:, q * P:(q + 1) * P], gated_w[:, b, h, :],
                                       start=(h == 0), stop=(h == NH2 - 1))
                mm.then_inc(s["out_ps"], 1)

            def product(dst, e, c, p):
                cs = slice(c * P, (c + 1) * P)
                pe.matmul(dst[:], w_hi[:, e, cs], x_hi[p][:], start=True, stop=False)
                pe.matmul(dst[:], w_hi[:, e, cs], x_lo[p][:], start=False, stop=False)
                return pe.matmul(dst[:], w_lo[:, e, cs], x_hi[p][:], start=False, stop=True)

            def tile(n, p, b):
                after(pe, s["x_hi_ready"], n - 1)
                after(pe, s["x_lo_ready"], n - 1)
                for i in range(UNITS):
                    e, h = unit(i)
                    after(pe, s["sig_ready"][(i - 2) % DEPTH], n, TURN, (i - 2) // DEPTH + 1)
                    product(ps_b[i % 2], e, NH2 + h, p).then_inc(s["b_ps"][i % 2], 1)
                    after(pe, s["glu_ready"][i % DEPTH], n, TURN, i // DEPTH)
                    product(ps_a[i % DEPTH], e, h, p).then_inc(s["a_ps"][i % DEPTH], 1)
                    if i in PROJECT_AT and (not isinstance(n, int) or n > 0):
                        project(n - 1, 1 - p, b - 1 + p, PROJECT_AT.index(i))
                    if i == ROUTED_AT and isinstance(n, int) and n == ROUTED_IN:
                        pe.wait_ge(s["comb_ready"], 1)
                        after(pe, s["moe_ready"], n - 1)
                        pe.transpose(ps_t[:, 0:P], late_comb[:], ident[:]).then_inc(s["combT_ps"], 1)

            run_tiles(pe, tile, last=lambda: [project(TILES - 1, 1, B - 1, half) for half in range(2)])

        @block.scalar
        def _(act):
            def split(n, p, b):
                after(act, s["h3_loaded"][p], b - (1 - p), 16, 16)
                after(act, s["a_ps"][-1], n - 2, TURN, TURN)
                act.activation(x_hi[p][:], h3[p][:], ACT.Copy).then_inc(s["x_hi_ready"], 1)

            def scale_bias(n, p, b):
                after(act, s["gated_ready"], b)
                after(act, s["moe_ready"], n - 1)
                for q in range(NQ):
                    at = n * NQ + q
                    ins_ = act.activation(token_bias[:, q, :], gated_b[:, b, :], ACT.Copy,
                                          scale=csum_all[:, at:at + 1] if isinstance(at, int) else csum_all[:, bass.ds(at, 1)])
                ins_.then_inc(s["bias_ready"], 1)

            def tile(n, p, b):
                for i in range(UNITS):
                    e, h = unit(i)
                    bias = e * CH + NH2 + h
                    after(act, s["b_ps"][i % 2], n, HALF, i // 2 + 1)
                    after(act, s["weighed_ready"][i % DEPTH], n, TURN, i // DEPTH)
                    act.activation(sig[i % DEPTH][:], ps_b[i % 2][:], ACT.Sigmoid, bias=b1_cols[:, bias:bias + 1]) \
                        .then_inc(s["sig_ready"][i % DEPTH], 1)
                    if i == GATED_BIAS_AT and (not isinstance(n, int) or n > 0):
                        scale_bias(n - 1, 1 - p, b - 1 + p)
                    if i == UNITS // 2 and (not isinstance(n, int) or n < TILES - 1):
                        split(n + 1, 1 - p, b + p)
                    if i == 6 and isinstance(n, int) and n == 1:
                        act.wait_ge(s["route_step"], 2)
                        lg = logits[:, EARLY:].rearrange("p n q e -> p (n q e)")
                        act.activation(lg, lg, ACT.Exp).then_inc(s["exp_ready"], 1)
                    if i == ROUTED_AT and isinstance(n, int) and n == ROUTED_IN:
                        act.wait_ge(s["combT_ps"], 1)
                        act.activation(late_combT[:], ps_t[:, 0:P], ACT.Copy).then_inc(s["combT_ready"], 1)

            run_tiles(act, tile, last=lambda: scale_bias(TILES - 1, 1, B - 1))

        @block.gpsimd
        def _(pool):
            def finish(n, p, b):
                after(pool, s["moe_ready"], n)
                after(pool, s["stored"][p], b - 1, 16, 16)
                after(pool, s["x2e_loaded"][p], b, 16, 16)
                pool.tensor_tensor(res[p][:], moe[:], x2[p][:], ALU.add).then_inc(s["res_ready"], 1)

            def tile(n, p, b):
                start = isinstance(n, int) and n == 0
                if start:
                    pool.wait_ge(first_comb, 16)
                else:
                    after(pool, s["comb_loaded"][p], b - (1 - p), 16, 16)
                for i in range(UNITS):
                    e, h = unit(i)
                    if start and i == SOON * NH2:
                        pool.wait_ge(rest_comb, 16)
                    after(pool, s["sig_ready"][i % DEPTH], n, TURN, i // DEPTH + 1)
                    after(pool, s["glu_ready"][i % DEPTH], n, TURN, i // DEPTH)
                    pool.tensor_tensor(weighed[i % DEPTH][:].rearrange("p (q t) -> p q t", q=NQ),
                                       sig[i % DEPTH][:].rearrange("p (q t) -> p q t", q=NQ),
                                       comb[p][:, :, e, :], ALU.mult).then_inc(s["weighed_ready"][i % DEPTH], 1)
                    if i == FINISH_AT and (not isinstance(n, int) or n > 0):
                        finish(n - 1, 1 - p, b - 1 + p)

            run_tiles(pool, tile, last=lambda: finish(TILES - 1, 1, TILES // 2 - 1))

        @block.vector
        def _(dve):
            def split(n, p, b):
                after(dve, s["x_hi_ready"], n - 1)
                after(dve, s["a_ps"][-1], n - 2, TURN, TURN)
                dve.tensor_tensor(x_lo[p][:], h3[p][:], x_hi[p][:].bitcast(F32), ALU.subtract).then_inc(s["x_lo_ready"], 1)

            router = Router(dve, s["route_step"], logits[:, EARLY:], expert_rank, csum_all[:, EARLY * NQ:], hit=hit[:],
                            first=first[:], second=second[:], comb=late_comb[:], top=top[:])

            def route_beside(n, i):
                if (n, i) == (1, 3):
                    router.shift()
                if (n, i) == (1, 10):
                    dve.wait_ge(s["exp_ready"], 1)
                    router.scores()
                if (n, i) == (2, 3):
                    router.find(router.P1)
                if (n, i) == (2, 12):
                    router.take_first()
                if (n, i) == (3, 3):
                    router.find(router.P2)
                if (n, i) == (3, 12):
                    router.take_second()
                if (n, i) == (4, 1):
                    router.shares(s["comb_ready"])

            def gate_output(b):
                dve.wait_ge(s["small_in"], 32)
                dve.tensor_tensor(gated_w[:, b], out_w[:], gb_all[:, b].unsqueeze(1).broadcast_to([P, NH2, P]), ALU.mult)
                dve.tensor_tensor(gated_b[:, b], out_b[:], gb_all[:, b], ALU.mult).then_inc(s["gated_ready"], 1)

            def bias_out(n, p, b, half):
                qs = slice(half * NQ // 2, (half + 1) * NQ // 2)
                after(dve, s["out_ps"], n, 2, half + 1)
                if half == 0:
                    after(dve, s["bias_ready"], n)
                    after(dve, s["res_ready"], n - 1)
                ins_ = dve.tensor_tensor(moe[:, qs, :], ps_w[half][:, qs.start * P:qs.stop * P].rearrange("p (q d) -> p q d", d=P),
                                         token_bias[:, qs, :], ALU.add)
                if half == 1:
                    ins_.then_inc(s["moe_ready"], 1)

            def tile(n, p, b):
                def add(i):
                    e, h = unit(i)
                    after(dve, s["glu_ready"][i % DEPTH], n, TURN, i // DEPTH + 1)
                    if i - NH2 < NH2:
                        after(dve, s["glu_ready"][i - NH2], n, TURN, 1)
                    else:
                        after(dve, s["added"][i % 2], n, HALF - 1 - i % 2, i // 2 - 1)
                    ins_ = dve.tensor_tensor(total[p][h][:], total[p][h][:], glu[i % DEPTH][:], ALU.add)
                    ins_.then_inc(s["total_ready"] if i == UNITS - 1 else s["added"][i % 2], 1)

                for i in range(UNITS):
                    e, h = unit(i)
                    bias = e * CH + h
                    after(dve, s["a_ps"][i % DEPTH], n, TURN, i // DEPTH + 1)
                    after(dve, s["weighed_ready"][i % DEPTH], n, TURN, i // DEPTH + 1)
                    if e == 0:
                        after(dve, s["out_ps"], n - 2, 2, 2)
                    elif i == NH2:
                        after(dve, s["total_ready"], n - 1)
                    dve.scalar_tensor_tensor(out=(total[p][h] if e == 0 else glu[i % DEPTH])[:], in0=ps_a[i % DEPTH][:],
                                             scalar=b1_cols[:, bias:bias + 1], in1=weighed[i % DEPTH][:],
                                             op0=ALU.add, op1=ALU.mult).then_inc(s["glu_ready"][i % DEPTH], 1)
                    if i - 1 >= NH2:
                        add(i - 1)
                    if i == GATE_AT and p == 0:
                        gate_output(b)
                    if i in BIAS_AT and (not isinstance(n, int) or n > 0):
                        bias_out(n - 1, 1 - p, b - 1 + p, BIAS_AT.index(i))
                    if i == SPLIT_AT and (not isinstance(n, int) or n < TILES - 1):
                        split(n + 1, 1 - p, b + p)
                    if isinstance(n, int):
                        route_beside(n, i)
                add(UNITS - 1)

            run_tiles(dve, tile, last=lambda: [bias_out(TILES - 1, 1, B - 1, half) for half in range(2)])


_INS = ["L0_attn_x", "L0_attn_ln1_w", "L0_attn_mu_r", "L0_attn_mu_k", "L0_attn_mu_v", "L0_attn_mu_w", "L0_attn_mu_g",
        "L0_attn_Wr", "L0_attn_Wk", "L0_attn_Wv", "L0_attn_Wg", "L0_attn_Wo", "L0_attn_w0", "L0_attn_wA", "L0_attn_wB",
        "L0_attn_u", "L0_attn_gn_w", "L0_attn_gn_b", "L0_attn_ln2_w", "L0_attn_ffn_w1", "L0_attn_ffn_w2",
        "L0_ffn_Wg", "L0_ffn_W1", "L0_ffn_b1", "L0_ffn_Wo", "L0_ffn_bo", "L0_c", "L0_wmod"]


def kernel(**inputs):
    import concourse.bacc as bacc
    from concourse.bass_utils import run_bass_kernel_spmd

    nc = bacc.Bacc("TRN2", target_bir_lowering=False, num_devices=1)
    arrays, args = {}, {}
    for name in _INS:
        a = np.ascontiguousarray(inputs[name])
        arrays[f"in_{name}"] = a
        args[name] = nc.dram_tensor(f"in_{name}", a.shape, mybir.dt.from_np(a.dtype), kind="ExternalInput").ap()
    shape = inputs["L0_attn_x"].shape
    out = nc.dram_tensor("out_0", shape, F32, kind="ExternalOutput").ap()
    build(nc, args, out)
    r = run_bass_kernel_spmd(nc, [arrays], core_ids=[0])
    return r.results[0]["out_0"]
```
